# Optimizing a Trainium2 kernel written in Bass

```python
import numpy as np
import jax
import jax.numpy as jnp

def _softmax(x, axis=-1):
    return jax.nn.softmax(x, axis=axis)

def _gelu(x):
    return jax.nn.gelu(x, approximate=True)

def _silu(x):
    return jax.nn.silu(x)

def _sigmoid(x):
    return jax.nn.sigmoid(x)

def _layernorm(x, axis=-1, eps=1e-05):
    m = jnp.mean(x, axis=axis, keepdims=True)
    v = jnp.var(x, axis=axis, keepdims=True)
    return (x - m) / jnp.sqrt(v + eps)

def _scatter_add(tgt, idx, src, axis=0):
    return tgt.at[idx].add(src)

def _segment_sum(src, seg, n):
    return jax.ops.segment_sum(src, seg, n)
kernel_name = 'mk_gnn_preln_d4_gnn_r16_35f5d2'

def setup_inputs(seed: int=0):
    np.random.seed(seed)
    _w = jnp.asarray

    def _rec_inputs():
        import jax
        import jax.numpy as jnp
        _gk = jax.random.key(seed)
        x = -0.000202 + 1 * jax.random.normal(jax.random.fold_in(_gk, 1), (6250, 64), jnp.float32)
        src = jax.random.randint(jax.random.fold_in(_gk, 2), (200000,), 0, 6250, jnp.int32)
        dst = jax.random.randint(jax.random.fold_in(_gk, 3), (200000,), 0, 6250, jnp.int32)
        _o = jnp.argsort(dst, stable=True)
        src = src[_o]
        dst = dst[_o]
        edge_weight1 = 0.000614103 + 0.999867 * jax.random.normal(jax.random.fold_in(_gk, 13), (200000, 1), jnp.float32)
        return (x, src, dst, edge_weight1)
    x, src, dst, edge_weight1 = _rec_inputs()

    def _L0_gnn_setup():
        import jax, jax.numpy as jnp
        import numpy as np
        N_NODES = 6250
        N_EDGES = 200000
        D_FEAT = 64
        key = jax.random.key(seed)
        k1, k2, k3 = jax.random.split(key, 3)
        label = jax.random.normal(k1, (N_NODES, D_FEAT), dtype=jnp.float32)
        src = jax.random.randint(k2, (N_EDGES,), 0, N_NODES, dtype=jnp.int64)
        dst = jax.random.randint(k3, (N_EDGES,), 0, N_NODES, dtype=jnp.int64)
        return {'label': label, 'src': src, 'dst': dst}
    _L0_gnn_all = _L0_gnn_setup()
    _L0_gnn_in = {k: v for k, v in _L0_gnn_all.items() if k in ()}
    del _L0_gnn_all

    def _L1_gnn_setup():
        import jax, jax.numpy as jnp
        import numpy as np
        N_NODES = 5000
        FEAT = 64
        HID = 32
        N_EDGES = 80000
        NEG_SLOPE = 0.2

        def _gat_layer(x, W, a_s, a_d, b, src, dst, n):
            h = x @ W
            logits = jax.nn.leaky_relu(h[src] @ a_s + h[dst] @ a_d, NEG_SLOPE)
            m = jax.ops.segment_max(logits, dst, num_segments=n)
            e = jnp.exp(logits - m[dst])
            denom = jax.ops.segment_sum(e, dst, num_segments=n)
            coef = e / (denom[dst] + 1e-16)
            out = jax.ops.segment_sum(coef[:, None] * h[src], dst, num_segments=n)
            return out + b
        key = jax.random.key(seed)
        ks = jax.random.split(key, 10)
        x = jax.random.normal(ks[0], (N_NODES, FEAT), dtype=jnp.float32)
        edge_index = jax.random.randint(ks[1], (2, N_EDGES), 0, N_NODES, dtype=jnp.int64)

        def glorot(k, shape):
            fan = sum(shape) if len(shape) > 1 else shape[0]
            return jax.random.normal(k, shape, dtype=jnp.float32) * jnp.sqrt(2.0 / fan)
        W1 = glorot(ks[2], (FEAT, HID))
        a_src1 = glorot(ks[3], (HID,))
        a_dst1 = glorot(ks[4], (HID,))
        b1 = jnp.zeros((HID,), dtype=jnp.float32)
        W2 = glorot(ks[5], (HID, FEAT))
        a_src2 = glorot(ks[6], (FEAT,))
        a_dst2 = glorot(ks[7], (FEAT,))
        b2 = jnp.zeros((FEAT,), dtype=jnp.float32)
        return {'x': x, 'edge_index': edge_index, 'W1': W1, 'a_src1': a_src1, 'a_dst1': a_dst1, 'b1': b1, 'W2': W2, 'a_src2': a_src2, 'a_dst2': a_dst2, 'b2': b2}
    _L1_gnn_all = _L1_gnn_setup()
    _L1_gnn_in = {k: v for k, v in _L1_gnn_all.items() if k in ('W1', 'a_src1', 'a_dst1', 'b1', 'W2', 'a_src2', 'a_dst2', 'b2')}
    del _L1_gnn_all

    def _L2_gnn_setup():
        import jax, jax.numpy as jnp
        import numpy as np
        N = 6250
        DEG = 32
        D = 64
        NEG_SLOPE = 0.2
        key = jax.random.key(seed)
        k1, k2, k3, k4 = jax.random.split(key, 4)
        x = jax.random.normal(k1, (N, D), jnp.float32)
        src = jnp.repeat(jnp.arange(N, dtype=jnp.int64), DEG)
        off = jax.random.randint(k2, (N * DEG,), 1, N, dtype=jnp.int64)
        dst = (src + off) % N
        edge_index = jnp.stack([src, dst])
        stdv_w = float(np.sqrt(6.0 / (D + D)))
        weight = jax.random.uniform(k3, (D, D), jnp.float32, -stdv_w, stdv_w)
        stdv_a = float(np.sqrt(6.0 / (1 + 2 * D)))
        att = jax.random.uniform(k4, (2 * D,), jnp.float32, -stdv_a, stdv_a)
        bias = jnp.zeros((D,), jnp.float32)
        return {'x': x, 'edge_index': edge_index, 'weight': weight, 'att': att, 'bias': bias}
    _L2_gnn_all = _L2_gnn_setup()
    _L2_gnn_in = {k: v for k, v in _L2_gnn_all.items() if k in ('weight', 'att', 'bias')}
    del _L2_gnn_all

    def _L3_gnn_setup():
        import jax, jax.numpy as jnp
        import numpy as np
        N_NODES = 3125
        N_EDGES = 50000
        IN_C, HID_C, OUT_C = (64, 128, 64)

        def _mp_layer(x, src, dst, edge_attr, W, b):
            n = x.shape[0]
            loops = jnp.arange(n, dtype=src.dtype)
            src2 = jnp.concatenate([src, loops])
            dst2 = jnp.concatenate([dst, loops])
            ea2 = jnp.concatenate([edge_attr, jnp.zeros((n, edge_attr.shape[1]), dtype=edge_attr.dtype)], axis=0)
            x_i = x[dst2]
            x_j = x[src2]
            msg = jnp.concatenate([x_i, x_j, ea2], axis=1) @ W + b
            agg = jax.ops.segment_sum(msg, dst2, num_segments=n)
            return jax.nn.relu(agg)
        key = jax.random.key(seed)
        k = jax.random.split(key, 8)
        x = jax.random.normal(k[0], (N_NODES, IN_C), dtype=jnp.float32)
        edge_index = jax.random.randint(k[1], (2, N_EDGES), 0, N_NODES, dtype=jnp.int64)
        edge_attr = jax.random.normal(k[2], (N_EDGES, 1), dtype=jnp.float32)
        s1 = 1.0 / np.sqrt(2 * IN_C + 1)
        s2 = 1.0 / np.sqrt(2 * HID_C + 1)
        W1 = jax.random.uniform(k[3], (2 * IN_C + 1, HID_C), jnp.float32, -s1, s1)
        b1 = jax.random.uniform(k[4], (HID_C,), jnp.float32, -s1, s1)
        W2 = jax.random.uniform(k[5], (2 * HID_C + 1, OUT_C), jnp.float32, -s2, s2)
        b2 = jax.random.uniform(k[6], (OUT_C,), jnp.float32, -s2, s2)
        return {'x': x, 'edge_index': edge_index, 'edge_attr': edge_attr, 'W1': W1, 'b1': b1, 'W2': W2, 'b2': b2}
    _L3_gnn_all = _L3_gnn_setup()
    _L3_gnn_in = {k: v for k, v in _L3_gnn_all.items() if k in ('W1', 'b1', 'W2', 'b2')}
    del _L3_gnn_all
    return {'x': x, 'src': src, 'dst': dst, 'edge_weight1': edge_weight1, 'L1_gnn_W1': _L1_gnn_in['W1'], 'L1_gnn_a_src1': _L1_gnn_in['a_src1'], 'L1_gnn_a_dst1': _L1_gnn_in['a_dst1'], 'L1_gnn_b1': _L1_gnn_in['b1'], 'L1_gnn_W2': _L1_gnn_in['W2'], 'L1_gnn_a_src2': _L1_gnn_in['a_src2'], 'L1_gnn_a_dst2': _L1_gnn_in['a_dst2'], 'L1_gnn_b2': _L1_gnn_in['b2'], 'L2_gnn_weight': _L2_gnn_in['weight'], 'L2_gnn_att': _L2_gnn_in['att'], 'L2_gnn_bias': _L2_gnn_in['bias'], 'L3_gnn_W1': _L3_gnn_in['W1'], 'L3_gnn_b1': _L3_gnn_in['b1'], 'L3_gnn_W2': _L3_gnn_in['W2'], 'L3_gnn_b2': _L3_gnn_in['b2']}

def reference(x, src, dst, edge_weight1, L1_gnn_W1, L1_gnn_a_src1, L1_gnn_a_dst1, L1_gnn_b1, L1_gnn_W2, L1_gnn_a_src2, L1_gnn_a_dst2, L1_gnn_b2, L2_gnn_weight, L2_gnn_att, L2_gnn_bias, L3_gnn_W1, L3_gnn_b1, L3_gnn_W2, L3_gnn_b2):
    import jax
    import jax.numpy as jnp

    def _L0_gnn_ref(label, src, dst):
        import jax, jax.numpy as jnp
        import numpy as np
        N_NODES = 6250
        N_EDGES = 200000
        D_FEAT = 64
        n = label.shape[0]
        ones = jnp.ones(src.shape[0], dtype=label.dtype)
        out_deg = jnp.clip(jax.ops.segment_sum(ones, src, num_segments=n), 1.0)
        in_deg = jnp.clip(jax.ops.segment_sum(ones, dst, num_segments=n), 1.0)
        h = label * (out_deg ** (-0.5))[:, None]
        agg = jax.ops.segment_sum(h[src], dst, num_segments=n)
        return agg * (in_deg ** (-0.5))[:, None]

    def _L1_gnn_ref(x, edge_index, W1, a_src1, a_dst1, b1, W2, a_src2, a_dst2, b2):
        import jax, jax.numpy as jnp
        import numpy as np
        N_NODES = 5000
        FEAT = 64
        HID = 32
        N_EDGES = 80000
        NEG_SLOPE = 0.2

        def _gat_layer(x, W, a_s, a_d, b, src, dst, n):
            h = x @ W
            logits = jax.nn.leaky_relu(h[src] @ a_s + h[dst] @ a_d, NEG_SLOPE)
            m = jax.ops.segment_max(logits, dst, num_segments=n)
            e = jnp.exp(logits - m[dst])
            denom = jax.ops.segment_sum(e, dst, num_segments=n)
            coef = e / (denom[dst] + 1e-16)
            out = jax.ops.segment_sum(coef[:, None] * h[src], dst, num_segments=n)
            return out + b
        n = x.shape[0]
        loops = jnp.arange(n, dtype=edge_index.dtype)
        src = jnp.concatenate([edge_index[0], loops])
        dst = jnp.concatenate([edge_index[1], loops])
        h = _gat_layer(x, W1, a_src1, a_dst1, b1, src, dst, n)
        h = jax.nn.relu(h)
        out = _gat_layer(h, W2, a_src2, a_dst2, b2, src, dst, n)
        return out

    def _L2_gnn_ref(x, edge_index, weight, att, bias):
        import jax, jax.numpy as jnp
        import numpy as np
        N = 6250
        DEG = 32
        D = 64
        NEG_SLOPE = 0.2
        n, d = x.shape
        h = x @ weight
        loop = jnp.arange(n, dtype=edge_index.dtype)
        src = jnp.concatenate([edge_index[0], loop])
        dst = jnp.concatenate([edge_index[1], loop])
        a_i, a_j = (att[:d], att[d:])
        s_i = h @ a_i
        s_j = h @ a_j
        alpha = s_i[dst] + s_j[src]
        alpha = jnp.where(alpha > 0, alpha, NEG_SLOPE * alpha)
        amax = jax.ops.segment_max(alpha, dst, num_segments=n)
        e = jnp.exp(alpha - amax[dst])
        denom = jax.ops.segment_sum(e, dst, num_segments=n)
        w = e / (denom[dst] + 1e-16)
        out = jax.ops.segment_sum(h[src] * w[:, None], dst, num_segments=n)
        out = out + bias
        norm = jnp.linalg.norm(out, axis=1, keepdims=True)
        return out / jnp.maximum(norm, 1e-12)

    def _L3_gnn_ref(x, edge_index, edge_attr, W1, b1, W2, b2):
        import jax, jax.numpy as jnp
        import numpy as np
        N_NODES = 3125
        N_EDGES = 50000
        IN_C, HID_C, OUT_C = (64, 128, 64)

        def _mp_layer(x, src, dst, edge_attr, W, b):
            n = x.shape[0]
            loops = jnp.arange(n, dtype=src.dtype)
            src2 = jnp.concatenate([src, loops])
            dst2 = jnp.concatenate([dst, loops])
            ea2 = jnp.concatenate([edge_attr, jnp.zeros((n, edge_attr.shape[1]), dtype=edge_attr.dtype)], axis=0)
            x_i = x[dst2]
            x_j = x[src2]
            msg = jnp.concatenate([x_i, x_j, ea2], axis=1) @ W + b
            agg = jax.ops.segment_sum(msg, dst2, num_segments=n)
            return jax.nn.relu(agg)
        src, dst = (edge_index[0], edge_index[1])
        h = _mp_layer(x, src, dst, edge_attr, W1, b1)
        h = jax.nn.relu(h)
        out = _mp_layer(h, src, dst, edge_attr, W2, b2)
        return jax.nn.log_softmax(out, axis=1)
    edge_index = jnp.stack([src, dst])
    h = jnp.maximum(_layernorm(x, axis=-1), 0.0)
    x = x + _L0_gnn_ref(h, src, dst)
    h = jnp.maximum(_layernorm(x, axis=-1), 0.0)
    x = x + _L1_gnn_ref(h, edge_index, L1_gnn_W1, L1_gnn_a_src1, L1_gnn_a_dst1, L1_gnn_b1, L1_gnn_W2, L1_gnn_a_src2, L1_gnn_a_dst2, L1_gnn_b2)
    h = jnp.maximum(_layernorm(x, axis=-1), 0.0)
    x = x + _L2_gnn_ref(h, edge_index, L2_gnn_weight, L2_gnn_att, L2_gnn_bias)
    h = jnp.maximum(_layernorm(x, axis=-1), 0.0)
    x = x + _L3_gnn_ref(h, edge_index, edge_weight1, L3_gnn_W1, L3_gnn_b1, L3_gnn_W2, L3_gnn_b2)
    return x

_drawn_inputs = setup_inputs


def setup_inputs(seed=0):
    import zlib

    import numpy as np

    out = dict(_drawn_inputs(seed))
    spreads = {'L1_gnn_b1': (0.0, 0.1), 'L1_gnn_b2': (0.0, 0.1), 'L2_gnn_bias': (0.0, 0.505)}
    factors = {'edge_weight1': 4.705,
     'L1_gnn_a_dst1': 23.542,
     'L1_gnn_a_src2': 8.0,
     'L1_gnn_a_dst2': 8.0,
     'L2_gnn_att': 6.588,
     'L3_gnn_b2': 8.0}
    for name, (base, spread) in spreads.items():
        noise = np.random.default_rng([zlib.crc32(name.encode()), seed]).standard_normal(out[name].shape)
        drawn = base * np.exp(spread * noise) if base else spread * noise
        out[name] = jnp.asarray(drawn.astype(out[name].dtype))
    for name, factor in factors.items():
        out[name] = (out[name] * factor).astype(out[name].dtype)
    return out
```

```python
import concourse.bass as bass
from concourse import mybir
from contextlib import ExitStack

N = 6250
E = 200000
D = 64
BLK = 128
NB = -(-N // BLK)
NP = NB * BLK
CHUNKS = 7
CB = NB // CHUNKS
CW = CB * BLK
HALF = CW // 2
NH = 2 * CHUNKS
GRP = 7
NGRP = NB // GRP
QW = HALF // 4
NQ = NP // QW
QC = CW // QW
WIN = 16
NWIN = NP // WIN
TILES = 1564
G = -(-TILES // BLK)
FULL = (E // BLK) // BLK
KEY = 64
A0 = 25
A1 = NB - A0
BQ = NWIN // 4
LN_EPS = 1e-5
DEN_EPS = 1e-16
NORM_EPS = 1e-12
SLOPE = 0.2

fp32 = mybir.dt.float32
fp16 = mybir.dt.float16
bf16 = mybir.dt.bfloat16
i32 = mybir.dt.int32
ALU = mybir.AluOpType
ACT = mybir.ActivationFunctionType
AX = mybir.AxisListType


def gnn_kernel(nc, ap, out):
    ctx = ExitStack()
    with ctx:
        def sb(name, shape, dt):
            return ctx.enter_context(nc.sbuf_tensor("sb_" + name, shape, dt))

        def sem(name):
            return ctx.enter_context(nc.semaphore(name))

        counts = nc.dram_tensor("counts", (NH, BLK, NB, HALF), fp16, kind="Internal").ap()
        linked = nc.dram_tensor("linked", (NQ, QW, NP), fp16, kind="Internal").ap()
        bounds_dram = nc.dram_tensor("bounds_dram", (2, NWIN), i32, kind="Internal").ap()
        ea_dram = nc.dram_tensor("ea_dram", (NP,), fp32, kind="Internal").ap()

        X = sb("X", [BLK, NB, D], fp32)
        ident = sb("ident", [BLK, BLK], fp32)
        ident16 = sb("ident16", [BLK, BLK], fp16)
        zero16 = sb("zero16", [BLK, BLK], fp16)
        iota_f = sb("iota_f", [BLK, BLK], fp32)
        iota_b = sb("iota_b", [BLK, BLK], fp16)
        ones = sb("ones", [BLK, BLK], fp32)
        fold = sb("fold", [BLK, D + 1], fp32)
        part = sb("part", [BLK, 1], fp32)
        out_deg = sb("out_deg", [BLK, NB], fp32)
        ea_sum = sb("ea_sum", [BLK, NB], fp32)
        deg = sb("deg", [BLK, NB], fp32)
        ARENA = 184 * 1024
        arena = sb("arena", [BLK, ARENA // 4], fp32)

        def view(offset, shape, dt):
            size = 2 if dt in (fp16, bf16) else 4
            for s in shape[1:]:
                size *= s
            words = -(-size // 4)
            assert offset % 4 == 0 and offset + 4 * words <= ARENA, (offset, shape)
            v = arena[0:shape[0], offset // 4:offset // 4 + words]
            if dt != fp32:
                v = v.bitcast(dt)
            if len(shape) == 3:
                v = v[:, 0:shape[1] * shape[2]].rearrange("p (a b) -> p a b", a=shape[1])
            if len(shape) == 4:
                v = v[:, 0:shape[1] * shape[2] * shape[3]].rearrange("p (a b c) -> p a b c", a=shape[1], b=shape[2])
            return v, offset + 4 * words

        psum = ctx.enter_context(nc.psum_tensor("psum", [BLK, 8, 512], fp32))

        def banks(first, count):
            return psum[:, first:first + count, :].rearrange("p k n -> p (k n)")

        SL = 4
        stage, o = view(0, [BLK, 2, NB * HALF], fp16)
        linked_sb, o = view(o, [QW, 2, NP], fp16)
        et, o = view(o, [BLK, 4, G * BLK], fp32)
        key_t, srcb_t, srca_t, dst_t = (et[:, k, :] for k in range(4))
        ea3, o = view(o, [BLK, G * BLK, 3], bf16)
        key_iota, o = view(o, [BLK, NB, WIN], fp16)
        neg_key, o = view(o, [BLK, NWIN], fp32)
        neg_dst, o = view(o, [BLK, NWIN], fp32)
        hot_key, o = view(o, [BLK, SL, 2 * NB * WIN], fp16)
        hot_src, o = view(o, [BLK, SL, 2 * BLK], fp16)
        hot_dst, o = view(o, [BLK, SL, 2 * BLK], bf16)
        ea_win, o = view(o, [WIN, NWIN, 3], fp32)
        ea_row, o = view(o, [WIN, NWIN], fp32)
        bounds, o = view(o, [1, 2 * NWIN], i32)
        dst_i, o = view(0, [BLK, G * BLK], i32)
        src_i, o = view(o, [BLK, G * BLK], i32)
        tmp_i, o = view(o, [BLK, G * BLK], i32)
        raw, o = view(o, [BLK, 5, G * BLK], fp32)
        ea_rest, o = view(o, [BLK, G * BLK], fp32)
        ea_part, o = view(o, [BLK, G * BLK], fp32)
        grp, o = view(o, [BLK, 5, BLK], fp32)
        win_first, o = view(o, [BLK, NWIN], fp32)
        win_last, o = view(o, [BLK, NWIN], fp32)
        over, o = view(o, [BLK, 2, NWIN], fp32)
        hilo, o = view(o, [BLK, 2, NWIN], fp32)
        tile_lo, o = view(o, [BLK, G], fp32)
        tile_hi, o = view(o, [BLK, G], fp32)
        tile_up, o = view(o, [BLK, G], fp32)
        tile_dn, o = view(o, [BLK, G], fp32)
        hl_max, o = view(o, [BQ, 8], fp32)
        hl_int, o = view(o, [BQ, 8], i32)
        assert o <= 2 * NB * HALF * 2

        phase_done = sem("phase_done")
        iotas_done = sem("iotas_done")
        pads_set = sem("pads_set")
        edges_in = sem("edges_in")
        x_in = sem("x_in")
        group_copied = sem("group_copied")
        group_turned = sem("group_turned")
        group_kept = sem("group_kept")
        hilo_turned = sem("hilo_turned")
        bounds_ready = sem("bounds_ready")
        bounds_out = sem("bounds_out")
        bounds_in = sem("bounds_in")
        hist_ready = sem("hist_ready")
        hist_used = sem("hist_used")
        hist_done = sem("hist_done")
        keys_ready = sem("keys_ready")
        slot_free = sem("slot_free")
        window_done = sem("window_done")
        window_free = sem("window_free")
        stage_full = sem("stage_full")
        stage_ready = sem("stage_ready")
        stage_free = sem("stage_free")
        counts_out = sem("counts_out")
        turned = sem("turned")
        turned_kept = sem("turned_kept")
        linked_full = sem("linked_full")
        linked_out = sem("linked_out")
        linked_free = sem("linked_free")
        ea_copied = sem("ea_copied")
        ea_ready = sem("ea_ready")
        hilo_ready = sem("hilo_ready")
        ea_out = sem("ea_out")
        ea_in = sem("ea_in")

        def phase_end(eng, k):
            eng.drain().then_inc(phase_done, 1)
            eng.wait_ge(phase_done, 5 * k)

        block = ctx.enter_context(nc.Block())

        halves16 = ident16[:].rearrange("p (t n) -> p t n", t=2)

        def ap1(v):
            return v.rearrange("p o n -> p (o n)")

        HIN, o = view(0, [BLK, NB, D], fp32)
        AGG, o = view(o, [BLK, NB * (D + 1)], fp32)
        at = o
        H12, o = view(o, [BLK, NB, 2 * D], bf16)
        H3, o = view(o, [BLK, NB, D + 1], bf16)
        HF, _ = view(at, [BLK, NB * (D + 1)], fp32)
        cnt, at = view(o, [BLK, 3, GRP * CW], fp16)
        link, o = view(o, [QW, 2, NP], fp16)
        o = at
        ROW1, o = view(o, [BLK, NP], fp32)
        at = o
        ROW2, o = view(o, [BLK, NP], fp32)
        junk, _ = view(at, [QW, NP], fp16)
        US, _ = view(at, [BLK, NB, 2 * D], fp32)
        DE, _ = view(at - 4 * NP, [BLK, NB, 2], fp32)
        XC, at = view(at - 4 * NP, [BLK, NB, D], fp32)
        SQ, at = view(at, [BLK, NB, D], fp32)
        YE, o = view(o, [BLK, 4, CW], fp32)
        PW, o = view(o, [BLK, 3, CW], fp32)
        TA, o = view(o, [BLK, CW], fp32)
        TB, o = view(o, [BLK, CW], fp32)
        GI, o = view(o, [BLK, NB, D], fp32)
        TD = YE[:, 0, :]
        DET = YE[0:2, 1, :]
        stat = [sb("stat%d" % k, [BLK, NB], fp32) for k in range(3)]
        sj8 = sb("sj8", [BLK, NB], fp32)
        sj2 = sb("sj2", [BLK, NB], fp32)
        si = sb("si", [QW, NQ], fp32)
        top = sb("top", [QW, NQ], fp32)
        top_now = sb("top_now", [QW, 2], fp32)
        c1 = sb("c1", [QW, NQ], fp32)
        c2 = sb("c2", [QW, NQ], fp32)
        low = sb("low", [BLK, 1], fp32)
        W3a = sb("W3a", [BLK, BLK], fp32)
        W3b = sb("W3b", [2, BLK], fp32)
        W4 = sb("W4", [BLK, 2, D], fp32)
        row = {k: sb("row_" + k, [BLK, n], fp32) for k, n in
               (('L1_gnn_b1', 32), ('L1_gnn_b2', D), ('L2_gnn_bias', D), ('L3_gnn_b2', D), ('we2', D))}
        att = []
        for l, (ki, fo, wn, an, dn) in enumerate((
                (D, 32, ap['L1_gnn_W1'], ap['L1_gnn_a_src1'], ap['L1_gnn_a_dst1']),
                (32, D, ap['L1_gnn_W2'], ap['L1_gnn_a_src2'], ap['L1_gnn_a_dst2']),
                (D, D, ap['L2_gnn_weight'], ap['L2_gnn_att'][D:2 * D], ap['L2_gnn_att'][0:D]))):
            att.append((ki, fo, sb("W_att%d" % l, [ki, fo], fp32), sb("a_src%d" % l, [fo, 1], fp32),
                        sb("a_dst%d" % l, [fo, 1], fp32), sb("a_rows%d" % l, [fo, BLK], fp32), wn, an, dn))

        weights_in = sem("weights_in")
        input_ready = sem("input_ready")
        input_placed = sem("input_placed")
        input_turned = sem("input_turned")
        feats_done = sem("feats_done")
        feats_kept = sem("feats_kept")
        scores_done = sem("scores_done")
        scores_kept = sem("scores_kept")
        link_in = [sem("link_in%d" % s) for s in range(2)]
        link_free = sem("link_free")
        diag_ready = sem("diag_ready")
        diag_spread = sem("diag_spread")
        diag_kept = sem("diag_kept")
        cnt_in = [sem("cnt_in%d" % g) for g in range(NGRP)]
        cnt_free = sem("cnt_free")
        y_ready = sem("y_ready")
        e_ready = sem("e_ready")
        p_ready = sem("p_ready")
        p_used = sem("p_used")
        agg_done = sem("agg_done")
        agg_kept = sem("agg_kept")
        agg_turned = sem("agg_turned")
        agg_stored = sem("agg_stored")
        root_in = sem("root_in")
        root_out = sem("root_out")
        mlp_copied = sem("mlp_copied")
        mlp_turned = sem("mlp_turned")
        mlp_kept = sem("mlp_kept")
        mlp_out = sem("mlp_out")
        mlp_relu = sem("mlp_relu")
        mlp_turned2 = sem("mlp_turned2")
        mlp_kept2 = sem("mlp_kept2")
        mlp_out2 = sem("mlp_out2")
        mlp_stored = sem("mlp_stored")
        out_stored = sem("out_stored")

        ROWS = CHUNKS * NB

        def load_counts(sp, L):
            with sp.Fori(0, CHUNKS) as c:
                for g in range(NGRP):
                    before = (0, -2, -1, 1, 2, 3, 4)[g]
                    sp.wait_ge(cnt_free, c * NGRP + (L * ROWS // GRP + 3 + before))
                    to = cnt[:, g % 3, :].rearrange("p (a t d) -> p a t d", a=GRP, t=2)
                    for t in range(2):
                        sp.dma_start(to[:, :, t, :], counts[bass.ds(c * 2 + t, 1), :, g * GRP:(g + 1) * GRP, :].rearrange("o b a d -> b (o a) d")
                                     ).then_inc(cnt_in[g], 16)

        def counts_of(g, j):
            return cnt[:, g % 3, j * CW:(j + 1) * CW]

        @block.sync
        def _(sp):
            sp.wait_ge(pads_set, 4)
            sp.dma_start(X[:, 0:NB - 1, :], ap['x'][0:(NB - 1) * BLK, :].rearrange("(a b) f -> b a f", b=BLK)).then_inc(x_in, 16)
            sp.dma_start(X[0:N - (NB - 1) * BLK, NB - 1, :], ap['x'][(NB - 1) * BLK:N, :]).then_inc(x_in, 16)
            whole = E // BLK - FULL * BLK
            for flat, to in ((ap['dst'], dst_i), (ap['src'], src_i), (ap['edge_weight1'].rearrange("e o -> (e o)"), raw[:, 4, :])):
                to3 = to.rearrange("p (g e) -> p g e", g=G)
                at = FULL * BLK * BLK
                sp.dma_start(to3[:, 0:FULL, :], flat[0:at].rearrange("(g p e) -> p g e", p=BLK, e=BLK)).then_inc(edges_in, 16)
                sp.dma_start(to3[0:whole, FULL, :], flat[at:at + whole * BLK].rearrange("(p e) -> p e", e=BLK)).then_inc(edges_in, 16)
                sp.dma_start(to3[whole:whole + 1, FULL, 0:E % BLK],
                             flat[at + whole * BLK:E].rearrange("(o e) -> o e", o=1)).then_inc(edges_in, 16)
            for (_, _, w, a, d, _, wn, an, dn) in att:
                sp.dma_start(w[:], wn).then_inc(weights_in, 16)
                sp.dma_start(a[:], an.unsqueeze(1)).then_inc(weights_in, 16)
                sp.dma_start(d[:], dn.unsqueeze(1)).then_inc(weights_in, 16)
            sp.dma_start(W3a[:], ap['L3_gnn_W1'][0:BLK, :]).then_inc(weights_in, 16)
            sp.dma_start(W3b[0:1, :], ap['L3_gnn_b1'].unsqueeze(0)).then_inc(weights_in, 16)
            sp.dma_start(W3b[1:2, :], ap['L3_gnn_W1'][BLK:BLK + 1, :]).then_inc(weights_in, 16)
            sp.dma_start(W4[:], ap['L3_gnn_W2'][0:2 * BLK, :].rearrange("(t k) f -> k t f", t=2)).then_inc(weights_in, 16)
            for k in ('L1_gnn_b1', 'L1_gnn_b2', 'L2_gnn_bias', 'L3_gnn_b2'):
                sp.dma_start(row[k][:], ap[k].partition_broadcast(BLK)).then_inc(weights_in, 16)
            sp.dma_start(row['we2'][:], ap['L3_gnn_W2'][2 * BLK, :].partition_broadcast(BLK)).then_inc(weights_in, 16)
            sp.wait_ge(weights_in, 18 * 16)
            sp.wait_ge(x_in, 32)
            phase_end(sp, 1)
            sp.wait_ge(bounds_ready, 1)
            for s in range(2):
                sp.dma_start(bounds_dram[s, :].rearrange("(q p) -> p q", p=BQ), hl_int[:, 4 * s:4 * s + 4], allow_slow_non_contiguous=True).then_inc(bounds_out, 16)
            sp.wait_ge(bounds_out, 32)
            sp.dma_start(bounds[:], bounds_dram.rearrange("s w -> (s w)").rearrange("(o n) -> o n", o=1)).then_inc(bounds_in, 16)
            sp.wait_ge(bounds_in, 16)
            phase_end(sp, 2)
            phase_end(sp, 3)
            with sp.Fori(0, NH) as h:
                sp.wait_ge(stage_ready, h + 1)
                sp.dma_start(counts[bass.ds(h, 1)].rearrange("o b a d -> b (o a d)"),
                             ap1(stage[:, bass.ds(h % 2, 1), :])).then_inc(counts_out, 16)
                with sp.Fori(0, 4) as q:
                    sp.wait_ge(linked_full, (h + 1) * 4 + q + 1)
                    sp.dma_start(linked[bass.ds(h * 4 + q, 1)].rearrange("o d s -> d (o s)"),
                                 ap1(linked_sb[:, bass.ds(q % 2, 1), :])).then_inc(linked_out, 16)
                    sp.wait_ge(linked_out, (h * 4 + q + 1) * 16)
                    sp.sem_inc(linked_free, 1)
                sp.wait_ge(counts_out, (h + 1) * 16)
                sp.sem_inc(stage_free, 1)
            sp.wait_ge(ea_ready, 1)
            sp.dma_start(ea_dram.rearrange("(w d) -> d w", d=WIN), ea_row[:], allow_slow_non_contiguous=True).then_inc(ea_out, 16)
            sp.wait_ge(ea_out, 16)
            sp.dma_start(ea_sum[:], ea_dram.rearrange("(a b) -> b a", b=BLK), allow_slow_non_contiguous=True).then_inc(ea_in, 16)
            sp.wait_ge(ea_in, 16)
            phase_end(sp, 4)
            phase_end(sp, 5)
            sp.sem_inc(cnt_free, 3)
            load_counts(sp, 0)
            phase_end(sp, 6)
            for l in range(3):
                phase_end(sp, 7 + 4 * l)
                if l == 0:
                    sp.sem_inc(link_free, 2)
                with sp.Fori(0, NQ // 2) as b:
                    for s in range(2):
                        sp.wait_ge(link_free, b * 2 + (l * NQ + s + 1))
                        sp.dma_start(link[:, s, :], linked[bass.ds(b * 2 + s, 1)].rearrange("o d s -> d (o s)")).then_inc(link_in[s], 16)
                phase_end(sp, 8 + 4 * l)
                phase_end(sp, 9 + 4 * l)
                load_counts(sp, 1 + l)
                phase_end(sp, 10 + 4 * l)
            phase_end(sp, 19)
            load_counts(sp, 4)
            phase_end(sp, 20)
            phase_end(sp, 21)
            load_counts(sp, 5)
            phase_end(sp, 22)
            phase_end(sp, 23)
            sp.dma_start(out[0:(NB - 1) * BLK, :].rearrange("(a b) f -> b a f", b=BLK), X[:, 0:NB - 1, :]).then_inc(out_stored, 16)
            sp.dma_start(out[(NB - 1) * BLK:N, :], X[0:N - (NB - 1) * BLK, NB - 1, :]).then_inc(out_stored, 16)
            sp.wait_ge(out_stored, 32)

        @block.gpsimd
        def _(pool):
            nc.gpsimd.memset(dst_i[:], NP - 1).then_inc(pads_set, 1)
            nc.gpsimd.memset(src_i[:], NP - 1).then_inc(pads_set, 1)
            nc.gpsimd.memset(raw[:, 4, :], 0.0).then_inc(pads_set, 1)
            nc.gpsimd.memset(X[:, NB - 1, :], 0.0).then_inc(pads_set, 1)
            nc.gpsimd.iota(iota_f[:], [[1, BLK]], base=0, channel_multiplier=0, allow_small_or_imprecise_dtypes=True)
            nc.gpsimd.iota(part[:], [[1, 1]], base=0, channel_multiplier=1, allow_small_or_imprecise_dtypes=True)
            nc.gpsimd.iota(key_iota[:], [[1, NB], [KEY, WIN]], base=0, channel_multiplier=0, allow_small_or_imprecise_dtypes=True)
            nc.gpsimd.iota(win_first[:], [[WIN, NWIN]], base=0, channel_multiplier=0, allow_small_or_imprecise_dtypes=True)
            nc.gpsimd.iota(win_last[:], [[WIN, NWIN]], base=WIN - 1, channel_multiplier=0, allow_small_or_imprecise_dtypes=True)
            nc.gpsimd.iota(neg_key[:], [[-WIN * KEY, NWIN]], base=0, channel_multiplier=0, allow_small_or_imprecise_dtypes=True)
            nc.gpsimd.iota(neg_dst[:], [[-WIN, NWIN]], base=0, channel_multiplier=0, allow_small_or_imprecise_dtypes=True)
            nc.gpsimd.iota(tile_up[:], [[BLK, G]], base=1, channel_multiplier=1, allow_small_or_imprecise_dtypes=True)
            nc.gpsimd.iota(tile_dn[:], [[-BLK, G]], base=TILES, channel_multiplier=-1, allow_small_or_imprecise_dtypes=True)
            nc.gpsimd.memset(zero16[:], 0.0)
            nc.gpsimd.memset(ones[:], 1.0)
            nc.gpsimd.memset(hot_dst[:], 0.0)
            pool.drain().then_inc(iotas_done, 1)
            phase_end(pool, 1)
            phase_end(pool, 2)
            nc.gpsimd.memset(stage[:, 1, :], 0.0)
            phase_end(pool, 3)
            with pool.Fori(0, NH) as h:
                pool.wait_ge(stage_full, h + 1)
                odd = h % 2
                for k in range(3):
                    blk_at = (h // 2) * CB + odd * 4 + k
                    at = stage[:, bass.ds(odd, 1), bass.ds(blk_at * HALF + odd * (BLK // 2) + k * BLK, BLK)]
                    nc.gpsimd.tensor_tensor(ap1(at), ap1(at), ident16[:], ALU.add)
                at = stage[:, bass.ds(odd, 1), bass.ds(((h // 2) * CB + 3) * HALF + 3 * BLK - odd * 3 * BLK, BLK // 2)]
                nc.gpsimd.tensor_tensor(ap1(at), ap1(at), ap1(halves16[:, bass.ds(odd, 1), :]), ALU.add)
                pool.drain().then_inc(stage_ready, 1)
            phase_end(pool, 4)
            for k in range(5, 24):
                phase_end(pool, k)

        @block.vector
        def _(dve):
            dve.wait_ge(iotas_done, 1)
            nc.vector.tensor_copy(iota_b[:], iota_f[:])
            nc.vector.tensor_scalar(ident[:], iota_f[:], part[:, 0:1], None, ALU.is_equal)
            dve.drain()
            nc.vector.tensor_copy(ident16[:], ident[:])
            nc.vector.memset(fold[:], 0.0)
            dve.drain()
            nc.vector.tensor_tensor(fold[:, 0:D], ident[:, 0:D], ident[:, D:2 * D], ALU.add)
            dve.wait_ge(edges_in, 9 * 16)
            nc.vector.tensor_copy(raw[:, 3, :], dst_i[:])
            nc.vector.tensor_single_scalar(tmp_i[:], src_i[:], 7, ALU.arith_shift_right)
            dve.drain()
            nc.vector.tensor_copy(raw[:, 2, :], tmp_i[:])
            dve.drain()
            nc.vector.tensor_single_scalar(tmp_i[:], src_i[:], BLK - 1, ALU.bitwise_and)
            dve.drain()
            nc.vector.tensor_copy(raw[:, 1, :], tmp_i[:])
            nc.vector.scalar_tensor_tensor(raw[:, 0, :], raw[:, 3, :], float(KEY), raw[:, 2, :], ALU.mult, ALU.add)
            dst3 = raw[:, 3, :].rearrange("p (g e) -> p g e", g=G)
            nc.vector.tensor_reduce(tile_lo[:], dst3, AX.X, ALU.min)
            nc.vector.tensor_reduce(tile_hi[:], dst3, AX.X, ALU.max)
            nc.vector.memset(hilo[:], 0.0)
            phase_end(dve, 1)
            for g in range(G):
                nc.vector.tensor_scalar(over[:, 0, :], win_last[:], tile_lo[:, g:g + 1], None, ALU.is_ge)
                dve.drain()
                nc.vector.scalar_tensor_tensor(over[:, 1, :], win_first[:], tile_hi[:, g:g + 1], over[:, 0, :], ALU.is_le, ALU.mult)
                dve.drain()
                nc.vector.scalar_tensor_tensor(hilo[:, 0, :], over[:, 1, :], tile_up[:, g:g + 1], hilo[:, 0, :], ALU.mult, ALU.max)
                nc.vector.scalar_tensor_tensor(hilo[:, 1, :], over[:, 1, :], tile_dn[:, g:g + 1], hilo[:, 1, :], ALU.mult, ALU.max)
                dve.drain()
            dve.drain().then_inc(hilo_ready, 1)
            dve.wait_ge(hilo_turned, 1)
            nc.vector.tensor_reduce(hl_max[:], banks(2, 2)[0:BQ, :].rearrange("p (k n) -> p k n", k=8), AX.X, ALU.max)
            dve.drain()
            nc.vector.tensor_scalar(hl_max[:, 4:8], hl_max[:, 4:8], -1.0, float(TILES), ALU.mult, ALU.add)
            nc.vector.tensor_scalar(hl_max[:, 0:4], hl_max[:, 0:4], float(TILES), 1.0, ALU.min, ALU.add)
            dve.drain()
            nc.vector.tensor_copy(hl_int[:], hl_max[:])
            dve.drain()
            nc.vector.tensor_single_scalar(hl_int[:], hl_int[:], 1, ALU.arith_shift_right)
            dve.drain()
            nc.vector.tensor_copy(hl_max[:], hl_int[:])
            dve.drain()
            nc.vector.tensor_scalar(hl_max[:, 0:4], hl_max[:, 0:4], 1.0, None, ALU.max)
            dve.drain()
            nc.vector.scalar_tensor_tensor(hl_max[:, 4:8], hl_max[:, 0:4], -1.0, hl_max[:, 4:8], ALU.add, ALU.min)
            dve.drain()
            nc.vector.tensor_copy(hl_int[:], hl_max[:])
            dve.drain().then_inc(bounds_ready, 1)
            dve.wait_ge(group_kept, 2 * G)
            nc.vector.tensor_copy(ea3[:, :, 0], ea_rest[:])
            dve.drain()
            nc.vector.tensor_tensor(ea_part[:], ea_rest[:], ea3[:, :, 0], ALU.subtract)
            dve.drain()
            nc.vector.tensor_copy(ea3[:, :, 1], ea_part[:])
            dve.drain()
            nc.vector.tensor_tensor(ea3[:, :, 2], ea_part[:], ea3[:, :, 1], ALU.subtract)
            phase_end(dve, 2)
            with dve.Fori(0, TILES // 4) as i:
                for j in range(4):
                    dve.wait_ge(hist_used, i * 4 + j + 1)
                    nc.vector.tensor_scalar(hot_src[:, j, 0:BLK], iota_b[:], srcb_t[:, bass.ds(i * 4 + j, 1)], None, ALU.is_equal)
                    nc.vector.tensor_scalar(hot_src[:, j, BLK:BLK + NB], iota_b[:, 0:NB], srca_t[:, bass.ds(i * 4 + j, 1)],
                                            None, ALU.is_equal).then_inc(hist_ready, 1)
            dve.wait_ge(hist_done, 1)
            nc.vector.tensor_scalar(out_deg[:], psum[:, 0, 0:NB], 1.0, None, ALU.max)
            phase_end(dve, 3)
            visits = dve.alloc_register("dve_visits")
            dve.reg_mov(visits, 0)
            with dve.Fori(0, NWIN) as w:
                lo = dve.value_load(bounds[0:1, bass.ds(w + NWIN, 1)], min_val=0, max_val=TILES // 2 - 1)
                hi = dve.value_load(bounds[0:1, bass.ds(w, 1)], min_val=1, max_val=TILES // 2)
                with dve.Fori(lo, hi) as i:
                    v = dve.snap(visits)
                    dve.wait_ge(slot_free, v + 1)
                    for t in range(2):
                        nc.vector.tensor_scalar(ap1(hot_key[:, bass.ds(v % SL, 1), t * NB * WIN:(t + 1) * NB * WIN]),
                                                key_iota.rearrange("p a d -> p (a d)"), key_t[:, bass.ds(i * 2 + t, 1)],
                                                neg_key[:, bass.ds(w, 1)], ALU.subtract, ALU.is_equal)
                        nc.vector.tensor_scalar(ap1(hot_src[:, bass.ds(v % SL, 1), t * BLK:(t + 1) * BLK]), iota_b[:],
                                                srcb_t[:, bass.ds(i * 2 + t, 1)], None, ALU.is_equal)
                        last = nc.vector.tensor_scalar(ap1(hot_dst[:, bass.ds(v % SL, 1), t * BLK:t * BLK + WIN]), iota_b[:, 0:WIN],
                                                       dst_t[:, bass.ds(i * 2 + t, 1)], neg_dst[:, bass.ds(w, 1)],
                                                       ALU.subtract, ALU.is_equal)
                    last.then_inc(keys_ready, 1)
                    dve.reg_add(visits, visits, 1)
            dve.wait_ge(ea_copied, 1)
            nc.vector.tensor_reduce(ea_row[:], ea_win[:], AX.X, ALU.add)
            dve.drain().then_inc(ea_ready, 1)
            phase_end(dve, 4)
            def root(k):
                dve.drain().then_inc(root_in, 1)
                dve.wait_ge(root_out, k)
                nc.vector.reciprocal(stat[1][:], stat[1][:])
                dve.drain()

            def per_node(v, width=D):
                return v[:].unsqueeze(2).broadcast_to([BLK, NB, width])

            def per_feature(v, width=D):
                return v[:].unsqueeze(1).broadcast_to([BLK, NB, width])

            def layernorm_relu(k):
                nc.vector.tensor_reduce(stat[0][:], X[:], AX.X, ALU.add)
                dve.drain()
                nc.vector.tensor_scalar(stat[0][:], stat[0][:], 1.0 / D, None, ALU.mult)
                dve.drain()
                nc.vector.tensor_tensor(XC[:], X[:], per_node(stat[0]), ALU.subtract)
                dve.drain()
                nc.vector.tensor_tensor(SQ[:], XC[:], XC[:], ALU.mult)
                dve.drain()
                nc.vector.tensor_reduce(stat[2][:], SQ[:], AX.X, ALU.add)
                dve.drain()
                nc.vector.tensor_scalar(stat[2][:], stat[2][:], 1.0 / D, LN_EPS, ALU.mult, ALU.add)
                root(k)
                nc.vector.tensor_tensor(HIN[:], XC[:], per_node(stat[1]), ALU.mult)
                dve.drain()
                nc.vector.tensor_scalar(HIN[:], HIN[:], 0.0, None, ALU.max)
                dve.drain()

            def split_features():
                nc.vector.tensor_copy(H12[:, :, 0:D], HIN[:])
                nc.vector.memset(H3[:, :, D:D + 1], 1.0)
                dve.drain()
                nc.vector.tensor_tensor(XC[:], HIN[:], H12[:, :, 0:D], ALU.subtract)
                dve.drain()
                nc.vector.tensor_copy(H12[:, :, D:2 * D], XC[:])
                dve.drain()
                nc.vector.tensor_tensor(H3[:, :, 0:D], XC[:], H12[:, :, D:2 * D], ALU.subtract)

            def count_sums(n):
                with dve.Fori(0, CHUNKS) as c:
                    dve.wait_ge(agg_done, c + (n + 1))
                    nc.vector.tensor_copy(TB[0:D + 1, :].rearrange("p (t d) -> p t d", t=2), psum[0:D + 1, 2:4, 0:HALF]).then_inc(agg_kept, 1)
                    dve.wait_ge(agg_turned, c + (n + 1))

            AGG3 = AGG[:, 0:NB * (D + 1)].rearrange("p (a f) -> p a f", a=NB)

            for (_, fo, _, a, _, a_rows, _, _, _) in att:
                nc.vector.tensor_scalar(a_rows[:], ones[0:fo, :], a[:, 0:1], None, ALU.mult)
            layernorm_relu(1)
            nc.vector.tensor_copy(stat[2][:], out_deg[:])
            root(2)
            nc.vector.tensor_tensor(HIN[:], HIN[:], per_node(stat[1]), ALU.mult)
            dve.drain()
            split_features()
            phase_end(dve, 5)
            count_sums(0)
            phase_end(dve, 6)
            nc.vector.tensor_copy(deg[:], AGG3[:, :, D])
            nc.vector.tensor_tensor(XC[:], AGG3[:, :, 0:D], HIN[:], ALU.subtract)
            dve.drain()
            nc.vector.tensor_scalar(stat[2][:], deg[:], -1.0, 1.0, ALU.add, ALU.max)
            root(3)
            nc.vector.tensor_tensor(XC[:], XC[:], per_node(stat[1]), ALU.mult)
            dve.drain()
            nc.vector.tensor_tensor(X[:], X[:], XC[:], ALU.add)
            dve.drain()
            layernorm_relu(4)
            for l, (ki, fo, W, a_src, a_dst, a_rows, _, _, _) in enumerate(att):
                dve.drain().then_inc(input_ready, 1)
                with dve.Fori(0, CHUNKS) as c:
                    dve.wait_ge(feats_done, c + (l * CHUNKS + 1))
                    HF3 = HF[:, 0:NB * (fo + 1)].rearrange("p (a f) -> p a f", a=NB)
                    nc.vector.tensor_copy(HF3[:, bass.ds(c * CB, CB), 0:fo], psum[:, 2, 0:CB * fo].rearrange("p (a f) -> p a f", a=CB)).then_inc(feats_kept, 1)
                    dve.wait_ge(scores_done, c + (l * CHUNKS + 1))
                    nc.vector.tensor_copy(ROW1[:, bass.ds(c * CW, CW)].rearrange("p (t d) -> p t d", t=2), psum[:, 5:7, 0:HALF])
                    nc.vector.tensor_scalar(sj8[:, bass.ds(c * CB, CB)], psum[:, 7, 0:CB], 1.0 - SLOPE, None, ALU.mult)
                    nc.vector.tensor_scalar(sj2[:, bass.ds(c * CB, CB)], psum[:, 7, 0:CB], SLOPE, None, ALU.mult)
                    nc.vector.tensor_copy(si[:, bass.ds(c * QC, QC)], psum[0:QW, 7, 16:16 + QC]).then_inc(scores_kept, 1)
                nc.vector.memset(HF3[:, :, fo:fo + 1], 1.0)
                dve.drain()
                nc.vector.tensor_reduce(low[:], ROW1[:], AX.X, ALU.min)
                dve.drain()
                nc.vector.tensor_scalar(ROW1[:], ROW1[:], low[:, 0:1], 1.0, ALU.subtract, ALU.add)
                phase_end(dve, 7 + 4 * l)
                with dve.Fori(0, NQ // 2) as b:
                    for s in range(2):
                        dve.wait_ge(link_in[s], b * 16 + (l * NQ // 2 + 1) * 16)
                        nc.vector.memset(top_now[:, s:s + 1], 0.0)
                        dve.drain()
                        nc.vector.tensor_tensor_reduce(out=junk[:], in0=link[:, s, :], in1=ROW1[0:QW, :], scale=1.0, scalar=0.0,
                                                       op0=ALU.mult, op1=ALU.max, accum_out=top_now[:, s:s + 1])
                        dve.drain().then_inc(link_free, 1)
                        nc.vector.tensor_copy(top[:, bass.ds(b * 2 + s, 1)], top_now[:, s:s + 1])
                dve.drain()
                nc.vector.tensor_scalar(top[:], top[:], low[0:QW, 0:1], -1.0, ALU.add, ALU.add)
                dve.drain()
                nc.vector.tensor_tensor(c1[:], si[:], top[:], ALU.add)
                dve.drain()
                nc.vector.scalar_tensor_tensor(top[:], c1[:], SLOPE, c1[:], ALU.mult, ALU.max)
                dve.drain()
                nc.vector.tensor_tensor(c1[:], si[:], top[:], ALU.subtract)
                nc.vector.scalar_tensor_tensor(c2[:], si[:], SLOPE, top[:], ALU.mult, ALU.subtract)
                phase_end(dve, 8 + 4 * l)
                with dve.Fori(0, NH) as h:
                    for k, (c, T) in enumerate(((c1, TA), (c2, TB))):
                        for q in range(4):
                            nc.vector.tensor_scalar(T[0:QW, q * QW:(q + 1) * QW], ident[0:QW, 0:QW], c[:, bass.ds(h * 4 + q, 1)], None, ALU.mult)
                    dve.drain().then_inc(diag_ready, 1)
                    dve.wait_ge(diag_spread, h + (l * NH + 1))
                phase_end(dve, 9 + 4 * l)

                def exponent(r, c):
                    if r >= 4:
                        dve.wait_ge(p_ready, c * NB + (l * ROWS + r - 3))
                    nc.vector.scalar_tensor_tensor(YE[:, r % 4, :], ROW1[:, bass.ds(c * CW, CW)], sj8[:, r:r + 1],
                                                   ROW2[:, bass.ds(c * CW, CW)], ALU.add, ALU.max).then_inc(y_ready, 1)

                with dve.Fori(0, CHUNKS) as c:
                    exponent(0, c)
                    exponent(1, c)
                    for r in range(NB):
                        if r + 2 < NB:
                            exponent(r + 2, c)
                        g, j = divmod(r, GRP)
                        if j == 0:
                            dve.wait_ge(cnt_in[g], c * 32 + 32 * ((1 + l) * CHUNKS + 1))
                        dve.wait_ge(e_ready, c * NB + (l * ROWS + r + 1))
                        dve.wait_ge(p_used, c * NB + (l * ROWS + max(r - 2, 0) + 1))
                        last = nc.vector.scalar_tensor_tensor(PW[:, r % 3, :], YE[:, r % 4, :], 1.0, counts_of(g, j), ALU.min, ALU.mult)
                        last.then_inc(p_ready, 1)
                        if j == GRP - 1:
                            dve.drain().then_inc(cnt_free, 1)
                phase_end(dve, 10 + 4 * l)
                A3 = AGG[:, 0:NB * (fo + 1)].rearrange("p (a f) -> p a f", a=NB)
                XO = XC[:, :, 0:fo]
                nc.vector.tensor_scalar(stat[0][:], A3[:, :, fo], DEN_EPS, None, ALU.add)
                dve.drain()
                nc.vector.reciprocal(stat[0][:], stat[0][:])
                dve.drain()
                nc.vector.tensor_tensor(XO, A3[:, :, 0:fo], per_node(stat[0], fo), ALU.mult)
                dve.drain()
                if l == 0:
                    nc.vector.tensor_tensor(XO, XO, per_feature(row['L1_gnn_b1'], fo), ALU.add)
                    dve.drain()
                    nc.vector.tensor_scalar(HIN[:, :, 0:fo], XO, 0.0, None, ALU.max)
                    dve.drain()
                if l == 1:
                    nc.vector.tensor_tensor(XO, XO, per_feature(row['L1_gnn_b2']), ALU.add)
                    dve.drain()
                    nc.vector.tensor_tensor(X[:], X[:], XO, ALU.add)
                    dve.drain()
                    layernorm_relu(5)
                if l == 2:
                    nc.vector.tensor_tensor(XO, XO, per_feature(row['L2_gnn_bias']), ALU.add)
                    dve.drain()
                    nc.vector.tensor_tensor(SQ[:], XO, XO, ALU.mult)
                    dve.drain()
                    nc.vector.tensor_reduce(stat[2][:], SQ[:], AX.X, ALU.add)
                    dve.drain().then_inc(root_in, 1)
                    dve.wait_ge(root_out, 6)
                    nc.vector.tensor_scalar(stat[1][:], stat[1][:], NORM_EPS, None, ALU.max)
                    dve.drain()
                    nc.vector.reciprocal(stat[1][:], stat[1][:])
                    dve.drain()
                    nc.vector.tensor_tensor(XO, XO, per_node(stat[1]), ALU.mult)
                    dve.drain()
                    nc.vector.tensor_tensor(X[:], X[:], XO, ALU.add)
                    dve.drain()
                    layernorm_relu(7)
            split_features()
            phase_end(dve, 19)
            count_sums(4 * CHUNKS)
            phase_end(dve, 20)
            nc.vector.tensor_tensor(US[:, :, 0:D], HIN[:], per_node(deg), ALU.mult)
            nc.vector.tensor_copy(US[:, :, D:2 * D], AGG3[:, :, 0:D])
            nc.vector.tensor_copy(DE[:, :, 0], deg[:])
            nc.vector.tensor_copy(DE[:, :, 1], ea_sum[:])
            dve.drain().then_inc(mlp_copied, 1)
            with dve.Fori(0, CHUNKS) as c:
                dve.wait_ge(mlp_turned, c + 1)
                nc.vector.tensor_copy(DET, banks(2, 2)[0:2, 0:CW]).then_inc(mlp_kept, 1)
                dve.wait_ge(mlp_out2, c + 1)
                both = banks(0, 2)[:, 0:CW].rearrange("p (a f) -> p a f", a=CB)
                nc.vector.tensor_copy(GI[:, bass.ds(c * CB, CB), :], both[:, :, 0:D])
                nc.vector.tensor_copy(HIN[:, bass.ds(c * CB, CB), :], both[:, :, D:2 * D])
                dve.drain().then_inc(mlp_stored, 1)
            split_features()
            phase_end(dve, 21)
            count_sums(5 * CHUNKS)
            phase_end(dve, 22)
            nc.vector.tensor_tensor(GI[:], GI[:], per_feature(row['L3_gnn_b2']), ALU.add)
            nc.vector.tensor_copy(XC[:], per_feature(row['we2']))
            dve.drain()
            nc.vector.tensor_tensor(GI[:], GI[:], per_node(deg), ALU.mult)
            nc.vector.tensor_tensor(XC[:], XC[:], per_node(ea_sum), ALU.mult)
            dve.drain()
            nc.vector.tensor_tensor(GI[:], GI[:], AGG3[:, :, 0:D], ALU.add)
            dve.drain()
            nc.vector.tensor_tensor(GI[:], GI[:], XC[:], ALU.add)
            dve.drain()
            nc.vector.tensor_scalar(GI[:], GI[:], 0.0, None, ALU.max)
            dve.drain()
            nc.vector.tensor_reduce(stat[0][:], GI[:], AX.X, ALU.max)
            dve.drain()
            nc.vector.tensor_tensor(GI[:], GI[:], per_node(stat[0]), ALU.subtract)
            dve.drain().then_inc(root_in, 1)
            dve.wait_ge(root_out, 8)
            nc.vector.tensor_reduce(stat[2][:], SQ[:], AX.X, ALU.add)
            dve.drain().then_inc(root_in, 1)
            dve.wait_ge(root_out, 9)
            nc.vector.tensor_tensor(GI[:], GI[:], per_node(stat[1]), ALU.subtract)
            dve.drain()
            nc.vector.tensor_tensor(X[:], X[:], GI[:], ALU.add)
            phase_end(dve, 23)

        @block.tensor
        def _(pe):
            phase_end(pe, 1)
            with pe.Fori(0, G) as g:
                pe.wait_ge(group_copied, g + 1)
                for k in range(5):
                    last = nc.tensor.transpose(banks(0, 2)[:, k * BLK:(k + 1) * BLK], grp[:, k, :], ident[:])
                last.then_inc(group_turned, 1)
                pe.wait_ge(group_kept, 2 * (g + 1))
            pe.wait_ge(hilo_ready, 1)
            for s in range(2):
                for q in range(4):
                    k = s * 4 + q
                    last = nc.tensor.transpose(banks(2, 2)[0:BQ, k * BLK:(k + 1) * BLK], hilo[:, s, q * BQ:(q + 1) * BQ], ident[:])
            last.then_inc(hilo_turned, 1)
            phase_end(pe, 2)
            pe.sem_inc(hist_used, 4)
            nc.tensor.matmul(psum[:, 0, 0:NB], zero16[:], ident16[:, 0:NB], start=True, stop=False, skip_group_check=True)
            with pe.Fori(0, TILES // 4) as i:
                for j in range(4):
                    pe.wait_ge(hist_ready, i * 4 + j + 1)
                    nc.tensor.matmul(psum[:, 0, 0:NB], hot_src[:, j, 0:BLK], hot_src[:, j, BLK:BLK + NB],
                                     start=False, stop=False, skip_group_check=True).then_inc(hist_used, 1)
            nc.tensor.matmul(psum[:, 0, 0:NB], zero16[:], ident16[:, 0:NB], start=False, stop=True,
                             skip_group_check=True).then_inc(hist_done, 1)
            phase_end(pe, 3)
            pe.sem_inc(slot_free, SL)
            pe.sem_inc(window_free, 2)
            pe.sem_inc(turned_kept, 1)
            visits = pe.alloc_register("pe_visits")
            pe.reg_mov(visits, 0)

            def turn(slot, q, r, n):
                pe.wait_ge(turned_kept, n + 1)
                for j in range(GRP):
                    last = nc.tensor.matmul(banks(4, 2)[0:QW, j * BLK:(j + 1) * BLK],
                                            ap1(stage[:, bass.ds(slot, 1), bass.ds((r * GRP + j) * HALF + q * QW, QW)]),
                                            ident16[:], start=True, stop=True)
                last.then_inc(turned, 1)

            with pe.Fori(0, NH) as h:
                with pe.Fori(0, 4) as q:
                    with pe.Fori(0, GRP) as r:
                        w = h * 28 + q * 7 + r
                        lo = pe.value_load(bounds[0:1, bass.ds(w + NWIN, 1)], min_val=0, max_val=TILES // 2 - 1)
                        hi = pe.value_load(bounds[0:1, bass.ds(w, 1)], min_val=1, max_val=TILES // 2)
                        pe.wait_ge(window_free, w + 1)
                        buf = (q + r) % 2

                        def bank(k, n0, n1, buf=buf):
                            return ap1(psum[:, bass.ds(buf * 2 + k, 1), n0:n1])

                        for k in range(2):
                            nc.tensor.matmul(bank(k, 0, 4), zero16[:], ident16[:, 0:4], start=True, stop=False, skip_group_check=True)
                        with pe.Fori(lo, hi) as i:
                            v = pe.snap(visits)
                            pe.wait_ge(keys_ready, v + 1)
                            s = v % SL
                            for t in range(2):
                                src = ap1(hot_src[:, bass.ds(s, 1), t * BLK:(t + 1) * BLK])
                                at = t * NB * WIN
                                nc.tensor.matmul(bank(0, 0, A0 * WIN), src, ap1(hot_key[:, bass.ds(s, 1), at:at + A0 * WIN]),
                                                 start=False, stop=False, skip_group_check=True)
                                nc.tensor.matmul(bank(1, 0, A1 * WIN), src, ap1(hot_key[:, bass.ds(s, 1), at + A0 * WIN:at + NB * WIN]),
                                                 start=False, stop=False, skip_group_check=True)
                                last = nc.tensor.matmul(bank(1, 400, 403), ap1(hot_dst[:, bass.ds(s, 1), t * BLK:(t + 1) * BLK]),
                                                        ap1(ea3[:, bass.ds(i * 2 + t, 1), :]),
                                                        start=False, stop=False, skip_group_check=True)
                            last.then_inc(slot_free, 1)
                            pe.reg_add(visits, visits, 1)
                        for k in range(2):
                            last = nc.tensor.matmul(bank(k, 0, 4), zero16[:], ident16[:, 0:4], start=False, stop=True, skip_group_check=True)
                        last.then_inc(window_done, 1)
                        turn((h + 1) % 2, q, r, w)
                pe.wait_ge(stage_ready, h + 1)
            with pe.Fori(0, 4) as q:
                with pe.Fori(0, GRP) as r:
                    turn((NH - 1) % 2, q, r, q * 7 + r + NWIN)
            phase_end(pe, 4)
            def count_sums(L, kept):
                with pe.Fori(0, CHUNKS) as c:
                    for g in range(NGRP):
                        pe.wait_ge(cnt_in[g], c * 32 + 32 * (L * CHUNKS + 1))
                        for j in range(GRP):
                            r = g * GRP + j
                            for k, part_of in enumerate((H12[:, r, :], H3[:, r, :])):
                                for t in range(2):
                                    to = psum[:, 2 * k + t, 0:HALF] if k == 0 else psum[0:D + 1, 2 * k + t, 0:HALF]
                                    last = nc.tensor.matmul(to, part_of, counts_of(g, j)[:, t * HALF:(t + 1) * HALF],
                                                            start=(r == 0), stop=(r == NB - 1))
                        if g < NGRP - 1:
                            last.then_inc(cnt_free, 1)
                    last.then_inc(agg_done, 1)
                    pe.wait_ge(agg_kept, c * 2 + (kept + 2))
                    pe.sem_inc(cnt_free, 1)
                    for b in range(CB):
                        to = psum[:, 4, b * (D + 1):(b + 1) * (D + 1)]
                        nc.tensor.matmul(to, TA[:, b * BLK:(b + 1) * BLK], fold[:], start=True, stop=False)
                        last = nc.tensor.matmul(to, TB[0:D + 1, b * BLK:(b + 1) * BLK], ident[0:D + 1, 0:D + 1], start=False, stop=True)
                    last.then_inc(agg_turned, 1)

            phase_end(pe, 5)
            count_sums(0, 0)
            phase_end(pe, 6)
            for l, (ki, fo, W, a_src, a_dst, a_rows, _, _, _) in enumerate(att):
                with pe.Fori(0, CHUNKS) as c:
                    n = l * CHUNKS + 1
                    pe.wait_ge(input_placed, c * 2 + (2 * n - 1))
                    for b in range(CB):
                        last = nc.tensor.matmul(banks(0, 2)[0:ki, b * BLK:(b + 1) * BLK], TA[:, b * ki:(b + 1) * ki], ident[:],
                                                start=True, stop=True)
                    last.then_inc(input_turned, 1)
                    pe.wait_ge(input_placed, c * 2 + 2 * n)
                    for b in range(CB):
                        nc.tensor.matmul(psum[:, 2, b * fo:(b + 1) * fo], TB[0:ki, b * BLK:(b + 1) * BLK], W[:], start=True, stop=True)
                    for t in range(2):
                        last = nc.tensor.matmul(psum[0:fo, 3 + t, 0:HALF], W[:], TB[0:ki, t * HALF:(t + 1) * HALF], start=True, stop=True)
                    last.then_inc(feats_done, 1)
                    pe.wait_ge(feats_kept, c * 2 + 2 * n)
                    for t in range(2):
                        nc.tensor.matmul(psum[:, 5 + t, 0:HALF], a_rows[:], YE[0:fo, 0, t * HALF:(t + 1) * HALF], start=True, stop=True)
                    for b in range(CB):
                        nc.tensor.matmul(psum[:, 7, b:b + 1], YE[0:fo, 0, b * BLK:(b + 1) * BLK], a_src[:], start=True, stop=True)
                    for q in range(QC):
                        last = nc.tensor.matmul(psum[0:QW, 7, 16 + q:17 + q], YE[0:fo, 0, q * QW:(q + 1) * QW], a_dst[:], start=True, stop=True)
                    last.then_inc(scores_done, 1)
                phase_end(pe, 7 + 4 * l)
                phase_end(pe, 8 + 4 * l)
                with pe.Fori(0, NH) as h:
                    pe.wait_ge(diag_ready, h + (l * NH + 1))
                    pe.wait_ge(diag_kept, h + (l * NH + 1))
                    nc.tensor.matmul(psum[:, 0, 0:HALF], ones[0:QW, :], TA[0:QW, 0:HALF], start=True, stop=True)
                    nc.tensor.matmul(psum[:, 1, 0:HALF], ones[0:QW, :], TB[0:QW, 0:HALF], start=True, stop=True).then_inc(diag_spread, 1)
                phase_end(pe, 9 + 4 * l)
                if l == 0:
                    pe.sem_inc(p_used, 1)
                with pe.Fori(0, CHUNKS) as c:
                    for r in range(NB):
                        pe.wait_ge(p_ready, c * NB + (l * ROWS + r + 1))
                        for t in range(2):
                            last = nc.tensor.matmul(psum[0:fo + 1, t, 0:HALF], HF[:, r * (fo + 1):(r + 1) * (fo + 1)],
                                                    PW[:, r % 3, t * HALF:(t + 1) * HALF], start=(r == 0), stop=(r == NB - 1))
                        last.then_inc(p_used, 1)
                    pe.drain().then_inc(agg_done, 1)
                    pe.wait_ge(agg_kept, c + (2 * CHUNKS + l * CHUNKS + 1))
                    for b in range(CB):
                        last = nc.tensor.matmul(psum[:, 4, b * (fo + 1):(b + 1) * (fo + 1)], TA[0:fo + 1, b * BLK:(b + 1) * BLK],
                                                ident[0:fo + 1, 0:fo + 1], start=True, stop=True)
                    last.then_inc(agg_turned, 1)
                phase_end(pe, 10 + 4 * l)
            phase_end(pe, 19)
            count_sums(4, CHUNKS * 5)
            phase_end(pe, 20)
            with pe.Fori(0, CHUNKS) as c:
                pe.wait_ge(mlp_copied, c + 2)
                for b in range(CB):
                    nc.tensor.transpose(banks(0, 2)[:, b * BLK:(b + 1) * BLK], TA[:, b * BLK:(b + 1) * BLK], ident[:])
                    last = nc.tensor.transpose(banks(2, 2)[0:2, b * BLK:(b + 1) * BLK], TD[:, b * 2:b * 2 + 2], ident[:])
                last.then_inc(mlp_turned, 1)
                pe.wait_ge(mlp_kept, c * 2 + 2)
                for b in range(CB):
                    to = banks(4, 2)[:, b * BLK:(b + 1) * BLK]
                    nc.tensor.matmul(to, TB[:, b * BLK:(b + 1) * BLK], W3a[:], start=True, stop=False)
                    last = nc.tensor.matmul(to, DET[:, b * BLK:(b + 1) * BLK], W3b[:], start=False, stop=True)
                last.then_inc(mlp_out, 1)
                pe.wait_ge(mlp_relu, c + 1)
                for b in range(CB):
                    last = nc.tensor.transpose(banks(6, 2)[:, b * BLK:(b + 1) * BLK], TA[:, b * BLK:(b + 1) * BLK], ident[:])
                last.then_inc(mlp_turned2, 1)
                pe.wait_ge(mlp_kept2, c + 1)
                for b in range(CB):
                    last = nc.tensor.matmul(banks(0, 2)[:, b * BLK:(b + 1) * BLK], TB[:, b * BLK:(b + 1) * BLK],
                                            W4[:].rearrange("k t f -> k (t f)"), start=True, stop=True)
                last.then_inc(mlp_out2, 1)
            phase_end(pe, 21)
            count_sums(5, CHUNKS * 7)
            phase_end(pe, 22)
            phase_end(pe, 23)

        @block.scalar
        def _(act):
            phase_end(act, 1)
            with act.Fori(0, G) as g:
                nc.scalar.copy(grp[:], raw[:, :, bass.ds(g * BLK, BLK)]).then_inc(group_copied, 1)
                act.wait_ge(group_turned, g + 1)
                nc.scalar.copy(et[:, :, bass.ds(g * BLK, BLK)], psum[:, 0, :].rearrange("p (k n) -> p k n", k=4)).then_inc(group_kept, 1)
                nc.scalar.copy(ea_rest[:, bass.ds(g * BLK, BLK)], psum[:, 1, 0:BLK]).then_inc(group_kept, 1)
            phase_end(act, 2)
            phase_end(act, 3)
            act.sem_inc(stage_free, 2)
            act.sem_inc(linked_free, 6)
            with act.Fori(0, NH) as h:
                act.wait_ge(stage_free, h + 1)
                with act.Fori(0, 4) as q:
                    act.wait_ge(linked_free, h * 4 + q + 1)
                    with act.Fori(0, GRP) as r:
                        w = h * 28 + q * 7 + r
                        act.wait_ge(window_done, w + 1)
                        buf = (q + r) % 2
                        to = ap1(stage[:, bass.ds(h % 2, 1), :]).rearrange("p (a d) -> p a d", a=NB)
                        to = to[:, :, bass.ds((q * 7 + r) * WIN, WIN)]
                        nc.scalar.copy(to[:, 0:A0, :], ap1(psum[:, bass.ds(buf * 2, 1), 0:A0 * WIN]).rearrange("p (a d) -> p a d", a=A0))
                        nc.scalar.copy(to[:, A0:NB, :], ap1(psum[:, bass.ds(buf * 2 + 1, 1), 0:A1 * WIN]).rearrange("p (a d) -> p a d", a=A1))
                        nc.scalar.copy(ap1(ea_win[:, bass.ds(w, 1), :]), ap1(psum[0:WIN, bass.ds(buf * 2 + 1, 1), 400:403])).then_inc(window_free, 1)
                        act.wait_ge(turned, w + 1)
                        nc.scalar.activation(ap1(linked_sb[:, bass.ds(q % 2, 1), bass.ds(r * CW, CW)]), banks(4, 2)[0:QW, 0:CW],
                                             ACT.Sign).then_inc(turned_kept, 1)
                    act.drain().then_inc(linked_full, 1)
                act.drain().then_inc(stage_full, 1)
            act.drain().then_inc(ea_copied, 1)
            with act.Fori(0, 4) as q:
                act.wait_ge(linked_free, NH * 4 + q + 1)
                with act.Fori(0, GRP) as r:
                    act.wait_ge(turned, NWIN + q * 7 + r + 1)
                    nc.scalar.activation(ap1(linked_sb[:, bass.ds(q % 2, 1), bass.ds(r * CW, CW)]), banks(4, 2)[0:QW, 0:CW],
                                         ACT.Sign).then_inc(turned_kept, 1)
                act.drain().then_inc(linked_full, 1)
            phase_end(act, 4)
            def root(k):
                act.wait_ge(root_in, k)
                nc.scalar.activation(stat[1][:], stat[2][:], ACT.Sqrt).then_inc(root_out, 1)

            def count_sums(n):
                with act.Fori(0, CHUNKS) as c:
                    act.wait_ge(agg_done, c + (n + 1))
                    nc.scalar.copy(TA[:].rearrange("p (t d) -> p t d", t=2), psum[:, 0:2, 0:HALF]).then_inc(agg_kept, 1)
                    act.wait_ge(agg_turned, c + (n + 1))
                    nc.scalar.copy(AGG[:, bass.ds(c * CB * (D + 1), CB * (D + 1))], psum[:, 4, 0:CB * (D + 1)])

            root(1)
            root(2)
            phase_end(act, 5)
            count_sums(0)
            phase_end(act, 6)
            root(3)
            root(4)
            for l, (ki, fo, W, a_src, a_dst, a_rows, _, _, _) in enumerate(att):
                act.wait_ge(input_ready, l + 1)
                with act.Fori(0, CHUNKS) as c:
                    n = l * CHUNKS + 1
                    nc.scalar.copy(TA[:, 0:CB * ki].rearrange("p (a f) -> p a f", a=CB), HIN[:, bass.ds(c * CB, CB), 0:ki]).then_inc(input_placed, 1)
                    act.wait_ge(input_turned, c + n)
                    nc.scalar.copy(TB[0:ki, :], banks(0, 2)[0:ki, 0:CW]).then_inc(input_placed, 1)
                    act.wait_ge(feats_done, c + n)
                    nc.scalar.copy(YE[0:fo, 0, :].rearrange("p (t d) -> p t d", t=2), psum[0:fo, 3:5, 0:HALF]).then_inc(feats_kept, 1)
                    act.wait_ge(scores_kept, c + n)
                phase_end(act, 7 + 4 * l)
                phase_end(act, 8 + 4 * l)
                if l == 0:
                    act.sem_inc(diag_kept, 1)
                with act.Fori(0, NH) as h:
                    act.wait_ge(diag_spread, h + (l * NH + 1))
                    nc.scalar.copy(ROW1[:, bass.ds(h * HALF, HALF)], psum[:, 0, 0:HALF])
                    nc.scalar.copy(ROW2[:, bass.ds(h * HALF, HALF)], psum[:, 1, 0:HALF]).then_inc(diag_kept, 1)
                phase_end(act, 9 + 4 * l)
                with act.Fori(0, CHUNKS) as c:
                    for r in range(NB):
                        act.wait_ge(y_ready, c * NB + (l * ROWS + r + 1))
                        nc.scalar.activation(YE[:, r % 4, :], YE[:, r % 4, :], ACT.Exp, bias=sj2[:, r:r + 1]).then_inc(e_ready, 1)
                    act.wait_ge(agg_done, c + (CHUNKS + l * CHUNKS + 1))
                    nc.scalar.copy(TA[0:fo + 1, :].rearrange("p (t d) -> p t d", t=2), psum[0:fo + 1, 0:2, 0:HALF]).then_inc(agg_kept, 1)
                    act.wait_ge(agg_turned, c + (CHUNKS + l * CHUNKS + 1))
                    nc.scalar.copy(AGG[:, bass.ds(c * CB * (fo + 1), CB * (fo + 1))], psum[:, 4, 0:CB * (fo + 1)])
                phase_end(act, 10 + 4 * l)
                if l == 1:
                    root(5)
                if l == 2:
                    root(6)
                    root(7)
            phase_end(act, 19)
            count_sums(CHUNKS * 4)
            phase_end(act, 20)
            act.wait_ge(mlp_copied, 1)
            with act.Fori(0, CHUNKS) as c:
                nc.scalar.copy(TD[:, 0:2 * CB].rearrange("p (a f) -> p a f", a=CB), DE[:, bass.ds(c * CB, CB), :])
                nc.scalar.copy(TA[:].rearrange("p (a f) -> p a f", a=CB), US[:, bass.ds(c * CB, CB), :]).then_inc(mlp_copied, 1)
                act.wait_ge(mlp_turned, c + 1)
                nc.scalar.copy(TB[:], banks(0, 2)[:, 0:CW]).then_inc(mlp_kept, 1)
                act.wait_ge(mlp_out, c + 1)
                nc.scalar.activation(TA[:], banks(4, 2)[:, 0:CW], ACT.Relu).then_inc(mlp_relu, 1)
                act.wait_ge(mlp_turned2, c + 1)
                nc.scalar.copy(TB[:], banks(6, 2)[:, 0:CW]).then_inc(mlp_kept2, 1)
                act.wait_ge(mlp_stored, c + 1)
            phase_end(act, 21)
            count_sums(CHUNKS * 5)
            phase_end(act, 22)
            act.wait_ge(root_in, 8)
            nc.scalar.activation(SQ[:], GI[:], ACT.Exp).then_inc(root_out, 1)
            act.wait_ge(root_in, 9)
            nc.scalar.activation(stat[1][:], stat[2][:], ACT.Ln).then_inc(root_out, 1)
            phase_end(act, 23)


_INS = ['x', 'src', 'dst', 'edge_weight1', 'L1_gnn_W1', 'L1_gnn_a_src1', 'L1_gnn_a_dst1', 'L1_gnn_b1', 'L1_gnn_W2',
        'L1_gnn_a_src2', 'L1_gnn_a_dst2', 'L1_gnn_b2', 'L2_gnn_weight', 'L2_gnn_att', 'L2_gnn_bias', 'L3_gnn_W1',
        'L3_gnn_b1', 'L3_gnn_W2', 'L3_gnn_b2']


def kernel(**inputs):
    import numpy as _np
    import concourse.bacc as _bacc
    from concourse import mybir as _mybir
    from concourse.bass_utils import run_bass_kernel_spmd as _run

    nc = _bacc.Bacc("TRN2", target_bir_lowering=False, num_devices=1)
    arrays, aps = {}, {}
    for name in _INS:
        a = _np.ascontiguousarray(inputs[name])
        arrays["in_" + name] = a
        aps[name] = nc.dram_tensor("in_" + name, a.shape, _mybir.dt.from_np(a.dtype), kind="ExternalInput").ap()
    out = nc.dram_tensor("out_0", (N, D), _mybir.dt.from_np(_np.dtype("float32")), kind="ExternalOutput").ap()
    gnn_kernel(nc, aps, out)
    r = _run(nc, [arrays], core_ids=[0])
    return r.results[0]["out_0"]
```

```python
import concourse.bass as bass
from concourse import mybir
from contextlib import ExitStack

N = 6250
E = 200000
D = 64
BLK = 128
NB = -(-N // BLK)
NP = NB * BLK
CHUNKS = 7
CB = NB // CHUNKS
CW = CB * BLK
HALF = CW // 2
NH = 2 * CHUNKS
GRP = 7
NGRP = NB // GRP
QW = HALF // 4
NQ = NP // QW
QC = CW // QW
WIN = 16
NWIN = NP // WIN
HT = 16
TILES = -(-E // (BLK * HT)) * HT
G = -(-TILES // BLK)
FULL = (E // BLK) // BLK
KEY = 64
A0 = 25
A1 = NB - A0
BQ = NWIN // 4
SUB = 8
SUBS = BLK // SUB
ST = 3
CAP = ST * BLK
WS = 7
LN_EPS = 1e-5
DEN_EPS = 1e-16
NORM_EPS = 1e-12
SLOPE = 0.2

fp32 = mybir.dt.float32
fp16 = mybir.dt.float16
bf16 = mybir.dt.bfloat16
i32 = mybir.dt.int32
ALU = mybir.AluOpType
ACT = mybir.ActivationFunctionType
AX = mybir.AxisListType


def gnn_kernel(nc, ap, out):
    ctx = ExitStack()
    with ctx:
        def sb(name, shape, dt):
            return ctx.enter_context(nc.sbuf_tensor("sb_" + name, shape, dt))

        def sem(name):
            return ctx.enter_context(nc.semaphore(name))

        counts = nc.dram_tensor("counts", (NH + 1, BLK, NB, HALF), fp16, kind="Internal").ap()
        linked = nc.dram_tensor("linked", (NQ + 4, QW, NP), fp16, kind="Internal").ap()
        bounds_dram = nc.dram_tensor("bounds_dram", (2, NWIN), i32, kind="Internal").ap()
        records = nc.dram_tensor("records", (TILES * BLK, 2), fp32, kind="Internal").ap()
        starts_dram = nc.dram_tensor("starts_dram", (2 * NWIN,), i32, kind="Internal").ap()

        X = sb("X", [BLK, NB, D], fp32)
        ident = sb("ident", [BLK, BLK], fp32)
        ident16 = sb("ident16", [BLK, BLK], fp16)
        zero16 = sb("zero16", [BLK, BLK], fp16)
        iota_f = sb("iota_f", [BLK, BLK], fp32)
        iota_b = sb("iota_b", [BLK, BLK], fp16)
        zero_b = sb("zero_b", [BLK, 4 * NB], bf16)
        ones = sb("ones", [BLK, BLK], fp32)
        fold = sb("fold", [BLK, D + 1], fp32)
        part = sb("part", [BLK, 1], fp32)
        out_deg = sb("out_deg", [BLK, NB], fp32)
        ea_sum = sb("ea_sum", [BLK, NB], fp32)
        deg = sb("deg", [BLK, NB], fp32)
        sub_rows = sb("sub_rows", [BLK, 2, SUBS], fp32)
        misfit = sb("misfit", [BLK, 4], fp32)
        ARENA = 184 * 1024
        arena = sb("arena", [BLK, ARENA // 4], fp32)

        def view(offset, shape, dt):
            size = 2 if dt in (fp16, bf16) else 4
            for s in shape[1:]:
                size *= s
            words = -(-size // 4)
            assert offset % 4 == 0 and offset + 4 * words <= ARENA, (offset, shape)
            v = arena[0:shape[0], offset // 4:offset // 4 + words]
            if dt != fp32:
                v = v.bitcast(dt)
            if len(shape) == 3:
                v = v[:, 0:shape[1] * shape[2]].rearrange("p (a b) -> p a b", a=shape[1])
            if len(shape) == 4:
                v = v[:, 0:shape[1] * shape[2] * shape[3]].rearrange("p (a b c) -> p a b c", a=shape[1], b=shape[2])
            return v, offset + 4 * words

        psum = ctx.enter_context(nc.psum_tensor("psum", [BLK, 8, 512], fp32))

        def banks(first, count):
            return psum[:, first:first + count, :].rearrange("p k n -> p (k n)")

        SL = 4
        stage, o = view(0, [BLK, 2, NB * HALF], fp16)
        linked_sb, o = view(o, [QW, 2, NP], fp16)
        bounds, o = view(o, [1, 2 * NWIN], i32)
        starts, o = view(o, [1, 2 * NWIN + 8], i32)
        iota_t, o = view(o, [BLK, BLK, HT], bf16)
        neg_key, o = view(o, [BLK, NWIN], fp32)
        build_at = o
        et, o = view(o, [BLK, 4, G * BLK], fp32)
        key_t, srcb_t, srca_t, dst_t = (et[:, k, :] for k in range(4))
        key_iota, o = view(o, [BLK, NB, WIN], fp16)
        hot_key, o = view(o, [BLK, SL, 2 * NB * WIN], fp16)
        hot_src, o = view(o, [BLK, SL, 2 * BLK], fp16)
        sub_iota, o = view(build_at, [BLK, 2, NB * SUB], fp16)
        rec, o = view(o, [BLK, WS, 2, ST * 2], fp32)
        key_rel, o = view(o, [BLK, WS, 2 * ST], fp32)
        src_rel, o = view(o, [BLK, WS, 2 * ST], bf16)
        sub_key, o = view(o, [BLK, WS, 2 * ST, NB * SUB], fp16)
        sub_src, o = view(o, [BLK, WS * BLK, 2 * ST], bf16)
        sub_src = sub_src.rearrange("p (w b) t -> p w b t", w=WS)
        dst_i, o = view(0, [BLK, G * BLK], i32)
        src_i, o = view(o, [BLK, G * BLK], i32)
        tmp_i, o = view(o, [BLK, G * BLK], i32)
        falls_at, _ = view(4 * G * BLK, [BLK, G * BLK], fp32)
        next_i, o = view(o, [BLK, G], i32)
        raw, o = view(o, [BLK, 5, G * BLK], fp32)
        record, o = view(o, [BLK, G * BLK, 2], fp32)
        grp, o = view(o, [BLK, 5, BLK], fp32)
        win_first, o = view(o, [BLK, NWIN], fp32)
        win_last, o = view(o, [BLK, NWIN], fp32)
        over, o = view(o, [BLK, 2, NWIN], fp32)
        hilo, o = view(o, [BLK, 2, NWIN], fp32)
        tile_lo, o = view(o, [BLK, G], fp32)
        tile_hi, o = view(o, [BLK, G], fp32)
        tile_up, o = view(o, [BLK, G], fp32)
        tile_dn, o = view(o, [BLK, G], fp32)
        next_f, o = view(o, [BLK, G], fp32)
        hl_max, o = view(o, [BQ, 8], fp32)
        hl_int, o = view(o, [BQ, 8], i32)
        assert o <= 2 * NB * HALF * 2
        ea_rest, o = view(0, [BLK, G * BLK], fp32)
        ea_part, o = view(o, [BLK, G * BLK], fp32)
        ea3, o = view(o, [BLK, 3, G * BLK], bf16)
        hist_b, o = view(o, [BLK, 2, G * BLK], bf16)
        hist_a, o = view(o, [BLK, 2, G * BLK], bf16)
        ints, _ = view(o, [BLK, 2, G * BLK], i32)
        hot_b, o = view(o, [BLK, 4, BLK * HT], bf16)
        hot_a, o = view(o, [BLK, 10, NB * HT], bf16)
        in_deg, o = view(o, [BLK, 1, NB], fp32)
        prefix, o = view(o, [BLK, 2, NB], fp32)
        sub_at, o = view(o, [SUBS, NB], i32)
        sub_max, o = view(o, [SUBS, 2], fp32)
        misfit_top, o = view(o, [1, 1], fp32)
        assert o <= 2 * NB * HALF * 2

        phase_done = sem("phase_done")
        iotas_done = sem("iotas_done")
        pads_set = sem("pads_set")
        edges_in = sem("edges_in")
        x_in = sem("x_in")
        group_copied = sem("group_copied")
        group_turned = sem("group_turned")
        group_kept = sem("group_kept")
        hilo_turned = sem("hilo_turned")
        bounds_ready = sem("bounds_ready")
        bounds_out = sem("bounds_out")
        bounds_in = sem("bounds_in")
        hist_ready = sem("hist_ready")
        hist_used = sem("hist_used")
        hist_done = sem("hist_done")
        keys_ready = sem("keys_ready")
        slot_free = sem("slot_free")
        window_done = sem("window_done")
        window_free = sem("window_free")
        stage_full = sem("stage_full")
        stage_ready = sem("stage_ready")
        stage_free = sem("stage_free")
        counts_out = sem("counts_out")
        turned = sem("turned")
        turned_kept = sem("turned_kept")
        linked_full = sem("linked_full")
        linked_out = sem("linked_out")
        linked_free = sem("linked_free")
        hilo_ready = sem("hilo_ready")
        record_ready = sem("record_ready")
        record_out = sem("record_out")
        degrees_ready = sem("degrees_ready")
        starts_summed = sem("starts_summed")
        starts_ready = sem("starts_ready")
        starts_out = sem("starts_out")
        misfit_ready = sem("misfit_ready")
        misfit_turned = sem("misfit_turned")
        flag_ready = sem("flag_ready")
        rec_in = [sem("rec_in%d" % s) for s in range(WS)]
        rel_ready = sem("rel_ready")
        turn_done = sem("turn_done")
        counts_stored = sem("counts_stored")
        linked_stored = [sem("linked_stored%d" % s) for s in range(2)]

        def phase_end(eng, k):
            eng.drain().then_inc(phase_done, 1)
            eng.wait_ge(phase_done, 5 * k)

        block = ctx.enter_context(nc.Block())

        halves16 = ident16[:].rearrange("p (t n) -> p t n", t=2)

        def ap1(v):
            return v.rearrange("p o n -> p (o n)")

        HIN, o = view(0, [BLK, NB, D], fp32)
        AGG, o = view(o, [BLK, NB * (D + 1)], fp32)
        at = o
        H12, o = view(o, [BLK, NB, 2 * D], bf16)
        H3, o = view(o, [BLK, NB, D + 1], bf16)
        HF, _ = view(at, [BLK, NB * (D + 1)], fp32)
        cnt, at = view(o, [BLK, 3, GRP * CW], fp16)
        link, o = view(o, [QW, 2, NP], fp16)
        o = at
        ROW1, o = view(o, [BLK, NP], fp32)
        at = o
        ROW2, o = view(o, [BLK, NP], fp32)
        junk, _ = view(at, [QW, NP], fp16)
        US, _ = view(at, [BLK, NB, 2 * D], fp32)
        DE, _ = view(at - 4 * NP, [BLK, NB, 2], fp32)
        XC, at = view(at - 4 * NP, [BLK, NB, D], fp32)
        SQ, at = view(at, [BLK, NB, D], fp32)
        YE, o = view(o, [BLK, 4, CW], fp32)
        PW, o = view(o, [BLK, 3, CW], fp32)
        TA, o = view(o, [BLK, CW], fp32)
        TB, o = view(o, [BLK, CW], fp32)
        GI, o = view(o, [BLK, NB, D], fp32)
        TD = YE[:, 0, :]
        DET = YE[0:2, 1, :]
        stat = [sb("stat%d" % k, [BLK, NB], fp32) for k in range(3)]
        sj8 = sb("sj8", [BLK, NB], fp32)
        sj2 = sb("sj2", [BLK, NB], fp32)
        si = sb("si", [QW, NQ], fp32)
        top = sb("top", [QW, NQ], fp32)
        top_now = sb("top_now", [QW, 2], fp32)
        c1 = sb("c1", [QW, NQ], fp32)
        c2 = sb("c2", [QW, NQ], fp32)
        low = sb("low", [BLK, 1], fp32)
        W3a = sb("W3a", [BLK, BLK], fp32)
        W3b = sb("W3b", [2, BLK], fp32)
        W4 = sb("W4", [BLK, 2, D], fp32)
        row = {k: sb("row_" + k, [BLK, n], fp32) for k, n in
               (('L1_gnn_b1', 32), ('L1_gnn_b2', D), ('L2_gnn_bias', D), ('L3_gnn_b2', D), ('we2', D))}
        att = []
        for l, (ki, fo, wn, an, dn) in enumerate((
                (D, 32, ap['L1_gnn_W1'], ap['L1_gnn_a_src1'], ap['L1_gnn_a_dst1']),
                (32, D, ap['L1_gnn_W2'], ap['L1_gnn_a_src2'], ap['L1_gnn_a_dst2']),
                (D, D, ap['L2_gnn_weight'], ap['L2_gnn_att'][D:2 * D], ap['L2_gnn_att'][0:D]))):
            att.append((ki, fo, sb("W_att%d" % l, [ki, fo], fp32), sb("a_src%d" % l, [fo, 1], fp32),
                        sb("a_dst%d" % l, [fo, 1], fp32), sb("a_rows%d" % l, [fo, BLK], fp32), wn, an, dn))

        weights_in = sem("weights_in")
        input_ready = sem("input_ready")
        input_placed = sem("input_placed")
        input_turned = sem("input_turned")
        feats_done = sem("feats_done")
        feats_kept = sem("feats_kept")
        scores_done = sem("scores_done")
        scores_kept = sem("scores_kept")
        link_in = [sem("link_in%d" % s) for s in range(2)]
        link_free = sem("link_free")
        diag_ready = sem("diag_ready")
        diag_spread = sem("diag_spread")
        diag_kept = sem("diag_kept")
        cnt_in = [sem("cnt_in%d" % g) for g in range(NGRP)]
        cnt_free = sem("cnt_free")
        y_ready = sem("y_ready")
        e_ready = sem("e_ready")
        p_ready = sem("p_ready")
        p_used = sem("p_used")
        agg_done = sem("agg_done")
        agg_kept = sem("agg_kept")
        agg_turned = sem("agg_turned")
        agg_stored = sem("agg_stored")
        root_in = sem("root_in")
        root_out = sem("root_out")
        mlp_copied = sem("mlp_copied")
        mlp_turned = sem("mlp_turned")
        mlp_kept = sem("mlp_kept")
        mlp_out = sem("mlp_out")
        mlp_relu = sem("mlp_relu")
        mlp_turned2 = sem("mlp_turned2")
        mlp_kept2 = sem("mlp_kept2")
        mlp_out2 = sem("mlp_out2")
        mlp_stored = sem("mlp_stored")
        out_stored = sem("out_stored")

        ROWS = CHUNKS * NB

        def load_counts(sp, L):
            with sp.Fori(0, CHUNKS) as c:
                for g in range(NGRP):
                    before = (0, -2, -1, 1, 2, 3, 4)[g]
                    sp.wait_ge(cnt_free, c * NGRP + (L * ROWS // GRP + 3 + before))
                    to = cnt[:, g % 3, :].rearrange("p (a t d) -> p a t d", a=GRP, t=2)
                    for t in range(2):
                        sp.dma_start(to[:, :, t, :], counts[bass.ds(c * 2 + (t + 1), 1), :, g * GRP:(g + 1) * GRP, :].rearrange("o b a d -> b (o a) d")
                                     ).then_inc(cnt_in[g], 16)

        def counts_of(g, j):
            return cnt[:, g % 3, j * CW:(j + 1) * CW]

        @block.sync
        def _(sp):
            sp.wait_ge(pads_set, 5)
            sp.dma_start(X[:, 0:NB - 1, :], ap['x'][0:(NB - 1) * BLK, :].rearrange("(a b) f -> b a f", b=BLK)).then_inc(x_in, 16)
            sp.dma_start(X[0:N - (NB - 1) * BLK, NB - 1, :], ap['x'][(NB - 1) * BLK:N, :]).then_inc(x_in, 16)
            whole = E // BLK - FULL * BLK
            for flat, to in ((ap['dst'], dst_i), (ap['src'], src_i), (ap['edge_weight1'].rearrange("e o -> (e o)"), raw[:, 4, :])):
                to3 = to.rearrange("p (g e) -> p g e", g=G)
                at = FULL * BLK * BLK
                sp.dma_start(to3[:, 0:FULL, :], flat[0:at].rearrange("(g p e) -> p g e", p=BLK, e=BLK)).then_inc(edges_in, 16)
                sp.dma_start(to3[0:whole, FULL, :], flat[at:at + whole * BLK].rearrange("(p e) -> p e", e=BLK)).then_inc(edges_in, 16)
                sp.dma_start(to3[whole:whole + 1, FULL, 0:E % BLK],
                             flat[at + whole * BLK:E].rearrange("(o e) -> o e", o=1)).then_inc(edges_in, 16)
            sp.dma_start(next_i[:, 0:FULL], ap['dst'][BLK:BLK + FULL * BLK * BLK].rearrange("(g p e) -> p g e", p=BLK, e=BLK)[:, :, 0],
                         allow_slow_non_contiguous=True).then_inc(edges_in, 16)
            at = FULL * BLK * BLK + BLK
            sp.dma_start(next_i[0:whole - 1, FULL:FULL + 1], ap['dst'][at:at + (whole - 1) * BLK].rearrange("(p e) -> p e", e=BLK)[:, 0:1],
                         allow_slow_non_contiguous=True).then_inc(edges_in, 16)
            sp.dma_start(next_i[whole - 1:whole, FULL:FULL + 1], ap['dst'][at + (whole - 1) * BLK:at + (whole - 1) * BLK + 1].rearrange("(o e) -> o e", o=1)
                         ).then_inc(edges_in, 16)
            for (_, _, w, a, d, _, wn, an, dn) in att:
                sp.dma_start(w[:], wn).then_inc(weights_in, 16)
                sp.dma_start(a[:], an.unsqueeze(1)).then_inc(weights_in, 16)
                sp.dma_start(d[:], dn.unsqueeze(1)).then_inc(weights_in, 16)
            sp.dma_start(W3a[:], ap['L3_gnn_W1'][0:BLK, :]).then_inc(weights_in, 16)
            sp.dma_start(W3b[0:1, :], ap['L3_gnn_b1'].unsqueeze(0)).then_inc(weights_in, 16)
            sp.dma_start(W3b[1:2, :], ap['L3_gnn_W1'][BLK:BLK + 1, :]).then_inc(weights_in, 16)
            sp.dma_start(W4[:], ap['L3_gnn_W2'][0:2 * BLK, :].rearrange("(t k) f -> k t f", t=2)).then_inc(weights_in, 16)
            for k in ('L1_gnn_b1', 'L1_gnn_b2', 'L2_gnn_bias', 'L3_gnn_b2'):
                sp.dma_start(row[k][:], ap[k].partition_broadcast(BLK)).then_inc(weights_in, 16)
            sp.dma_start(row['we2'][:], ap['L3_gnn_W2'][2 * BLK, :].partition_broadcast(BLK)).then_inc(weights_in, 16)
            sp.wait_ge(weights_in, 18 * 16)
            sp.wait_ge(x_in, 32)
            sp.wait_ge(record_ready, 1)
            rec3 = record.rearrange("p (g e) c -> p g (e c)", g=G)
            last_tiles = TILES - FULL * BLK
            sp.dma_start(records[0:FULL * BLK * BLK, :].rearrange("(g p e) c -> p g (e c)", p=BLK, e=BLK), rec3[:, 0:FULL, :]).then_inc(record_out, 16)
            sp.dma_start(records[FULL * BLK * BLK:TILES * BLK, :].rearrange("(p e) c -> p (e c)", e=BLK), rec3[0:last_tiles, FULL, :]).then_inc(record_out, 16)
            sp.wait_ge(record_out, 32)
            phase_end(sp, 1)
            sp.wait_ge(bounds_ready, 1)
            for s in range(2):
                sp.dma_start(bounds_dram[s, :].rearrange("(q p) -> p q", p=BQ), hl_int[:, 4 * s:4 * s + 4], allow_slow_non_contiguous=True).then_inc(bounds_out, 16)
            sp.wait_ge(bounds_out, 32)
            sp.dma_start(bounds[:], bounds_dram.rearrange("s w -> (s w)").rearrange("(o n) -> o n", o=1)).then_inc(bounds_in, 16)
            sp.wait_ge(bounds_in, 16)
            phase_end(sp, 2)
            sp.wait_ge(starts_ready, 1)
            sp.dma_start(starts_dram.rearrange("(a j) -> j a", j=SUBS), sub_at[:], allow_slow_non_contiguous=True).then_inc(starts_out, 16)
            sp.wait_ge(starts_out, 16)
            sp.dma_start(starts[:, 0:2 * NWIN], starts_dram.rearrange("(o n) -> o n", o=1)).then_inc(starts_out, 16)
            sp.wait_ge(starts_out, 32)
            phase_end(sp, 3)

            fast = sp.value_load(starts[0:1, 2 * NWIN:2 * NWIN + 1], min_val=0, max_val=1)
            with sp.If(fast == 1):
                with sp.Fori(0, NWIN // WS) as i:
                    for s in range(WS):
                        sp.wait_ge(rel_ready, i * WS + s + 1)
                        for k in range(2):
                            first = sp.value_load(starts[0:1, bass.ds(i * 2 * WS + (2 * s + k), 1)], min_val=0, max_val=TILES * BLK - CAP)
                            sp.dma_start(rec[:, s, k, :], records[bass.ds(first, CAP), :].rearrange("(p t) c -> p (t c)", p=BLK)).then_inc(rec_in[s], 16)
            with sp.If(fast == 0):
                with sp.Fori(0, NH) as h:
                    sp.wait_ge(stage_ready, h + 2)
                    sp.dma_start(counts[bass.ds(h + 1, 1)].rearrange("o b a d -> b (o a d)"),
                                 ap1(stage[:, bass.ds(h % 2, 1), :])).then_inc(counts_out, 16)
                    with sp.Fori(0, 4) as q:
                        sp.wait_ge(linked_full, (h + 1) * 4 + q + 1)
                        sp.dma_start(linked[bass.ds(h * 4 + q + 4, 1)].rearrange("o d s -> d (o s)"),
                                     ap1(linked_sb[:, bass.ds(q % 2, 1), :])).then_inc(linked_out, 16)
                        sp.wait_ge(linked_out, (h * 4 + q + 1) * 16)
                        sp.sem_inc(linked_free, 1)
                    sp.wait_ge(counts_out, (h + 1) * 16)
                    sp.sem_inc(stage_free, 1)
            phase_end(sp, 4)
            phase_end(sp, 5)
            sp.sem_inc(cnt_free, 3)
            load_counts(sp, 0)
            phase_end(sp, 6)
            for l in range(3):
                phase_end(sp, 7 + 4 * l)
                if l == 0:
                    sp.sem_inc(link_free, 2)
                with sp.Fori(0, NQ // 2) as b:
                    for s in range(2):
                        sp.wait_ge(link_free, b * 2 + (l * NQ + s + 1))
                        sp.dma_start(link[:, s, :], linked[bass.ds(b * 2 + (s + 4), 1)].rearrange("o d s -> d (o s)")).then_inc(link_in[s], 16)
                phase_end(sp, 8 + 4 * l)
                phase_end(sp, 9 + 4 * l)
                load_counts(sp, 1 + l)
                phase_end(sp, 10 + 4 * l)
            phase_end(sp, 19)
            load_counts(sp, 4)
            phase_end(sp, 20)
            phase_end(sp, 21)
            load_counts(sp, 5)
            phase_end(sp, 22)
            phase_end(sp, 23)
            sp.dma_start(out[0:(NB - 1) * BLK, :].rearrange("(a b) f -> b a f", b=BLK), X[:, 0:NB - 1, :]).then_inc(out_stored, 16)
            sp.dma_start(out[(NB - 1) * BLK:N, :], X[0:N - (NB - 1) * BLK, NB - 1, :]).then_inc(out_stored, 16)
            sp.wait_ge(out_stored, 32)

        @block.gpsimd
        def _(pool):
            nc.gpsimd.memset(dst_i[:], NP - 1).then_inc(pads_set, 1)
            nc.gpsimd.memset(src_i[:], NP - 1).then_inc(pads_set, 1)
            nc.gpsimd.memset(raw[:, 4, :], 0.0).then_inc(pads_set, 1)
            nc.gpsimd.memset(X[:, NB - 1, :], 0.0).then_inc(pads_set, 1)
            nc.gpsimd.memset(next_i[:], NP - 1).then_inc(pads_set, 1)
            nc.gpsimd.iota(iota_f[:], [[1, BLK]], base=0, channel_multiplier=0, allow_small_or_imprecise_dtypes=True)
            nc.gpsimd.iota(part[:], [[1, 1]], base=0, channel_multiplier=1, allow_small_or_imprecise_dtypes=True)
            nc.gpsimd.iota(key_iota[:], [[1, NB], [KEY, WIN]], base=0, channel_multiplier=0, allow_small_or_imprecise_dtypes=True)
            nc.gpsimd.iota(win_first[:], [[WIN, NWIN]], base=0, channel_multiplier=0, allow_small_or_imprecise_dtypes=True)
            nc.gpsimd.iota(win_last[:], [[WIN, NWIN]], base=WIN - 1, channel_multiplier=0, allow_small_or_imprecise_dtypes=True)
            nc.gpsimd.iota(neg_key[:], [[-WIN * KEY, NWIN]], base=0, channel_multiplier=0, allow_small_or_imprecise_dtypes=True)
            nc.gpsimd.iota(iota_t[:], [[1, BLK], [0, HT]], base=0, channel_multiplier=0, allow_small_or_imprecise_dtypes=True)
            nc.gpsimd.iota(tile_up[:], [[BLK, G]], base=1, channel_multiplier=1, allow_small_or_imprecise_dtypes=True)
            nc.gpsimd.iota(tile_dn[:], [[-BLK, G]], base=TILES, channel_multiplier=-1, allow_small_or_imprecise_dtypes=True)
            nc.gpsimd.memset(zero16[:], 0.0)
            nc.gpsimd.memset(zero_b[:], 0.0)
            nc.gpsimd.memset(ones[:], 1.0)
            pool.drain().then_inc(iotas_done, 1)
            phase_end(pool, 1)
            phase_end(pool, 2)
            phase_end(pool, 3)
            nc.gpsimd.memset(stage[:, 1, :], 0.0)
            pool.drain().then_inc(stage_ready, 1)

            def self_loops(h):
                pool.wait_ge(stage_full, h + 1)
                odd = h % 2
                for k in range(3):
                    blk_at = (h // 2) * CB + odd * 4 + k
                    at = stage[:, bass.ds(odd, 1), bass.ds(blk_at * HALF + odd * (BLK // 2) + k * BLK, BLK)]
                    nc.gpsimd.tensor_tensor(ap1(at), ap1(at), ident16[:], ALU.add)
                at = stage[:, bass.ds(odd, 1), bass.ds(((h // 2) * CB + 3) * HALF + 3 * BLK - odd * 3 * BLK, BLK // 2)]
                nc.gpsimd.tensor_tensor(ap1(at), ap1(at), ap1(halves16[:, bass.ds(odd, 1), :]), ALU.add)
                pool.drain().then_inc(stage_ready, 1)

            fast = pool.value_load(starts[0:1, 2 * NWIN:2 * NWIN + 1], min_val=0, max_val=1)
            with pool.If(fast == 1):
                nc.gpsimd.iota(sub_iota[:], [[SUB * KEY, 2], [1, NB], [KEY, SUB]], base=0, channel_multiplier=0, allow_small_or_imprecise_dtypes=True)
                pool.drain()
                pool.sem_inc(rel_ready, WS)

                def keys_of(w, s, i, whole):
                    pool.wait_ge(rec_in[s], i * 128 + 32 * (whole + 1))
                    pool.wait_ge(keys_ready, w + 1)
                    both = rec[:, s, :, :].rearrange("p k (t c) -> p (k t) c", c=2)
                    nc.gpsimd.tensor_tensor(key_rel[:, s, :], both[:, :, 0], neg_key[:, bass.ds(w, 1)].broadcast_to([BLK, 2 * ST]), ALU.add)
                    nc.gpsimd.tensor_copy(src_rel[:, s, :], both[:, :, 1]).then_inc(rel_ready, 1)

                AHEAD = 4
                for k in range(AHEAD):
                    keys_of(k, k % WS, 0, k // WS)
                with pool.Fori(0, NH - 1) as h:
                    for k in range(AHEAD, 28 + AHEAD):
                        keys_of(h * 28 + k, k % WS, h, k // WS)
                    self_loops(h)
                for k in range((NH - 1) * 28 + AHEAD, NWIN):
                    keys_of(k, k % WS, 0, k // WS)
                self_loops(NH - 1)
            with pool.If(fast == 0):
                with pool.Fori(0, NH) as h:
                    self_loops(h)
            phase_end(pool, 4)
            for k in range(5, 24):
                phase_end(pool, k)

        @block.vector
        def _(dve):
            dve.wait_ge(iotas_done, 1)
            nc.vector.tensor_copy(iota_b[:], iota_f[:])
            nc.vector.tensor_scalar(ident[:], iota_f[:], part[:, 0:1], None, ALU.is_equal)
            dve.drain()
            nc.vector.tensor_copy(ident16[:], ident[:])
            nc.vector.memset(fold[:], 0.0)
            dve.drain()
            nc.vector.tensor_tensor(fold[:, 0:D], ident[:, 0:D], ident[:, D:2 * D], ALU.add)
            nc.vector.tensor_scalar(sub_rows[:, 1, :], iota_f[:, 0:SUBS], float(SUB), None, ALU.mult)
            dve.drain()
            nc.vector.tensor_scalar(sub_rows[:, 0, :], sub_rows[:, 1, :], part[:, 0:1], 0.0, ALU.subtract, ALU.is_gt)
            dve.drain()
            nc.vector.tensor_scalar(sub_rows[:, 1, :], sub_rows[:, 1, :], part[:, 0:1], float(-SUB), ALU.subtract, ALU.is_gt)
            dve.drain()
            nc.vector.tensor_tensor(sub_rows[:, 1, :], sub_rows[:, 1, :], sub_rows[:, 0, :], ALU.subtract)
            dve.wait_ge(edges_in, 12 * 16)
            nc.vector.tensor_copy(raw[:, 3, :], dst_i[:])
            nc.vector.tensor_single_scalar(tmp_i[:], src_i[:], 7, ALU.arith_shift_right)
            dve.drain()
            nc.vector.tensor_copy(raw[:, 2, :], tmp_i[:])
            dve.drain()
            nc.vector.tensor_single_scalar(tmp_i[:], src_i[:], BLK - 1, ALU.bitwise_and)
            dve.drain()
            nc.vector.tensor_copy(raw[:, 1, :], tmp_i[:])
            nc.vector.scalar_tensor_tensor(raw[:, 0, :], raw[:, 3, :], float(KEY), raw[:, 2, :], ALU.mult, ALU.add)
            dst3 = raw[:, 3, :].rearrange("p (g e) -> p g e", g=G)
            nc.vector.tensor_reduce(tile_lo[:], dst3, AX.X, ALU.min)
            nc.vector.tensor_reduce(tile_hi[:], dst3, AX.X, ALU.max)
            nc.vector.memset(hilo[:], 0.0)
            dve.drain()
            nc.vector.tensor_copy(record[:, :, 0], raw[:, 0, :])
            nc.vector.tensor_copy(record[:, :, 1], raw[:, 1, :])
            dve.drain().then_inc(record_ready, 1)
            nc.vector.tensor_copy(next_f[:], next_i[:])
            falls = falls_at.rearrange("p (g e) -> p g e", g=G)
            nc.vector.tensor_tensor(falls[:, :, 0:BLK - 1], dst3[:, :, 0:BLK - 1], dst3[:, :, 1:BLK], ALU.is_gt)
            dve.drain()
            nc.vector.tensor_tensor(falls[:, :, BLK - 1], dst3[:, :, BLK - 1], next_f[:], ALU.is_gt)
            nc.vector.memset(misfit[:], 0.0)
            dve.drain()
            nc.vector.tensor_reduce(misfit[:, 0:1], falls_at[:], AX.X, ALU.max)
            phase_end(dve, 1)
            for g in range(G):
                nc.vector.tensor_scalar(over[:, 0, :], win_last[:], tile_lo[:, g:g + 1], None, ALU.is_ge)
                dve.drain()
                nc.vector.scalar_tensor_tensor(over[:, 1, :], win_first[:], tile_hi[:, g:g + 1], over[:, 0, :], ALU.is_le, ALU.mult)
                dve.drain()
                nc.vector.scalar_tensor_tensor(hilo[:, 0, :], over[:, 1, :], tile_up[:, g:g + 1], hilo[:, 0, :], ALU.mult, ALU.max)
                nc.vector.scalar_tensor_tensor(hilo[:, 1, :], over[:, 1, :], tile_dn[:, g:g + 1], hilo[:, 1, :], ALU.mult, ALU.max)
                dve.drain()
            dve.drain().then_inc(hilo_ready, 1)
            dve.wait_ge(hilo_turned, 1)
            nc.vector.tensor_reduce(hl_max[:], banks(2, 2)[0:BQ, :].rearrange("p (k n) -> p k n", k=8), AX.X, ALU.max)
            dve.drain()
            nc.vector.tensor_scalar(hl_max[:, 4:8], hl_max[:, 4:8], -1.0, float(TILES), ALU.mult, ALU.add)
            nc.vector.tensor_scalar(hl_max[:, 0:4], hl_max[:, 0:4], float(TILES), 1.0, ALU.min, ALU.add)
            dve.drain()
            nc.vector.tensor_copy(hl_int[:], hl_max[:])
            dve.drain()
            nc.vector.tensor_single_scalar(hl_int[:], hl_int[:], 1, ALU.arith_shift_right)
            dve.drain()
            nc.vector.tensor_copy(hl_max[:], hl_int[:])
            dve.drain()
            nc.vector.tensor_scalar(hl_max[:, 0:4], hl_max[:, 0:4], 1.0, None, ALU.max)
            dve.drain()
            nc.vector.scalar_tensor_tensor(hl_max[:, 4:8], hl_max[:, 0:4], -1.0, hl_max[:, 4:8], ALU.add, ALU.min)
            dve.drain()
            nc.vector.tensor_copy(hl_int[:], hl_max[:])
            dve.drain().then_inc(bounds_ready, 1)
            dve.wait_ge(group_kept, 2 * G)
            nc.vector.tensor_copy(ea3[:, 0, :], ea_rest[:])
            nc.vector.tensor_copy(ints[:, 0, :], dst_t)
            dve.drain()
            nc.vector.tensor_tensor(ea_part[:], ea_rest[:], ea3[:, 0, :], ALU.subtract)
            nc.vector.tensor_single_scalar(ints[:, 1, :], ints[:, 0, :], 7, ALU.arith_shift_right)
            dve.drain()
            nc.vector.tensor_copy(ea3[:, 1, :], ea_part[:])
            nc.vector.tensor_copy(hist_a[:, 1, :], ints[:, 1, :])
            nc.vector.tensor_single_scalar(ints[:, 0, :], ints[:, 0, :], BLK - 1, ALU.bitwise_and)
            dve.drain()
            nc.vector.tensor_tensor(ea3[:, 2, :], ea_part[:], ea3[:, 1, :], ALU.subtract)
            nc.vector.tensor_copy(hist_b[:, 1, :], ints[:, 0, :])
            nc.vector.tensor_copy(hist_b[:, 0, :], srcb_t)
            nc.vector.tensor_copy(hist_a[:, 0, :], srca_t)
            phase_end(dve, 2)
            with dve.Fori(0, TILES // HT // 2) as i:
                for s in range(2):
                    dve.wait_ge(hist_used, i * 2 + s + 1)
                    tiles = bass.ds(i * 2 * HT + s * HT, HT)
                    rows = hot_b[:, 2 * s:2 * s + 2, :].rearrange("p k (b t) -> p k b t", t=HT)
                    cols = hot_a[:, 5 * s:5 * s + 5, :].rearrange("p k (a t) -> p k a t", t=HT)
                    nc.vector.tensor_tensor(cols[:, 0:2], iota_t[:, 0:NB, :].unsqueeze(1).broadcast_to([BLK, 2, NB, HT]),
                                            hist_a[:, :, tiles].unsqueeze(2).broadcast_to([BLK, 2, NB, HT]), ALU.is_equal)
                    nc.vector.tensor_tensor(rows, iota_t[:].unsqueeze(1).broadcast_to([BLK, 2, BLK, HT]),
                                            hist_b[:, :, tiles].unsqueeze(2).broadcast_to([BLK, 2, BLK, HT]), ALU.is_equal)
                    dve.drain()
                    nc.vector.tensor_tensor(cols[:, 2:5], cols[:, 1:2].broadcast_to([BLK, 3, NB, HT]),
                                            ea3[:, :, tiles].unsqueeze(2).broadcast_to([BLK, 3, NB, HT]), ALU.mult).then_inc(hist_ready, 1)
            dve.wait_ge(hist_done, 1)
            nc.vector.tensor_scalar(out_deg[:], psum[:, 0, 0:NB], 1.0, None, ALU.max)
            nc.vector.tensor_copy(in_deg[:, 0, :], psum[:, 1, 0:NB])
            nc.vector.tensor_reduce(ea_sum[:], psum[:, 1, NB:4 * NB].rearrange("p (k a) -> p a k", k=3), AX.X, ALU.add)
            nc.vector.memset(prefix[:, 0, 0:1], 0.0)
            dve.drain()
            nc.vector.tensor_copy(prefix[:, 0, 1:NB], in_deg[:, 0, 0:NB - 1])
            dve.drain()
            at, step = 0, 1
            while step < NB:
                nc.vector.tensor_copy(prefix[:, 1 - at, 0:step], prefix[:, at, 0:step])
                nc.vector.tensor_tensor(prefix[:, 1 - at, step:NB], prefix[:, at, step:NB], prefix[:, at, 0:NB - step], ALU.add)
                dve.drain()
                at, step = 1 - at, 2 * step
            assert at == 0
            dve.drain().then_inc(degrees_ready, 1)
            dve.wait_ge(starts_summed, 1)
            nc.vector.tensor_copy(sub_at[:], psum[0:SUBS, 2, 0:NB])
            dve.drain().then_inc(starts_ready, 1)
            nc.vector.memset(sub_max[:], 0.0)
            dve.drain()
            nc.vector.tensor_reduce(sub_max[:, 0:1], psum[0:SUBS, 3, 0:NB - 1], AX.X, ALU.max)
            real = -(-(N - (NB - 1) * BLK) // SUB)
            nc.vector.tensor_copy(sub_max[0:real, 1:2], psum[0:real, 3, NB - 1:NB])
            dve.drain()
            nc.vector.tensor_scalar(sub_max[:], sub_max[:], float(CAP), None, ALU.is_gt)
            dve.drain()
            nc.vector.tensor_tensor(misfit[0:SUBS, 1:2], sub_max[:, 0:1], sub_max[:, 1:2], ALU.add)
            dve.drain()
            nc.vector.tensor_tensor(misfit[:, 2:3], misfit[:, 0:1], misfit[:, 1:2], ALU.add)
            dve.drain().then_inc(misfit_ready, 1)
            dve.wait_ge(misfit_turned, 1)
            nc.vector.tensor_reduce(misfit_top[:], psum[0:1, 4, 0:BLK], AX.X, ALU.max)
            dve.drain()
            nc.vector.tensor_scalar(misfit_top[:], misfit_top[:], 0.0, None, ALU.is_equal)
            dve.drain()
            nc.vector.tensor_copy(starts[:, 2 * NWIN:2 * NWIN + 1], misfit_top[:])
            phase_end(dve, 3)
            fast = dve.value_load(starts[0:1, 2 * NWIN:2 * NWIN + 1], min_val=0, max_val=1)
            with dve.If(fast == 1):
                dve.sem_inc(keys_ready, WS)
                with dve.Fori(0, NWIN // WS) as i:
                    for s in range(WS):
                        dve.wait_ge(rel_ready, i * WS + (s + WS + 1))
                        dve.wait_ge(turn_done, i * WS + s + 1)
                        nc.vector.tensor_tensor(sub_src[:, s], iota_t[:, :, 0:2 * ST],
                                                src_rel[:, s, :].unsqueeze(1).broadcast_to([BLK, BLK, 2 * ST]), ALU.is_equal)
                        for k in range(2):
                            for t in range(ST):
                                last = nc.vector.tensor_scalar(sub_key[:, s, k * ST + t, :], sub_iota[:, k, :],
                                                               key_rel[:, s, k * ST + t:k * ST + t + 1], None, ALU.is_equal)
                        last.then_inc(keys_ready, 1)
            with dve.If(fast == 0):
                visits = dve.alloc_register("dve_visits")
                dve.reg_mov(visits, 0)
                with dve.Fori(0, NWIN) as w:
                    lo = dve.value_load(bounds[0:1, bass.ds(w + NWIN, 1)], min_val=0, max_val=TILES // 2 - 1)
                    hi = dve.value_load(bounds[0:1, bass.ds(w, 1)], min_val=1, max_val=TILES // 2)
                    with dve.Fori(lo, hi) as i:
                        v = dve.snap(visits)
                        dve.wait_ge(slot_free, v + 1)
                        for t in range(2):
                            nc.vector.tensor_scalar(ap1(hot_key[:, bass.ds(v % SL, 1), t * NB * WIN:(t + 1) * NB * WIN]),
                                                    key_iota.rearrange("p a d -> p (a d)"), key_t[:, bass.ds(i * 2 + t, 1)],
                                                    neg_key[:, bass.ds(w, 1)], ALU.subtract, ALU.is_equal)
                            last = nc.vector.tensor_scalar(ap1(hot_src[:, bass.ds(v % SL, 1), t * BLK:(t + 1) * BLK]), iota_b[:],
                                                    srcb_t[:, bass.ds(i * 2 + t, 1)], None, ALU.is_equal)
                        last.then_inc(keys_ready, 1)
                        dve.reg_add(visits, visits, 1)
            phase_end(dve, 4)
            def root(k):
                dve.drain().then_inc(root_in, 1)
                dve.wait_ge(root_out, k)
                nc.vector.reciprocal(stat[1][:], stat[1][:])
                dve.drain()

            def per_node(v, width=D):
                return v[:].unsqueeze(2).broadcast_to([BLK, NB, width])

            def per_feature(v, width=D):
                return v[:].unsqueeze(1).broadcast_to([BLK, NB, width])

            def layernorm_relu(k):
                nc.vector.tensor_reduce(stat[0][:], X[:], AX.X, ALU.add)
                dve.drain()
                nc.vector.tensor_scalar(stat[0][:], stat[0][:], 1.0 / D, None, ALU.mult)
                dve.drain()
                nc.vector.tensor_tensor(XC[:], X[:], per_node(stat[0]), ALU.subtract)
                dve.drain()
                nc.vector.tensor_tensor(SQ[:], XC[:], XC[:], ALU.mult)
                dve.drain()
                nc.vector.tensor_reduce(stat[2][:], SQ[:], AX.X, ALU.add)
                dve.drain()
                nc.vector.tensor_scalar(stat[2][:], stat[2][:], 1.0 / D, LN_EPS, ALU.mult, ALU.add)
                root(k)
                nc.vector.tensor_tensor(HIN[:], XC[:], per_node(stat[1]), ALU.mult)
                dve.drain()
                nc.vector.tensor_scalar(HIN[:], HIN[:], 0.0, None, ALU.max)
                dve.drain()

            def split_features():
                nc.vector.tensor_copy(H12[:, :, 0:D], HIN[:])
                nc.vector.memset(H3[:, :, D:D + 1], 1.0)
                dve.drain()
                nc.vector.tensor_tensor(XC[:], HIN[:], H12[:, :, 0:D], ALU.subtract)
                dve.drain()
                nc.vector.tensor_copy(H12[:, :, D:2 * D], XC[:])
                dve.drain()
                nc.vector.tensor_tensor(H3[:, :, 0:D], XC[:], H12[:, :, D:2 * D], ALU.subtract)

            def count_sums(n):
                with dve.Fori(0, CHUNKS) as c:
                    dve.wait_ge(agg_done, c + (n + 1))
                    nc.vector.tensor_copy(TB[0:D + 1, :].rearrange("p (t d) -> p t d", t=2), psum[0:D + 1, 2:4, 0:HALF]).then_inc(agg_kept, 1)
                    dve.wait_ge(agg_turned, c + (n + 1))

            AGG3 = AGG[:, 0:NB * (D + 1)].rearrange("p (a f) -> p a f", a=NB)

            for (_, fo, _, a, _, a_rows, _, _, _) in att:
                nc.vector.tensor_scalar(a_rows[:], ones[0:fo, :], a[:, 0:1], None, ALU.mult)
            layernorm_relu(1)
            nc.vector.tensor_copy(stat[2][:], out_deg[:])
            root(2)
            nc.vector.tensor_tensor(HIN[:], HIN[:], per_node(stat[1]), ALU.mult)
            dve.drain()
            split_features()
            phase_end(dve, 5)
            count_sums(0)
            phase_end(dve, 6)
            nc.vector.tensor_copy(deg[:], AGG3[:, :, D])
            nc.vector.tensor_tensor(XC[:], AGG3[:, :, 0:D], HIN[:], ALU.subtract)
            dve.drain()
            nc.vector.tensor_scalar(stat[2][:], deg[:], -1.0, 1.0, ALU.add, ALU.max)
            root(3)
            nc.vector.tensor_tensor(XC[:], XC[:], per_node(stat[1]), ALU.mult)
            dve.drain()
            nc.vector.tensor_tensor(X[:], X[:], XC[:], ALU.add)
            dve.drain()
            layernorm_relu(4)
            for l, (ki, fo, W, a_src, a_dst, a_rows, _, _, _) in enumerate(att):
                dve.drain().then_inc(input_ready, 1)
                with dve.Fori(0, CHUNKS) as c:
                    dve.wait_ge(feats_done, c + (l * CHUNKS + 1))
                    HF3 = HF[:, 0:NB * (fo + 1)].rearrange("p (a f) -> p a f", a=NB)
                    nc.vector.tensor_copy(HF3[:, bass.ds(c * CB, CB), 0:fo], psum[:, 2, 0:CB * fo].rearrange("p (a f) -> p a f", a=CB)).then_inc(feats_kept, 1)
                    dve.wait_ge(scores_done, c + (l * CHUNKS + 1))
                    nc.vector.tensor_copy(ROW1[:, bass.ds(c * CW, CW)].rearrange("p (t d) -> p t d", t=2), psum[:, 5:7, 0:HALF])
                    nc.vector.tensor_scalar(sj8[:, bass.ds(c * CB, CB)], psum[:, 7, 0:CB], 1.0 - SLOPE, None, ALU.mult)
                    nc.vector.tensor_scalar(sj2[:, bass.ds(c * CB, CB)], psum[:, 7, 0:CB], SLOPE, None, ALU.mult)
                    nc.vector.tensor_copy(si[:, bass.ds(c * QC, QC)], psum[0:QW, 7, 16:16 + QC]).then_inc(scores_kept, 1)
                nc.vector.memset(HF3[:, :, fo:fo + 1], 1.0)
                dve.drain()
                nc.vector.tensor_reduce(low[:], ROW1[:], AX.X, ALU.min)
                dve.drain()
                nc.vector.tensor_scalar(ROW1[:], ROW1[:], low[:, 0:1], 1.0, ALU.subtract, ALU.add)
                phase_end(dve, 7 + 4 * l)
                with dve.Fori(0, NQ // 2) as b:
                    for s in range(2):
                        dve.wait_ge(link_in[s], b * 16 + (l * NQ // 2 + 1) * 16)
                        nc.vector.memset(top_now[:, s:s + 1], 0.0)
                        dve.drain()
                        nc.vector.tensor_tensor_reduce(out=junk[:], in0=link[:, s, :], in1=ROW1[0:QW, :], scale=1.0, scalar=0.0,
                                                       op0=ALU.mult, op1=ALU.max, accum_out=top_now[:, s:s + 1])
                        dve.drain().then_inc(link_free, 1)
                        nc.vector.tensor_copy(top[:, bass.ds(b * 2 + s, 1)], top_now[:, s:s + 1])
                dve.drain()
                nc.vector.tensor_scalar(top[:], top[:], low[0:QW, 0:1], -1.0, ALU.add, ALU.add)
                dve.drain()
                nc.vector.tensor_tensor(c1[:], si[:], top[:], ALU.add)
                dve.drain()
                nc.vector.scalar_tensor_tensor(top[:], c1[:], SLOPE, c1[:], ALU.mult, ALU.max)
                dve.drain()
                nc.vector.tensor_tensor(c1[:], si[:], top[:], ALU.subtract)
                nc.vector.scalar_tensor_tensor(c2[:], si[:], SLOPE, top[:], ALU.mult, ALU.subtract)
                phase_end(dve, 8 + 4 * l)
                with dve.Fori(0, NH) as h:
                    for k, (c, T) in enumerate(((c1, TA), (c2, TB))):
                        for q in range(4):
                            nc.vector.tensor_scalar(T[0:QW, q * QW:(q + 1) * QW], ident[0:QW, 0:QW], c[:, bass.ds(h * 4 + q, 1)], None, ALU.mult)
                    dve.drain().then_inc(diag_ready, 1)
                    dve.wait_ge(diag_spread, h + (l * NH + 1))
                phase_end(dve, 9 + 4 * l)

                def exponent(r, c):
                    if r >= 4:
                        dve.wait_ge(p_ready, c * NB + (l * ROWS + r - 3))
                    nc.vector.scalar_tensor_tensor(YE[:, r % 4, :], ROW1[:, bass.ds(c * CW, CW)], sj8[:, r:r + 1],
                                                   ROW2[:, bass.ds(c * CW, CW)], ALU.add, ALU.max).then_inc(y_ready, 1)

                with dve.Fori(0, CHUNKS) as c:
                    exponent(0, c)
                    exponent(1, c)
                    for r in range(NB):
                        if r + 2 < NB:
                            exponent(r + 2, c)
                        g, j = divmod(r, GRP)
                        if j == 0:
                            dve.wait_ge(cnt_in[g], c * 32 + 32 * ((1 + l) * CHUNKS + 1))
                        dve.wait_ge(e_ready, c * NB + (l * ROWS + r + 1))
                        dve.wait_ge(p_used, c * NB + (l * ROWS + max(r - 2, 0) + 1))
                        last = nc.vector.scalar_tensor_tensor(PW[:, r % 3, :], YE[:, r % 4, :], 1.0, counts_of(g, j), ALU.min, ALU.mult)
                        last.then_inc(p_ready, 1)
                        if j == GRP - 1:
                            dve.drain().then_inc(cnt_free, 1)
                phase_end(dve, 10 + 4 * l)
                A3 = AGG[:, 0:NB * (fo + 1)].rearrange("p (a f) -> p a f", a=NB)
                XO = XC[:, :, 0:fo]
                nc.vector.tensor_scalar(stat[0][:], A3[:, :, fo], DEN_EPS, None, ALU.add)
                dve.drain()
                nc.vector.reciprocal(stat[0][:], stat[0][:])
                dve.drain()
                nc.vector.tensor_tensor(XO, A3[:, :, 0:fo], per_node(stat[0], fo), ALU.mult)
                dve.drain()
                if l == 0:
                    nc.vector.tensor_tensor(XO, XO, per_feature(row['L1_gnn_b1'], fo), ALU.add)
                    dve.drain()
                    nc.vector.tensor_scalar(HIN[:, :, 0:fo], XO, 0.0, None, ALU.max)
                    dve.drain()
                if l == 1:
                    nc.vector.tensor_tensor(XO, XO, per_feature(row['L1_gnn_b2']), ALU.add)
                    dve.drain()
                    nc.vector.tensor_tensor(X[:], X[:], XO, ALU.add)
                    dve.drain()
                    layernorm_relu(5)
                if l == 2:
                    nc.vector.tensor_tensor(XO, XO, per_feature(row['L2_gnn_bias']), ALU.add)
                    dve.drain()
                    nc.vector.tensor_tensor(SQ[:], XO, XO, ALU.mult)
                    dve.drain()
                    nc.vector.tensor_reduce(stat[2][:], SQ[:], AX.X, ALU.add)
                    dve.drain().then_inc(root_in, 1)
                    dve.wait_ge(root_out, 6)
                    nc.vector.tensor_scalar(stat[1][:], stat[1][:], NORM_EPS, None, ALU.max)
                    dve.drain()
                    nc.vector.reciprocal(stat[1][:], stat[1][:])
                    dve.drain()
                    nc.vector.tensor_tensor(XO, XO, per_node(stat[1]), ALU.mult)
                    dve.drain()
                    nc.vector.tensor_tensor(X[:], X[:], XO, ALU.add)
                    dve.drain()
                    layernorm_relu(7)
            split_features()
            phase_end(dve, 19)
            count_sums(4 * CHUNKS)
            phase_end(dve, 20)
            nc.vector.tensor_tensor(US[:, :, 0:D], HIN[:], per_node(deg), ALU.mult)
            nc.vector.tensor_copy(US[:, :, D:2 * D], AGG3[:, :, 0:D])
            nc.vector.tensor_copy(DE[:, :, 0], deg[:])
            nc.vector.tensor_copy(DE[:, :, 1], ea_sum[:])
            dve.drain().then_inc(mlp_copied, 1)
            with dve.Fori(0, CHUNKS) as c:
                dve.wait_ge(mlp_turned, c + 1)
                nc.vector.tensor_copy(DET, banks(2, 2)[0:2, 0:CW]).then_inc(mlp_kept, 1)
                dve.wait_ge(mlp_out2, c + 1)
                both = banks(0, 2)[:, 0:CW].rearrange("p (a f) -> p a f", a=CB)
                nc.vector.tensor_copy(GI[:, bass.ds(c * CB, CB), :], both[:, :, 0:D])
                nc.vector.tensor_copy(HIN[:, bass.ds(c * CB, CB), :], both[:, :, D:2 * D])
                dve.drain().then_inc(mlp_stored, 1)
            split_features()
            phase_end(dve, 21)
            count_sums(5 * CHUNKS)
            phase_end(dve, 22)
            nc.vector.tensor_tensor(GI[:], GI[:], per_feature(row['L3_gnn_b2']), ALU.add)
            nc.vector.tensor_copy(XC[:], per_feature(row['we2']))
            dve.drain()
            nc.vector.tensor_tensor(GI[:], GI[:], per_node(deg), ALU.mult)
            nc.vector.tensor_tensor(XC[:], XC[:], per_node(ea_sum), ALU.mult)
            dve.drain()
            nc.vector.tensor_tensor(GI[:], GI[:], AGG3[:, :, 0:D], ALU.add)
            dve.drain()
            nc.vector.tensor_tensor(GI[:], GI[:], XC[:], ALU.add)
            dve.drain()
            nc.vector.tensor_scalar(GI[:], GI[:], 0.0, None, ALU.max)
            dve.drain()
            nc.vector.tensor_reduce(stat[0][:], GI[:], AX.X, ALU.max)
            dve.drain()
            nc.vector.tensor_tensor(GI[:], GI[:], per_node(stat[0]), ALU.subtract)
            dve.drain().then_inc(root_in, 1)
            dve.wait_ge(root_out, 8)
            nc.vector.tensor_reduce(stat[2][:], SQ[:], AX.X, ALU.add)
            dve.drain().then_inc(root_in, 1)
            dve.wait_ge(root_out, 9)
            nc.vector.tensor_tensor(GI[:], GI[:], per_node(stat[1]), ALU.subtract)
            dve.drain()
            nc.vector.tensor_tensor(X[:], X[:], GI[:], ALU.add)
            phase_end(dve, 23)

        @block.tensor
        def _(pe):
            phase_end(pe, 1)
            with pe.Fori(0, G) as g:
                pe.wait_ge(group_copied, g + 1)
                for k in range(5):
                    last = nc.tensor.transpose(banks(0, 2)[:, k * BLK:(k + 1) * BLK], grp[:, k, :], ident[:])
                last.then_inc(group_turned, 1)
                pe.wait_ge(group_kept, 2 * (g + 1))
            pe.wait_ge(hilo_ready, 1)
            for s in range(2):
                for q in range(4):
                    k = s * 4 + q
                    last = nc.tensor.transpose(banks(2, 2)[0:BQ, k * BLK:(k + 1) * BLK], hilo[:, s, q * BQ:(q + 1) * BQ], ident[:])
            last.then_inc(hilo_turned, 1)
            phase_end(pe, 2)
            pe.sem_inc(hist_used, 2)
            for k in range(2):
                nc.tensor.matmul(psum[:, k, 0:4 * NB], zero_b[:, 0:BLK], zero_b[:, 0:4 * NB], start=True, stop=False, skip_group_check=True)
            with pe.Fori(0, TILES // HT // 2) as i:
                for s in range(2):
                    pe.wait_ge(hist_ready, i * 2 + s + 1)
                    for t in range(HT):
                        rows = hot_b[:, 2 * s:2 * s + 2, :].rearrange("p k (b t) -> p k b t", t=HT)[:, :, :, t]
                        cols = hot_a[:, 5 * s:5 * s + 5, :].rearrange("p k (a t) -> p k a t", t=HT)[:, :, :, t]
                        nc.tensor.matmul(psum[:, 0, 0:NB], rows[:, 0, :], cols[:, 0, :], start=False, stop=False, skip_group_check=True)
                        last = nc.tensor.matmul(psum[:, 1, 0:4 * NB], rows[:, 1, :], cols[:, 1:5, :], start=False, stop=False, skip_group_check=True)
                    last.then_inc(hist_used, 1)
            for k in range(2):
                last = nc.tensor.matmul(psum[:, k, 0:4 * NB], zero_b[:, 0:BLK], zero_b[:, 0:4 * NB], start=False, stop=True, skip_group_check=True)
            last.then_inc(hist_done, 1)
            pe.wait_ge(degrees_ready, 1)
            nc.tensor.matmul(psum[0:SUBS, 2, 0:NB], sub_rows[:, 0, :], in_deg[:, 0, :], start=True, stop=False)
            nc.tensor.matmul(psum[0:SUBS, 2, 0:NB], ones[:, 0:SUBS], prefix[:, 0, :], start=False, stop=True)
            nc.tensor.matmul(psum[0:SUBS, 3, 0:NB], sub_rows[:, 1, :], in_deg[:, 0, :], start=True, stop=True).then_inc(starts_summed, 1)
            pe.wait_ge(misfit_ready, 1)
            nc.tensor.matmul(psum[0:1, 4, 0:BLK], misfit[:, 2:3], ident[:], start=True, stop=True).then_inc(misfit_turned, 1)
            phase_end(pe, 3)
            fast = pe.value_load(starts[0:1, 2 * NWIN:2 * NWIN + 1], min_val=0, max_val=1)
            with pe.If(fast == 1):
                pe.sem_inc(window_free, 2)
                pe.sem_inc(turned_kept, 2)
                pe.sem_inc(turn_done, WS)

                def turn_part(slot, q, r, n):
                    pe.wait_ge(turned_kept, n + 1)
                    to = banks(4 + 2 * (r % 2), 2)[0:QW, :]
                    for j in range(GRP):
                        last = nc.tensor.matmul(to[:, j * BLK:(j + 1) * BLK],
                                                ap1(stage[:, bass.ds(slot, 1), bass.ds(q * QW + ((r % GRP) * GRP + j) * HALF, QW)]),
                                                ident16[:], start=True, stop=True)
                    last.then_inc(turn_done, 1)

                with pe.Fori(0, NH) as h:
                    with pe.Fori(0, 2) as i:
                        for k in range(2 * GRP):
                            w = h * 28 + i * 14 + k
                            s = k % WS
                            pe.wait_ge(keys_ready, w + (WS + 1))
                            pe.wait_ge(window_free, w + 1)
                            for half in range(2):
                                for t in range(ST):
                                    last = nc.tensor.matmul(psum[:, k % 2 * 2 + half, 0:NB * SUB], sub_src[:, s, :, half * ST + t],
                                                            sub_key[:, s, half * ST + t, :], start=t == 0, stop=t == ST - 1)
                            last.then_inc(window_done, 1)
                            if k == 0:
                                pe.wait_ge(stage_ready, h + 1)
                            turn_part((h + 1) % 2, i * 2 + k // GRP, k, w)
                pe.wait_ge(stage_ready, NH + 1)
                with pe.Fori(0, 2) as i:
                    for k in range(2 * GRP):
                        turn_part((NH - 1) % 2, i * 2 + k // GRP, k, i * 14 + (NWIN + k))
            with pe.If(fast == 0):
                pe.sem_inc(slot_free, SL)
                pe.wait_ge(stage_ready, 1)
                pe.sem_inc(window_free, 2)
                pe.sem_inc(turned_kept, 1)
                visits = pe.alloc_register("pe_visits")
                pe.reg_mov(visits, 0)

                def turn(slot, q, r, n):
                    pe.wait_ge(turned_kept, n + 1)
                    for j in range(GRP):
                        last = nc.tensor.matmul(banks(4, 2)[0:QW, j * BLK:(j + 1) * BLK],
                                                ap1(stage[:, bass.ds(slot, 1), bass.ds((r * GRP + j) * HALF + q * QW, QW)]),
                                                ident16[:], start=True, stop=True)
                    last.then_inc(turned, 1)

                with pe.Fori(0, NH) as h:
                    with pe.Fori(0, 4) as q:
                        with pe.Fori(0, GRP) as r:
                            w = h * 28 + q * 7 + r
                            lo = pe.value_load(bounds[0:1, bass.ds(w + NWIN, 1)], min_val=0, max_val=TILES // 2 - 1)
                            hi = pe.value_load(bounds[0:1, bass.ds(w, 1)], min_val=1, max_val=TILES // 2)
                            pe.wait_ge(window_free, w + 1)
                            buf = (q + r) % 2

                            def bank(k, n0, n1, buf=buf):
                                return ap1(psum[:, bass.ds(buf * 2 + k, 1), n0:n1])

                            for k in range(2):
                                nc.tensor.matmul(bank(k, 0, 4), zero16[:], ident16[:, 0:4], start=True, stop=False, skip_group_check=True)
                            with pe.Fori(lo, hi) as i:
                                v = pe.snap(visits)
                                pe.wait_ge(keys_ready, v + 1)
                                s = v % SL
                                for t in range(2):
                                    src = ap1(hot_src[:, bass.ds(s, 1), t * BLK:(t + 1) * BLK])
                                    at = t * NB * WIN
                                    nc.tensor.matmul(bank(0, 0, A0 * WIN), src, ap1(hot_key[:, bass.ds(s, 1), at:at + A0 * WIN]),
                                                     start=False, stop=False, skip_group_check=True)
                                    last = nc.tensor.matmul(bank(1, 0, A1 * WIN), src, ap1(hot_key[:, bass.ds(s, 1), at + A0 * WIN:at + NB * WIN]),
                                                     start=False, stop=False, skip_group_check=True)
                                last.then_inc(slot_free, 1)
                                pe.reg_add(visits, visits, 1)
                            for k in range(2):
                                last = nc.tensor.matmul(bank(k, 0, 4), zero16[:], ident16[:, 0:4], start=False, stop=True, skip_group_check=True)
                            last.then_inc(window_done, 1)
                            turn((h + 1) % 2, q, r, w)
                    pe.wait_ge(stage_ready, h + 2)
                with pe.Fori(0, 4) as q:
                    with pe.Fori(0, GRP) as r:
                        turn((NH - 1) % 2, q, r, q * 7 + r + NWIN)
            phase_end(pe, 4)
            def count_sums(L, kept):
                with pe.Fori(0, CHUNKS) as c:
                    for g in range(NGRP):
                        pe.wait_ge(cnt_in[g], c * 32 + 32 * (L * CHUNKS + 1))
                        for j in range(GRP):
                            r = g * GRP + j
                            for k, part_of in enumerate((H12[:, r, :], H3[:, r, :])):
                                for t in range(2):
                                    to = psum[:, 2 * k + t, 0:HALF] if k == 0 else psum[0:D + 1, 2 * k + t, 0:HALF]
                                    last = nc.tensor.matmul(to, part_of, counts_of(g, j)[:, t * HALF:(t + 1) * HALF],
                                                            start=(r == 0), stop=(r == NB - 1))
                        if g < NGRP - 1:
                            last.then_inc(cnt_free, 1)
                    last.then_inc(agg_done, 1)
                    pe.wait_ge(agg_kept, c * 2 + (kept + 2))
                    pe.sem_inc(cnt_free, 1)
                    for b in range(CB):
                        to = psum[:, 4, b * (D + 1):(b + 1) * (D + 1)]
                        nc.tensor.matmul(to, TA[:, b * BLK:(b + 1) * BLK], fold[:], start=True, stop=False)
                        last = nc.tensor.matmul(to, TB[0:D + 1, b * BLK:(b + 1) * BLK], ident[0:D + 1, 0:D + 1], start=False, stop=True)
                    last.then_inc(agg_turned, 1)

            phase_end(pe, 5)
            count_sums(0, 0)
            phase_end(pe, 6)
            for l, (ki, fo, W, a_src, a_dst, a_rows, _, _, _) in enumerate(att):
                with pe.Fori(0, CHUNKS) as c:
                    n = l * CHUNKS + 1
                    pe.wait_ge(input_placed, c * 2 + (2 * n - 1))
                    for b in range(CB):
                        last = nc.tensor.matmul(banks(0, 2)[0:ki, b * BLK:(b + 1) * BLK], TA[:, b * ki:(b + 1) * ki], ident[:],
                                                start=True, stop=True)
                    last.then_inc(input_turned, 1)
                    pe.wait_ge(input_placed, c * 2 + 2 * n)
                    for b in range(CB):
                        nc.tensor.matmul(psum[:, 2, b * fo:(b + 1) * fo], TB[0:ki, b * BLK:(b + 1) * BLK], W[:], start=True, stop=True)
                    for t in range(2):
                        last = nc.tensor.matmul(psum[0:fo, 3 + t, 0:HALF], W[:], TB[0:ki, t * HALF:(t + 1) * HALF], start=True, stop=True)
                    last.then_inc(feats_done, 1)
                    pe.wait_ge(feats_kept, c * 2 + 2 * n)
                    for t in range(2):
                        nc.tensor.matmul(psum[:, 5 + t, 0:HALF], a_rows[:], YE[0:fo, 0, t * HALF:(t + 1) * HALF], start=True, stop=True)
                    for b in range(CB):
                        nc.tensor.matmul(psum[:, 7, b:b + 1], YE[0:fo, 0, b * BLK:(b + 1) * BLK], a_src[:], start=True, stop=True)
                    for q in range(QC):
                        last = nc.tensor.matmul(psum[0:QW, 7, 16 + q:17 + q], YE[0:fo, 0, q * QW:(q + 1) * QW], a_dst[:], start=True, stop=True)
                    last.then_inc(scores_done, 1)
                phase_end(pe, 7 + 4 * l)
                phase_end(pe, 8 + 4 * l)
                with pe.Fori(0, NH) as h:
                    pe.wait_ge(diag_ready, h + (l * NH + 1))
                    pe.wait_ge(diag_kept, h + (l * NH + 1))
                    nc.tensor.matmul(psum[:, 0, 0:HALF], ones[0:QW, :], TA[0:QW, 0:HALF], start=True, stop=True)
                    nc.tensor.matmul(psum[:, 1, 0:HALF], ones[0:QW, :], TB[0:QW, 0:HALF], start=True, stop=True).then_inc(diag_spread, 1)
                phase_end(pe, 9 + 4 * l)
                if l == 0:
                    pe.sem_inc(p_used, 1)
                with pe.Fori(0, CHUNKS) as c:
                    for r in range(NB):
                        pe.wait_ge(p_ready, c * NB + (l * ROWS + r + 1))
                        for t in range(2):
                            last = nc.tensor.matmul(psum[0:fo + 1, t, 0:HALF], HF[:, r * (fo + 1):(r + 1) * (fo + 1)],
                                                    PW[:, r % 3, t * HALF:(t + 1) * HALF], start=(r == 0), stop=(r == NB - 1))
                        last.then_inc(p_used, 1)
                    pe.drain().then_inc(agg_done, 1)
                    pe.wait_ge(agg_kept, c + (2 * CHUNKS + l * CHUNKS + 1))
                    for b in range(CB):
                        last = nc.tensor.matmul(psum[:, 4, b * (fo + 1):(b + 1) * (fo + 1)], TA[0:fo + 1, b * BLK:(b + 1) * BLK],
                                                ident[0:fo + 1, 0:fo + 1], start=True, stop=True)
                    last.then_inc(agg_turned, 1)
                phase_end(pe, 10 + 4 * l)
            phase_end(pe, 19)
            count_sums(4, CHUNKS * 5)
            phase_end(pe, 20)
            with pe.Fori(0, CHUNKS) as c:
                pe.wait_ge(mlp_copied, c + 2)
                for b in range(CB):
                    nc.tensor.transpose(banks(0, 2)[:, b * BLK:(b + 1) * BLK], TA[:, b * BLK:(b + 1) * BLK], ident[:])
                    last = nc.tensor.transpose(banks(2, 2)[0:2, b * BLK:(b + 1) * BLK], TD[:, b * 2:b * 2 + 2], ident[:])
                last.then_inc(mlp_turned, 1)
                pe.wait_ge(mlp_kept, c * 2 + 2)
                for b in range(CB):
                    to = banks(4, 2)[:, b * BLK:(b + 1) * BLK]
                    nc.tensor.matmul(to, TB[:, b * BLK:(b + 1) * BLK], W3a[:], start=True, stop=False)
                    last = nc.tensor.matmul(to, DET[:, b * BLK:(b + 1) * BLK], W3b[:], start=False, stop=True)
                last.then_inc(mlp_out, 1)
                pe.wait_ge(mlp_relu, c + 1)
                for b in range(CB):
                    last = nc.tensor.transpose(banks(6, 2)[:, b * BLK:(b + 1) * BLK], TA[:, b * BLK:(b + 1) * BLK], ident[:])
                last.then_inc(mlp_turned2, 1)
                pe.wait_ge(mlp_kept2, c + 1)
                for b in range(CB):
                    last = nc.tensor.matmul(banks(0, 2)[:, b * BLK:(b + 1) * BLK], TB[:, b * BLK:(b + 1) * BLK],
                                            W4[:].rearrange("k t f -> k (t f)"), start=True, stop=True)
                last.then_inc(mlp_out2, 1)
            phase_end(pe, 21)
            count_sums(5, CHUNKS * 7)
            phase_end(pe, 22)
            phase_end(pe, 23)

        @block.scalar
        def _(act):
            phase_end(act, 1)
            with act.Fori(0, G) as g:
                nc.scalar.copy(grp[:], raw[:, :, bass.ds(g * BLK, BLK)]).then_inc(group_copied, 1)
                act.wait_ge(group_turned, g + 1)
                nc.scalar.copy(et[:, :, bass.ds(g * BLK, BLK)], psum[:, 0, :].rearrange("p (k n) -> p k n", k=4)).then_inc(group_kept, 1)
                nc.scalar.copy(ea_rest[:, bass.ds(g * BLK, BLK)], psum[:, 1, 0:BLK]).then_inc(group_kept, 1)
            phase_end(act, 2)
            phase_end(act, 3)
            fast = act.value_load(starts[0:1, 2 * NWIN:2 * NWIN + 1], min_val=0, max_val=1)
            with act.If(fast == 1):
                act.sem_inc(counts_stored, 16)
                for q in range(2):
                    act.sem_inc(linked_stored[q], 16)

                def keep_part(q, r, n):
                    act.wait_ge(turn_done, n + (WS + 1))
                    nc.scalar.activation(linked_sb[:, q, r * CW:(r + 1) * CW], banks(4 + 2 * ((q + r) % 2), 2)[0:QW, 0:CW],
                                         ACT.Sign).then_inc(turned_kept, 1)

                def store_linked(q, at):
                    act.drain()
                    act.dma_start(linked[bass.ds(at, 1)].rearrange("o d s -> d (o s)"), linked_sb[:, q, :]).then_inc(linked_stored[q], 16)

                with act.Fori(0, NH) as h:
                    act.wait_ge(counts_stored, (h + 1) * 16)
                    act.wait_ge(stage_ready, h + 1)
                    act.dma_start(counts[bass.ds(h, 1)].rearrange("o b a d -> b (o a d)"),
                                  ap1(stage[:, bass.ds((h + 1) % 2, 1), :])).then_inc(counts_stored, 16)
                    to = ap1(stage[:, bass.ds(h % 2, 1), :]).rearrange("p (a d) -> p a d", a=NB)
                    with act.Fori(0, 2) as i:
                        for q in range(2):
                            act.wait_ge(linked_stored[q], (h * 2 + i + 1) * 16)
                            for r in range(GRP):
                                k = q * GRP + r
                                w = h * 28 + i * 14 + k
                                act.wait_ge(window_done, w + 1)
                                at = to[:, :, bass.ds(i * 14 * WIN + k * WIN, WIN)].rearrange("p a (k d) -> p k a d", k=2)
                                nc.scalar.copy(at, psum[:, k % 2 * 2:k % 2 * 2 + 2, 0:NB * SUB].rearrange("p k (a d) -> p k a d", a=NB)
                                               ).then_inc(window_free, 1)
                                keep_part(q, r, w)
                            store_linked(q, h * 4 + i * 2 + q)
                    act.drain().then_inc(stage_full, 1)
                act.wait_ge(stage_ready, NH + 1)
                act.dma_start(counts[NH].rearrange("b a d -> b (a d)"), stage[:, (NH - 1) % 2, :]).then_inc(counts_stored, 16)
                with act.Fori(0, 2) as i:
                    for q in range(2):
                        act.wait_ge(linked_stored[q], (i + (2 * NH + 1)) * 16)
                        for r in range(GRP):
                            keep_part(q, r, i * 14 + (NWIN + q * GRP + r))
                        store_linked(q, i * 2 + (NH * 4 + q))
                act.wait_ge(counts_stored, (NH + 2) * 16)
                for q in range(2):
                    act.wait_ge(linked_stored[q], (2 * NH + 3) * 16)
            with act.If(fast == 0):
                act.sem_inc(stage_free, 2)
                act.sem_inc(linked_free, 6)
                with act.Fori(0, NH) as h:
                    act.wait_ge(stage_free, h + 1)
                    with act.Fori(0, 4) as q:
                        act.wait_ge(linked_free, h * 4 + q + 1)
                        with act.Fori(0, GRP) as r:
                            w = h * 28 + q * 7 + r
                            act.wait_ge(window_done, w + 1)
                            buf = (q + r) % 2
                            to = ap1(stage[:, bass.ds(h % 2, 1), :]).rearrange("p (a d) -> p a d", a=NB)
                            to = to[:, :, bass.ds((q * 7 + r) * WIN, WIN)]
                            nc.scalar.copy(to[:, 0:A0, :], ap1(psum[:, bass.ds(buf * 2, 1), 0:A0 * WIN]).rearrange("p (a d) -> p a d", a=A0))
                            nc.scalar.copy(to[:, A0:NB, :], ap1(psum[:, bass.ds(buf * 2 + 1, 1), 0:A1 * WIN]).rearrange("p (a d) -> p a d", a=A1)
                                           ).then_inc(window_free, 1)
                            act.wait_ge(turned, w + 1)
                            nc.scalar.activation(ap1(linked_sb[:, bass.ds(q % 2, 1), bass.ds(r * CW, CW)]), banks(4, 2)[0:QW, 0:CW],
                                                 ACT.Sign).then_inc(turned_kept, 1)
                        act.drain().then_inc(linked_full, 1)
                    act.drain().then_inc(stage_full, 1)
                with act.Fori(0, 4) as q:
                    act.wait_ge(linked_free, NH * 4 + q + 1)
                    with act.Fori(0, GRP) as r:
                        act.wait_ge(turned, NWIN + q * 7 + r + 1)
                        nc.scalar.activation(ap1(linked_sb[:, bass.ds(q % 2, 1), bass.ds(r * CW, CW)]), banks(4, 2)[0:QW, 0:CW],
                                             ACT.Sign).then_inc(turned_kept, 1)
                    act.drain().then_inc(linked_full, 1)
            phase_end(act, 4)
            def root(k):
                act.wait_ge(root_in, k)
                nc.scalar.activation(stat[1][:], stat[2][:], ACT.Sqrt).then_inc(root_out, 1)

            def count_sums(n):
                with act.Fori(0, CHUNKS) as c:
                    act.wait_ge(agg_done, c + (n + 1))
                    nc.scalar.copy(TA[:].rearrange("p (t d) -> p t d", t=2), psum[:, 0:2, 0:HALF]).then_inc(agg_kept, 1)
                    act.wait_ge(agg_turned, c + (n + 1))
                    nc.scalar.copy(AGG[:, bass.ds(c * CB * (D + 1), CB * (D + 1))], psum[:, 4, 0:CB * (D + 1)])

            root(1)
            root(2)
            phase_end(act, 5)
            count_sums(0)
            phase_end(act, 6)
            root(3)
            root(4)
            for l, (ki, fo, W, a_src, a_dst, a_rows, _, _, _) in enumerate(att):
                act.wait_ge(input_ready, l + 1)
                with act.Fori(0, CHUNKS) as c:
                    n = l * CHUNKS + 1
                    nc.scalar.copy(TA[:, 0:CB * ki].rearrange("p (a f) -> p a f", a=CB), HIN[:, bass.ds(c * CB, CB), 0:ki]).then_inc(input_placed, 1)
                    act.wait_ge(input_turned, c + n)
                    nc.scalar.copy(TB[0:ki, :], banks(0, 2)[0:ki, 0:CW]).then_inc(input_placed, 1)
                    act.wait_ge(feats_done, c + n)
                    nc.scalar.copy(YE[0:fo, 0, :].rearrange("p (t d) -> p t d", t=2), psum[0:fo, 3:5, 0:HALF]).then_inc(feats_kept, 1)
                    act.wait_ge(scores_kept, c + n)
                phase_end(act, 7 + 4 * l)
                phase_end(act, 8 + 4 * l)
                if l == 0:
                    act.sem_inc(diag_kept, 1)
                with act.Fori(0, NH) as h:
                    act.wait_ge(diag_spread, h + (l * NH + 1))
                    nc.scalar.copy(ROW1[:, bass.ds(h * HALF, HALF)], psum[:, 0, 0:HALF])
                    nc.scalar.copy(ROW2[:, bass.ds(h * HALF, HALF)], psum[:, 1, 0:HALF]).then_inc(diag_kept, 1)
                phase_end(act, 9 + 4 * l)
                with act.Fori(0, CHUNKS) as c:
                    for r in range(NB):
                        act.wait_ge(y_ready, c * NB + (l * ROWS + r + 1))
                        nc.scalar.activation(YE[:, r % 4, :], YE[:, r % 4, :], ACT.Exp, bias=sj2[:, r:r + 1]).then_inc(e_ready, 1)
                    act.wait_ge(agg_done, c + (CHUNKS + l * CHUNKS + 1))
                    nc.scalar.copy(TA[0:fo + 1, :].rearrange("p (t d) -> p t d", t=2), psum[0:fo + 1, 0:2, 0:HALF]).then_inc(agg_kept, 1)
                    act.wait_ge(agg_turned, c + (CHUNKS + l * CHUNKS + 1))
                    nc.scalar.copy(AGG[:, bass.ds(c * CB * (fo + 1), CB * (fo + 1))], psum[:, 4, 0:CB * (fo + 1)])
                phase_end(act, 10 + 4 * l)
                if l == 1:
                    root(5)
                if l == 2:
                    root(6)
                    root(7)
            phase_end(act, 19)
            count_sums(CHUNKS * 4)
            phase_end(act, 20)
            act.wait_ge(mlp_copied, 1)
            with act.Fori(0, CHUNKS) as c:
                nc.scalar.copy(TD[:, 0:2 * CB].rearrange("p (a f) -> p a f", a=CB), DE[:, bass.ds(c * CB, CB), :])
                nc.scalar.copy(TA[:].rearrange("p (a f) -> p a f", a=CB), US[:, bass.ds(c * CB, CB), :]).then_inc(mlp_copied, 1)
                act.wait_ge(mlp_turned, c + 1)
                nc.scalar.copy(TB[:], banks(0, 2)[:, 0:CW]).then_inc(mlp_kept, 1)
                act.wait_ge(mlp_out, c + 1)
                nc.scalar.activation(TA[:], banks(4, 2)[:, 0:CW], ACT.Relu).then_inc(mlp_relu, 1)
                act.wait_ge(mlp_turned2, c + 1)
                nc.scalar.copy(TB[:], banks(6, 2)[:, 0:CW]).then_inc(mlp_kept2, 1)
                act.wait_ge(mlp_stored, c + 1)
            phase_end(act, 21)
            count_sums(CHUNKS * 5)
            phase_end(act, 22)
            act.wait_ge(root_in, 8)
            nc.scalar.activation(SQ[:], GI[:], ACT.Exp).then_inc(root_out, 1)
            act.wait_ge(root_in, 9)
            nc.scalar.activation(stat[1][:], stat[2][:], ACT.Ln).then_inc(root_out, 1)
            phase_end(act, 23)


_INS = ['x', 'src', 'dst', 'edge_weight1', 'L1_gnn_W1', 'L1_gnn_a_src1', 'L1_gnn_a_dst1', 'L1_gnn_b1', 'L1_gnn_W2',
        'L1_gnn_a_src2', 'L1_gnn_a_dst2', 'L1_gnn_b2', 'L2_gnn_weight', 'L2_gnn_att', 'L2_gnn_bias', 'L3_gnn_W1',
        'L3_gnn_b1', 'L3_gnn_W2', 'L3_gnn_b2']


def kernel(**inputs):
    import numpy as _np
    import concourse.bacc as _bacc
    from concourse import mybir as _mybir
    from concourse.bass_utils import run_bass_kernel_spmd as _run

    nc = _bacc.Bacc("TRN2", target_bir_lowering=False, num_devices=1)
    arrays, aps = {}, {}
    for name in _INS:
        a = _np.ascontiguousarray(inputs[name])
        arrays["in_" + name] = a
        aps[name] = nc.dram_tensor("in_" + name, a.shape, _mybir.dt.from_np(a.dtype), kind="ExternalInput").ap()
    out = nc.dram_tensor("out_0", (N, D), _mybir.dt.from_np(_np.dtype("float32")), kind="ExternalOutput").ap()
    gnn_kernel(nc, aps, out)
    r = _run(nc, [arrays], core_ids=[0])
    return r.results[0]["out_0"]
```

```python
import concourse.bass as bass
from concourse import mybir
from contextlib import ExitStack

N = 6250
E = 200000
D = 64
BLK = 128
NB = -(-N // BLK)
NP = NB * BLK
CHUNKS = 7
CB = NB // CHUNKS
CW = CB * BLK
HALF = CW // 2
NH = 2 * CHUNKS
GRP = 7
NGRP = NB // GRP
TQ = -(-HALF // BLK)
LAP = TQ * BLK - HALF
WIN = 16
NWIN = NP // WIN
HT = 16
TILES = -(-E // (BLK * HT)) * HT
G = -(-TILES // BLK)
FULL = (E // BLK) // BLK
KEY = 64
A0 = 25
A1 = NB - A0
BQ = NWIN // 4
SUB = 8
SUBS = BLK // SUB
ST = 3
CAP = ST * BLK
PACK = 512
WS = 7
SS = 4
WH = HALF // WIN
UNIT = 0.25
LN_EPS = 1e-5
DEN_EPS = 1e-16
NORM_EPS = 1e-12
SLOPE = 0.2

fp32 = mybir.dt.float32
fp16 = mybir.dt.float16
bf16 = mybir.dt.bfloat16
i32 = mybir.dt.int32
ALU = mybir.AluOpType
LINK = mybir.dt.uint8
ACT = mybir.ActivationFunctionType
AX = mybir.AxisListType


def gnn_kernel(nc, ap, out):
    ctx = ExitStack()
    with ctx:
        def sb(name, shape, dt):
            return ctx.enter_context(nc.sbuf_tensor("sb_" + name, shape, dt))

        def sem(name):
            return ctx.enter_context(nc.semaphore(name))

        counts = nc.dram_tensor("counts", (NH + 1, BLK, NB, HALF), fp16, kind="Internal").ap()
        linked = nc.dram_tensor("linked", (NP + HALF, NP), LINK, kind="Internal").ap()
        bounds_dram = nc.dram_tensor("bounds_dram", (2, NWIN), i32, kind="Internal").ap()
        records = nc.dram_tensor("records", (TILES * BLK + PACK, 2), fp32, kind="Internal").ap()
        starts_dram = nc.dram_tensor("starts_dram", (2 * NWIN,), i32, kind="Internal").ap()

        X = sb("X", [BLK, NB, D], fp32)
        ident = sb("ident", [BLK, BLK], fp32)
        ident16 = sb("ident16", [BLK, BLK], fp16)
        unit16 = sb("unit16", [BLK, BLK], fp16)
        unscale = sb("unscale", [D + 1, D + 1], fp32)
        zero16 = sb("zero16", [BLK, BLK], fp16)
        iota_f = sb("iota_f", [BLK, BLK], fp32)
        iota_b = sb("iota_b", [BLK, BLK], fp16)
        zero_b = sb("zero_b", [BLK, 4 * NB], bf16)
        ones = sb("ones", [BLK, BLK], fp32)
        fold = sb("fold", [BLK, D + 1], fp32)
        part = sb("part", [BLK, 1], fp32)
        out_deg = sb("out_deg", [BLK, NB], fp32)
        ea_sum = sb("ea_sum", [BLK, NB], fp32)
        deg = sb("deg", [BLK, NB], fp32)
        sub_rows = sb("sub_rows", [BLK, 2, SUBS], fp32)
        misfit = sb("misfit", [BLK, 4], fp32)
        ARENA = 184 * 1024
        arena = sb("arena", [BLK, ARENA // 4], fp32)

        def view(offset, shape, dt):
            size = 1 if dt == LINK else 2 if dt in (fp16, bf16) else 4
            for s in shape[1:]:
                size *= s
            words = -(-size // 4)
            assert offset % 4 == 0 and offset + 4 * words <= ARENA, (offset, shape)
            v = arena[0:shape[0], offset // 4:offset // 4 + words]
            if dt != fp32:
                v = v.bitcast(dt)
            if len(shape) == 3:
                v = v[:, 0:shape[1] * shape[2]].rearrange("p (a b) -> p a b", a=shape[1])
            if len(shape) == 4:
                v = v[:, 0:shape[1] * shape[2] * shape[3]].rearrange("p (a b c) -> p a b c", a=shape[1], b=shape[2])
            return v, offset + 4 * words

        psum = ctx.enter_context(nc.psum_tensor("psum", [BLK, 8, 512], fp32))

        def banks(first, count):
            return psum[:, first:first + count, :].rearrange("p k n -> p (k n)")

        SL = 4
        stage, o = view(0, [BLK, 2, NB * HALF], fp16)
        linked_sb, o = view(o, [BLK, 2, NP], LINK)
        starts, o = view(o, [1, 2 * NWIN + 8], i32)
        iota_t, o = view(o, [BLK, BLK, HT], bf16)
        neg_key, o = view(o, [BLK, NWIN], fp32)
        build_at = o
        et, o = view(o, [BLK, 4, G * BLK], fp32)
        key_t, srcb_t, srca_t, dst_t = (et[:, k, :] for k in range(4))
        key_iota, o = view(o, [BLK, NB, WIN], fp16)
        hot_key, o = view(o, [BLK, SL, 2 * NB * WIN], fp16)
        hot_src, o = view(o, [BLK, SL, 2 * BLK], fp16)
        bounds, o = view(o, [1, 2 * NWIN], i32)
        sub_iota, o = view(build_at, [BLK, 2, NB * SUB], fp16)
        rec, o = view(o, [BLK, WS, 2, ST * 2], fp32)
        key_rel, o = view(o, [BLK, WS, 2 * ST], fp32)
        src_rel, o = view(o, [BLK, WS, 2 * ST], bf16)
        sub_key, o = view(o, [BLK, SS, 2 * ST, NB * SUB], fp16)
        sub_src, o = view(o, [BLK, SS * BLK, 2 * ST], bf16)
        sub_src = sub_src.rearrange("p (w b) t -> p w b t", w=SS)
        L12, o = view(o, [BLK, NB, 2 * D], bf16)
        L3p, o = view(o, [BLK, NB, D + 1], bf16)
        LA, o = view(o, [BLK, CW], fp32)
        LB, o = view(o, [BLK, CW], fp32)
        LAGG, o = view(o, [BLK, (CHUNKS + 1) * CB * (D + 1)], fp32)
        L_in, o = view(0, [BLK, NB, D], fp32)
        L_xc, o = view(o, [BLK, NB, D], fp32)
        L_sq, o = view(o, [BLK, NB, D], fp32)
        assert o <= NB * HALF * 2
        dst_i, o = view(0, [BLK, G * BLK], i32)
        src_i, o = view(o, [BLK, G * BLK], i32)
        tmp_i, o = view(o, [BLK, G * BLK], i32)
        falls_at, _ = view(4 * G * BLK, [BLK, G * BLK], fp32)
        next_i, o = view(o, [BLK, G], i32)
        raw, o = view(o, [BLK, 5, G * BLK], fp32)
        record, o = view(o, [BLK, G * BLK, 2], fp32)
        grp, o = view(o, [BLK, 5, BLK], fp32)
        win_first, o = view(o, [BLK, NWIN], fp32)
        win_last, o = view(o, [BLK, NWIN], fp32)
        over, o = view(o, [BLK, 2, NWIN], fp32)
        hilo, o = view(o, [BLK, 2, NWIN], fp32)
        tile_lo, o = view(o, [BLK, G], fp32)
        tile_hi, o = view(o, [BLK, G], fp32)
        tile_up, o = view(o, [BLK, G], fp32)
        tile_dn, o = view(o, [BLK, G], fp32)
        next_f, o = view(o, [BLK, G], fp32)
        hl_max, o = view(o, [BQ, 8], fp32)
        hl_int, o = view(o, [BQ, 8], i32)
        assert o <= 2 * NB * HALF * 2
        ea_rest, o = view(0, [BLK, G * BLK], fp32)
        ea_part, o = view(o, [BLK, G * BLK], fp32)
        ea3, o = view(o, [BLK, 3, G * BLK], bf16)
        hist_b, o = view(o, [BLK, 2, G * BLK], bf16)
        hist_a, o = view(o, [BLK, 2, G * BLK], bf16)
        ints, _ = view(o, [BLK, 2, G * BLK], i32)
        hot_b, o = view(o, [BLK, 4, BLK * HT], bf16)
        hot_a, o = view(o, [BLK, 10, NB * HT], bf16)
        in_deg, o = view(o, [BLK, 1, NB], fp32)
        prefix, o = view(o, [BLK, 2, NB], fp32)
        sub_at, o = view(o, [SUBS, NB], i32)
        sub_num, o = view(o, [SUBS, NB], i32)
        sub_max, o = view(o, [SUBS, 2], fp32)
        misfit_top, o = view(o, [1, 1], fp32)
        assert o <= 2 * NB * HALF * 2

        phase_done = sem("phase_done")
        iotas_done = sem("iotas_done")
        pads_set = sem("pads_set")
        edges_in = sem("edges_in")
        x_in = sem("x_in")
        group_copied = sem("group_copied")
        group_turned = sem("group_turned")
        group_kept = sem("group_kept")
        hilo_turned = sem("hilo_turned")
        bounds_ready = sem("bounds_ready")
        bounds_out = sem("bounds_out")
        bounds_in = sem("bounds_in")
        hist_ready = sem("hist_ready")
        hist_used = sem("hist_used")
        hist_done = sem("hist_done")
        keys_ready = sem("keys_ready")
        slot_free = sem("slot_free")
        window_done = sem("window_done")
        window_free = sem("window_free")
        stage_full = sem("stage_full")
        stage_ready = sem("stage_ready")
        stage_free = sem("stage_free")
        counts_out = sem("counts_out")
        turned = sem("turned")
        turned_kept = sem("turned_kept")
        linked_full = sem("linked_full")
        linked_out = sem("linked_out")
        linked_free = sem("linked_free")
        hilo_ready = sem("hilo_ready")
        record_ready = sem("record_ready")
        record_out = sem("record_out")
        degrees_ready = sem("degrees_ready")
        starts_summed = sem("starts_summed")
        starts_ready = sem("starts_ready")
        starts_out = sem("starts_out")
        misfit_ready = sem("misfit_ready")
        misfit_turned = sem("misfit_turned")
        flag_ready = sem("flag_ready")
        rec_in = [sem("rec_in%d" % s) for s in range(WS)]
        rel_ready = sem("rel_ready")
        turn_done = sem("turn_done")
        l0_ready = sem("l0_ready")
        half_summed = sem("half_summed")
        half_out = sem("half_out")
        chunk_turned = sem("chunk_turned")
        chunk_out = sem("chunk_out")
        counts_stored = sem("counts_stored")
        linked_stored = [sem("linked_stored%d" % s) for s in range(2)]

        def phase_end(eng, k):
            eng.drain().then_inc(phase_done, 1)
            eng.wait_ge(phase_done, 5 * k)

        def phase_reached(eng):
            eng.drain().then_inc(phase_done, 1)

        block = ctx.enter_context(nc.Block())

        halves16 = unit16[:].rearrange("p (t n) -> p t n", t=2)

        def part_at(i, q):
            return i * (2 * BLK - LAP) + BLK if q else i * (2 * BLK)

        def ap1(v):
            return v.rearrange("p o n -> p (o n)")

        CS = 4
        LS = 7
        HIN, o = view(0, [BLK, NB, D], fp32)
        AGG, o = view(o, [BLK, NB * (D + 1)], fp32)
        at = o
        H12, o = view(o, [BLK, NB, 2 * D], bf16)
        H3, o = view(o, [BLK, NB, D + 1], bf16)
        HF, _ = view(at, [BLK, NB * (D + 1)], fp32)
        cnt, at = view(o, [BLK, CS, GRP * CW], fp16)
        link, o = view(o, [BLK, LS, NP], LINK)
        o = at
        ROW1, o = view(o, [BLK, NP], fp32)
        at = o
        ROW2, o = view(o, [BLK, NP], fp32)
        junk, _ = view(at, [BLK, NP], fp16)
        US, _ = view(at, [BLK, NB, 2 * D], fp32)
        DE, _ = view(at - 4 * NP, [BLK, NB, 2], fp32)
        XC, at = view(at - 4 * NP, [BLK, NB, D], fp32)
        SQ, at = view(at, [BLK, NB, D], fp32)
        GI, _ = view(o + 2 * CW * 4, [BLK, NB, D], fp32)
        YE, o = view(o, [BLK, 5, CW], fp32)
        PW, o = view(o, [BLK, 4, CW], fp32)
        TA, o = view(o, [BLK, CW], fp32)
        TB, o = view(o, [BLK, CW], fp32)
        TD = YE[:, 0, :]
        DET = YE[0:2, 1, :]
        MA, MB = ROW1[:, CW:2 * CW], ROW1[:, 2 * CW:3 * CW]
        stat = [sb("stat%d" % k, [BLK, NB], fp32) for k in range(3)]
        sj8 = sb("sj8", [BLK, NB], fp32)
        sj2 = sb("sj2", [BLK, NB], fp32)
        si = sb("si", [BLK, NB], fp32)
        top = sb("top", [BLK, NB], fp32)
        top_now = sb("top_now", [BLK, LS], fp32)
        c1 = sb("c1", [BLK, NB], fp32)
        c2 = sb("c2", [BLK, NB], fp32)
        low = sb("low", [BLK, 1], fp32)
        W3a = sb("W3a", [BLK, BLK], fp32)
        W3b = sb("W3b", [2, BLK], fp32)
        W4 = sb("W4", [BLK, 2, D], fp32)
        row = {k: sb("row_" + k, [BLK, n], fp32) for k, n in
               (('L1_gnn_b1', 32), ('L1_gnn_b2', D), ('L2_gnn_bias', D), ('L3_gnn_b2', D), ('we2', D))}
        att = []
        for l, (ki, fo, wn, an, dn) in enumerate((
                (D, 32, ap['L1_gnn_W1'], ap['L1_gnn_a_src1'], ap['L1_gnn_a_dst1']),
                (32, D, ap['L1_gnn_W2'], ap['L1_gnn_a_src2'], ap['L1_gnn_a_dst2']),
                (D, D, ap['L2_gnn_weight'], ap['L2_gnn_att'][D:2 * D], ap['L2_gnn_att'][0:D]))):
            att.append((ki, fo, sb("W_att%d" % l, [ki, fo], fp32), sb("a_both%d" % l, [fo, 2], fp32),
                        sb("a_rows%d" % l, [fo, BLK], fp32), wn, an, dn))

        weights_in = sem("weights_in")
        input_ready = sem("input_ready")
        input_placed = sem("input_placed")
        input_turned = sem("input_turned")
        feats_done = sem("feats_done")
        feats_kept = sem("feats_kept")
        scores_done = sem("scores_done")
        scores_kept = sem("scores_kept")
        link_in = [sem("link_in%d" % s) for s in range(LS)]
        link_free = sem("link_free")
        diag_ready = sem("diag_ready")
        diag_spread = sem("diag_spread")
        diag_kept = sem("diag_kept")
        cnt_in = [sem("cnt_in%d" % g) for g in range(NGRP)]
        cnt_free = sem("cnt_free")
        y_ready = sem("y_ready")
        e_ready = sem("e_ready")
        p_ready = sem("p_ready")
        p_used = sem("p_used")
        agg_done = sem("agg_done")
        agg_kept = sem("agg_kept")
        agg_turned = sem("agg_turned")
        agg_stored = sem("agg_stored")
        root_in = sem("root_in")
        root_out = sem("root_out")
        mlp_copied = sem("mlp_copied")
        mlp_turned = sem("mlp_turned")
        mlp_kept = sem("mlp_kept")
        mlp_out = sem("mlp_out")
        mlp_relu = sem("mlp_relu")
        mlp_turned2 = sem("mlp_turned2")
        mlp_kept2 = sem("mlp_kept2")
        mlp_out2 = sem("mlp_out2")
        mlp_stored = sem("mlp_stored")
        out_stored = sem("out_stored")

        TURN = 4
        ROWS = CHUNKS * NB

        def load_counts(sp, L):
            with sp.Fori(0, CHUNKS) as c:
                for g in range(NGRP):
                    before = g - CS if g >= CS else g - NGRP + (CS if g + CS < NGRP else 0)
                    sp.wait_ge(cnt_free, c * NGRP + (L * ROWS // GRP + CS + 1 + before))
                    to = cnt[:, g % CS, :].rearrange("p (a t d) -> p a t d", a=GRP, t=2)
                    for t in range(2):
                        sp.dma_start(to[:, :, t, :], counts[bass.ds(c * 2 + (t + 1), 1), :, g * GRP:(g + 1) * GRP, :].rearrange("o b a d -> b (o a) d")
                                     ).then_inc(cnt_in[g], 16)

        def slot(r, slots):
            return slots if r == NB - 1 else r % slots

        def counts_of(g, j):
            return cnt[:, g % CS, j * CW:(j + 1) * CW]

        @block.sync
        def _(sp):
            sp.wait_ge(pads_set, 5)
            sp.dma_start(X[:, 0:NB - 1, :], ap['x'][0:(NB - 1) * BLK, :].rearrange("(a b) f -> b a f", b=BLK)).then_inc(x_in, 16)
            sp.dma_start(X[0:N - (NB - 1) * BLK, NB - 1, :], ap['x'][(NB - 1) * BLK:N, :]).then_inc(x_in, 16)
            whole = E // BLK - FULL * BLK
            for flat, to in ((ap['dst'], dst_i), (ap['src'], src_i), (ap['edge_weight1'].rearrange("e o -> (e o)"), raw[:, 4, :])):
                to3 = to.rearrange("p (g e) -> p g e", g=G)
                at = FULL * BLK * BLK
                sp.dma_start(to3[:, 0:FULL, :], flat[0:at].rearrange("(g p e) -> p g e", p=BLK, e=BLK)).then_inc(edges_in, 16)
                sp.dma_start(to3[0:whole, FULL, :], flat[at:at + whole * BLK].rearrange("(p e) -> p e", e=BLK)).then_inc(edges_in, 16)
                sp.dma_start(to3[whole:whole + 1, FULL, 0:E % BLK],
                             flat[at + whole * BLK:E].rearrange("(o e) -> o e", o=1)).then_inc(edges_in, 16)
            sp.dma_start(next_i[:, 0:FULL], ap['dst'][BLK:BLK + FULL * BLK * BLK].rearrange("(g p e) -> p g e", p=BLK, e=BLK)[:, :, 0],
                         allow_slow_non_contiguous=True).then_inc(edges_in, 16)
            at = FULL * BLK * BLK + BLK
            sp.dma_start(next_i[0:whole - 1, FULL:FULL + 1], ap['dst'][at:at + (whole - 1) * BLK].rearrange("(p e) -> p e", e=BLK)[:, 0:1],
                         allow_slow_non_contiguous=True).then_inc(edges_in, 16)
            sp.dma_start(next_i[whole - 1:whole, FULL:FULL + 1], ap['dst'][at + (whole - 1) * BLK:at + (whole - 1) * BLK + 1].rearrange("(o e) -> o e", o=1)
                         ).then_inc(edges_in, 16)
            for (_, _, w, a_both, _, wn, an, dn) in att:
                sp.dma_start(w[:], wn).then_inc(weights_in, 16)
                sp.dma_start(a_both[:, 0:1], an.unsqueeze(1)).then_inc(weights_in, 16)
                sp.dma_start(a_both[:, 1:2], dn.unsqueeze(1)).then_inc(weights_in, 16)
            sp.dma_start(W3a[:], ap['L3_gnn_W1'][0:BLK, :]).then_inc(weights_in, 16)
            sp.dma_start(W3b[0:1, :], ap['L3_gnn_b1'].unsqueeze(0)).then_inc(weights_in, 16)
            sp.dma_start(W3b[1:2, :], ap['L3_gnn_W1'][BLK:BLK + 1, :]).then_inc(weights_in, 16)
            sp.dma_start(W4[:], ap['L3_gnn_W2'][0:2 * BLK, :].rearrange("(t k) f -> k t f", t=2)).then_inc(weights_in, 16)
            for k in ('L1_gnn_b1', 'L1_gnn_b2', 'L2_gnn_bias', 'L3_gnn_b2'):
                sp.dma_start(row[k][:], ap[k].partition_broadcast(BLK)).then_inc(weights_in, 16)
            sp.dma_start(row['we2'][:], ap['L3_gnn_W2'][2 * BLK, :].partition_broadcast(BLK)).then_inc(weights_in, 16)
            sp.wait_ge(weights_in, 18 * 16)
            sp.wait_ge(x_in, 32)
            sp.wait_ge(record_ready, 1)
            rec3 = record.rearrange("p (g e) c -> p g (e c)", g=G)
            last_tiles = TILES - FULL * BLK
            sp.dma_start(records[0:FULL * BLK * BLK, :].rearrange("(g p e) c -> p g (e c)", p=BLK, e=BLK), rec3[:, 0:FULL, :]).then_inc(record_out, 16)
            sp.dma_start(records[FULL * BLK * BLK:TILES * BLK, :].rearrange("(p e) c -> p (e c)", e=BLK), rec3[0:last_tiles, FULL, :]).then_inc(record_out, 16)
            sp.wait_ge(record_out, 32)
            phase_end(sp, 1)
            sp.wait_ge(bounds_ready, 1)
            for s in range(2):
                sp.dma_start(bounds_dram[s, :].rearrange("(q p) -> p q", p=BQ), hl_int[:, 4 * s:4 * s + 4], allow_slow_non_contiguous=True).then_inc(bounds_out, 16)
            sp.wait_ge(bounds_out, 32)
            sp.dma_start(bounds[:], bounds_dram.rearrange("s w -> (s w)").rearrange("(o n) -> o n", o=1)).then_inc(bounds_in, 16)
            sp.wait_ge(bounds_in, 16)
            phase_end(sp, 2)
            sp.wait_ge(starts_ready, 1)
            sp.dma_start(starts_dram.rearrange("(a j) -> j a", j=SUBS), sub_at[:], allow_slow_non_contiguous=True).then_inc(starts_out, 16)
            sp.wait_ge(starts_out, 16)
            sp.dma_start(starts[:, 0:2 * NWIN], starts_dram.rearrange("(o n) -> o n", o=1)).then_inc(starts_out, 16)
            sp.wait_ge(starts_out, 32)
            phase_end(sp, 3)

            fast = sp.value_load(starts[0:1, 2 * NWIN:2 * NWIN + 1], min_val=0, max_val=1)
            with sp.If(fast == 1):
                with sp.Fori(0, NWIN // WS) as i:
                    for s in range(WS):
                        sp.wait_ge(rel_ready, i * WS + s + 1)
                        packed = sp.value_load(starts[0:1, bass.ds(i * 2 * WS + 2 * s, 1)], min_val=0, max_val=(TILES * BLK - CAP) * PACK)
                        for k in range(2):
                            first = packed // PACK + packed % PACK if k else packed // PACK
                            sp.dma_start(rec[:, s, k, :], records[bass.ds(first, CAP), :].rearrange("(p t) c -> p (t c)", p=BLK)).then_inc(rec_in[s], 16)
            with sp.If(fast == 0):
                with sp.Fori(0, NH) as h:
                    sp.wait_ge(stage_ready, h + 2)
                    sp.dma_start(counts[bass.ds(h + 1, 1)].rearrange("o b a d -> b (o a d)"),
                                 ap1(stage[:, bass.ds(h % 2, 1), :])).then_inc(counts_out, 16)
                    with sp.Fori(0, 2) as pair:
                        for odd in range(2):
                            q = pair * 2 + odd
                            sp.wait_ge(linked_full, (h + 1) * 4 + q + 1)
                            sp.dma_start(linked[bass.ds((h + 1) * HALF + part_at(pair, odd), BLK), :],
                                         ap1(linked_sb[:, bass.ds(q % 2, 1), :])).then_inc(linked_out, 16)
                            sp.wait_ge(linked_out, (h * 4 + q + 1) * 16)
                            sp.sem_inc(linked_free, 1)
                    sp.wait_ge(counts_out, (h + 1) * 16)
                    sp.sem_inc(stage_free, 1)
            phase_end(sp, 4)
            phase_end(sp, 5)
            sp.sem_inc(cnt_free, CS)
            with sp.If(fast == 0):
                load_counts(sp, 0)
            with sp.If(fast == 1):
                for g in range(NGRP):
                    sp.sem_inc(cnt_in[g], CHUNKS * 32)
                sp.sem_inc(cnt_free, ROWS // GRP)
                sp.sem_inc(agg_done, CHUNKS)
                sp.sem_inc(agg_kept, 2 * CHUNKS)
                sp.sem_inc(agg_turned, CHUNKS)
            phase_end(sp, 6)
            for l in range(3):
                phase_reached(sp)
                if l == 0:
                    sp.sem_inc(link_free, LS)
                with sp.Fori(0, NB // LS) as b:
                    for s in range(LS):
                        sp.wait_ge(link_free, b * LS + (l * NB + s + 1))
                        sp.dma_start(link[:, s, :], linked[bass.ds(b * LS * BLK + (s * BLK + HALF), BLK), :]).then_inc(link_in[s], 16)
                phase_end(sp, 8 + 4 * l)
                phase_reached(sp)
                load_counts(sp, 1 + l)
                phase_end(sp, 10 + 4 * l)
            phase_reached(sp)
            load_counts(sp, 4)
            phase_end(sp, 20)
            phase_reached(sp)
            load_counts(sp, 5)
            phase_end(sp, 22)
            phase_end(sp, 23)
            sp.dma_start(out[0:(NB - 1) * BLK, :].rearrange("(a b) f -> b a f", b=BLK), X[:, 0:NB - 1, :]).then_inc(out_stored, 16)
            sp.dma_start(out[(NB - 1) * BLK:N, :], X[0:N - (NB - 1) * BLK, NB - 1, :]).then_inc(out_stored, 16)
            sp.wait_ge(out_stored, 32)

        @block.gpsimd
        def _(pool):
            nc.gpsimd.memset(dst_i[:], NP - 1).then_inc(pads_set, 1)
            nc.gpsimd.memset(src_i[:], NP - 1).then_inc(pads_set, 1)
            nc.gpsimd.memset(raw[:, 4, :], 0.0).then_inc(pads_set, 1)
            nc.gpsimd.memset(X[:, NB - 1, :], 0.0).then_inc(pads_set, 1)
            nc.gpsimd.memset(next_i[:], NP - 1).then_inc(pads_set, 1)
            nc.gpsimd.iota(iota_f[:], [[1, BLK]], base=0, channel_multiplier=0, allow_small_or_imprecise_dtypes=True)
            nc.gpsimd.iota(part[:], [[1, 1]], base=0, channel_multiplier=1, allow_small_or_imprecise_dtypes=True)
            nc.gpsimd.iota(key_iota[:], [[1, NB], [KEY, WIN]], base=0, channel_multiplier=0, allow_small_or_imprecise_dtypes=True)
            nc.gpsimd.iota(win_first[:], [[WIN, NWIN]], base=0, channel_multiplier=0, allow_small_or_imprecise_dtypes=True)
            nc.gpsimd.iota(win_last[:], [[WIN, NWIN]], base=WIN - 1, channel_multiplier=0, allow_small_or_imprecise_dtypes=True)
            nc.gpsimd.iota(neg_key[:], [[-WIN * KEY, NWIN]], base=0, channel_multiplier=0, allow_small_or_imprecise_dtypes=True)
            nc.gpsimd.iota(iota_t[:], [[1, BLK], [0, HT]], base=0, channel_multiplier=0, allow_small_or_imprecise_dtypes=True)
            nc.gpsimd.iota(tile_up[:], [[BLK, G]], base=1, channel_multiplier=1, allow_small_or_imprecise_dtypes=True)
            nc.gpsimd.iota(tile_dn[:], [[-BLK, G]], base=TILES, channel_multiplier=-1, allow_small_or_imprecise_dtypes=True)
            nc.gpsimd.memset(zero16[:], 0.0)
            nc.gpsimd.memset(zero_b[:], 0.0)
            nc.gpsimd.memset(ones[:], 1.0)
            pool.drain().then_inc(iotas_done, 1)
            phase_end(pool, 1)
            phase_end(pool, 2)
            phase_end(pool, 3)

            def self_loops(h):
                pool.wait_ge(stage_full, h + 1)
                odd = h % 2
                for k in range(3):
                    blk_at = (h // 2) * CB + odd * 4 + k
                    at = stage[:, bass.ds(odd, 1), bass.ds(blk_at * HALF + odd * (BLK // 2) + k * BLK, BLK)]
                    nc.gpsimd.tensor_tensor(ap1(at), ap1(at), unit16[:], ALU.add)
                at = stage[:, bass.ds(odd, 1), bass.ds(((h // 2) * CB + 3) * HALF + 3 * BLK - odd * 3 * BLK, BLK // 2)]
                nc.gpsimd.tensor_tensor(ap1(at), ap1(at), ap1(halves16[:, bass.ds(odd, 1), :]), ALU.add)
                pool.drain().then_inc(stage_ready, 1)

            fast = pool.value_load(starts[0:1, 2 * NWIN:2 * NWIN + 1], min_val=0, max_val=1)
            with pool.If(fast == 1):
                nc.gpsimd.iota(sub_iota[:], [[SUB * KEY, 2], [1, NB], [KEY, SUB]], base=0, channel_multiplier=0, allow_small_or_imprecise_dtypes=True)
                pool.drain()
                pool.sem_inc(rel_ready, WS)

                def keys_of(w, s, i, whole):
                    pool.wait_ge(rec_in[s], i * 128 + 32 * (whole + 1))
                    pool.wait_ge(keys_ready, w + 1)
                    both = rec[:, s, :, :].rearrange("p k (t c) -> p (k t) c", c=2)
                    nc.gpsimd.tensor_tensor(key_rel[:, s, :], both[:, :, 0], neg_key[:, bass.ds(w, 1)].broadcast_to([BLK, 2 * ST]), ALU.add)
                    nc.gpsimd.tensor_copy(src_rel[:, s, :], both[:, :, 1]).then_inc(rel_ready, 1)

                AHEAD = 6
                for k in range(AHEAD):
                    keys_of(k, k % WS, 0, k // WS)
                with pool.Fori(0, NH - 1) as h:
                    for k in range(AHEAD, 28 + AHEAD):
                        keys_of(h * 28 + k, k % WS, h, k // WS)
                    self_loops(h)
                for k in range((NH - 1) * 28 + AHEAD, NWIN):
                    keys_of(k, k % WS, 0, k // WS)
                self_loops(NH - 1)
            with pool.If(fast == 0):
                with pool.Fori(0, NH) as h:
                    self_loops(h)
            phase_end(pool, 4)
            for k in range(5, 24):
                phase_end(pool, k)

        @block.vector
        def _(dve):
            def root(k):
                dve.drain().then_inc(root_in, 1)
                dve.wait_ge(root_out, k)
                nc.vector.reciprocal(stat[1][:], stat[1][:])
                dve.drain()

            def per_node(v, width=D):
                return v[:].unsqueeze(2).broadcast_to([BLK, NB, width])

            def per_feature(v, width=D):
                return v[:].unsqueeze(1).broadcast_to([BLK, NB, width])

            def layernorm_relu(k, XC=XC, SQ=SQ, HIN=HIN):
                nc.vector.tensor_reduce(stat[0][:], X[:], AX.X, ALU.add)
                dve.drain()
                nc.vector.tensor_scalar(stat[0][:], stat[0][:], 1.0 / D, None, ALU.mult)
                dve.drain()
                nc.vector.tensor_tensor(XC[:], X[:], per_node(stat[0]), ALU.subtract)
                dve.drain()
                nc.vector.tensor_tensor(SQ[:], XC[:], XC[:], ALU.mult)
                dve.drain()
                nc.vector.tensor_reduce(stat[2][:], SQ[:], AX.X, ALU.add)
                dve.drain()
                nc.vector.tensor_scalar(stat[2][:], stat[2][:], 1.0 / D, LN_EPS, ALU.mult, ALU.add)
                root(k)
                nc.vector.tensor_tensor(HIN[:], XC[:], per_node(stat[1]), ALU.mult)
                dve.drain()
                nc.vector.tensor_scalar(HIN[:], HIN[:], 0.0, None, ALU.max)
                dve.drain()

            def split_features(HIN=HIN, XC=XC, H12=H12, H3=H3):
                nc.vector.tensor_copy(H12[:, :, 0:D], HIN[:])
                nc.vector.memset(H3[:, :, D:D + 1], 1.0)
                dve.drain()
                nc.vector.tensor_tensor(XC[:], HIN[:], H12[:, :, 0:D], ALU.subtract)
                dve.drain()
                nc.vector.tensor_copy(H12[:, :, D:2 * D], XC[:])
                dve.drain()
                nc.vector.tensor_tensor(H3[:, :, 0:D], XC[:], H12[:, :, D:2 * D], ALU.subtract)

            def l0_features(HIN, XC, SQ, H12, H3):
                layernorm_relu(1, XC, SQ, HIN)
                nc.vector.tensor_copy(stat[2][:], out_deg[:])
                root(2)
                nc.vector.tensor_tensor(HIN[:], HIN[:], per_node(stat[1]), ALU.mult)
                dve.drain()
                split_features(HIN, XC, H12, H3)
            dve.wait_ge(iotas_done, 1)
            nc.vector.tensor_copy(iota_b[:], iota_f[:])
            nc.vector.tensor_scalar(ident[:], iota_f[:], part[:, 0:1], None, ALU.is_equal)
            dve.drain()
            nc.vector.tensor_copy(ident16[:], ident[:])
            nc.vector.tensor_scalar(unit16[:], ident[:], UNIT, None, ALU.mult)
            nc.vector.tensor_scalar(unscale[:], ident[0:D + 1, 0:D + 1], 1.0 / UNIT, None, ALU.mult)
            nc.vector.memset(fold[:], 0.0)
            dve.drain()
            nc.vector.tensor_tensor(fold[:, 0:D], ident[:, 0:D], ident[:, D:2 * D], ALU.add)
            dve.drain()
            nc.vector.tensor_scalar(fold[:, 0:D], fold[:, 0:D], 1.0 / UNIT, None, ALU.mult)
            nc.vector.tensor_scalar(sub_rows[:, 1, :], iota_f[:, 0:SUBS], float(SUB), None, ALU.mult)
            dve.drain()
            nc.vector.tensor_scalar(sub_rows[:, 0, :], sub_rows[:, 1, :], part[:, 0:1], 0.0, ALU.subtract, ALU.is_gt)
            dve.drain()
            nc.vector.tensor_scalar(sub_rows[:, 1, :], sub_rows[:, 1, :], part[:, 0:1], float(-SUB), ALU.subtract, ALU.is_gt)
            dve.drain()
            nc.vector.tensor_tensor(sub_rows[:, 1, :], sub_rows[:, 1, :], sub_rows[:, 0, :], ALU.subtract)
            dve.wait_ge(edges_in, 12 * 16)
            nc.vector.tensor_copy(raw[:, 3, :], dst_i[:])
            nc.vector.tensor_single_scalar(tmp_i[:], src_i[:], 7, ALU.arith_shift_right)
            dve.drain()
            nc.vector.tensor_copy(raw[:, 2, :], tmp_i[:])
            dve.drain()
            nc.vector.tensor_single_scalar(tmp_i[:], src_i[:], BLK - 1, ALU.bitwise_and)
            dve.drain()
            nc.vector.tensor_copy(raw[:, 1, :], tmp_i[:])
            nc.vector.scalar_tensor_tensor(raw[:, 0, :], raw[:, 3, :], float(KEY), raw[:, 2, :], ALU.mult, ALU.add)
            dst3 = raw[:, 3, :].rearrange("p (g e) -> p g e", g=G)
            nc.vector.tensor_reduce(tile_lo[:], dst3, AX.X, ALU.min)
            nc.vector.tensor_reduce(tile_hi[:], dst3, AX.X, ALU.max)
            nc.vector.memset(hilo[:], 0.0)
            dve.drain()
            nc.vector.tensor_copy(record[:, :, 0], raw[:, 0, :])
            nc.vector.tensor_copy(record[:, :, 1], raw[:, 1, :])
            dve.drain().then_inc(record_ready, 1)
            nc.vector.tensor_copy(next_f[:], next_i[:])
            falls = falls_at.rearrange("p (g e) -> p g e", g=G)
            nc.vector.tensor_tensor(falls[:, :, 0:BLK - 1], dst3[:, :, 0:BLK - 1], dst3[:, :, 1:BLK], ALU.is_gt)
            dve.drain()
            nc.vector.tensor_tensor(falls[:, :, BLK - 1], dst3[:, :, BLK - 1], next_f[:], ALU.is_gt)
            nc.vector.memset(misfit[:], 0.0)
            dve.drain()
            nc.vector.tensor_reduce(misfit[:, 0:1], falls_at[:], AX.X, ALU.max)
            phase_end(dve, 1)
            for g in range(G):
                nc.vector.tensor_scalar(over[:, 0, :], win_last[:], tile_lo[:, g:g + 1], None, ALU.is_ge)
                dve.drain()
                nc.vector.scalar_tensor_tensor(over[:, 1, :], win_first[:], tile_hi[:, g:g + 1], over[:, 0, :], ALU.is_le, ALU.mult)
                dve.drain()
                nc.vector.scalar_tensor_tensor(hilo[:, 0, :], over[:, 1, :], tile_up[:, g:g + 1], hilo[:, 0, :], ALU.mult, ALU.max)
                nc.vector.scalar_tensor_tensor(hilo[:, 1, :], over[:, 1, :], tile_dn[:, g:g + 1], hilo[:, 1, :], ALU.mult, ALU.max)
                dve.drain()
            dve.drain().then_inc(hilo_ready, 1)
            dve.wait_ge(hilo_turned, 1)
            nc.vector.tensor_reduce(hl_max[:], banks(2, 2)[0:BQ, :].rearrange("p (k n) -> p k n", k=8), AX.X, ALU.max)
            dve.drain()
            nc.vector.tensor_scalar(hl_max[:, 4:8], hl_max[:, 4:8], -1.0, float(TILES), ALU.mult, ALU.add)
            nc.vector.tensor_scalar(hl_max[:, 0:4], hl_max[:, 0:4], float(TILES), 1.0, ALU.min, ALU.add)
            dve.drain()
            nc.vector.tensor_copy(hl_int[:], hl_max[:])
            dve.drain()
            nc.vector.tensor_single_scalar(hl_int[:], hl_int[:], 1, ALU.arith_shift_right)
            dve.drain()
            nc.vector.tensor_copy(hl_max[:], hl_int[:])
            dve.drain()
            nc.vector.tensor_scalar(hl_max[:, 0:4], hl_max[:, 0:4], 1.0, None, ALU.max)
            dve.drain()
            nc.vector.scalar_tensor_tensor(hl_max[:, 4:8], hl_max[:, 0:4], -1.0, hl_max[:, 4:8], ALU.add, ALU.min)
            dve.drain()
            nc.vector.tensor_copy(hl_int[:], hl_max[:])
            dve.drain().then_inc(bounds_ready, 1)
            dve.wait_ge(group_kept, 2 * G)
            nc.vector.tensor_copy(ea3[:, 0, :], ea_rest[:])
            nc.vector.tensor_copy(ints[:, 0, :], dst_t)
            dve.drain()
            nc.vector.tensor_tensor(ea_part[:], ea_rest[:], ea3[:, 0, :], ALU.subtract)
            nc.vector.tensor_single_scalar(ints[:, 1, :], ints[:, 0, :], 7, ALU.arith_shift_right)
            dve.drain()
            nc.vector.tensor_copy(ea3[:, 1, :], ea_part[:])
            nc.vector.tensor_copy(hist_a[:, 1, :], ints[:, 1, :])
            nc.vector.tensor_single_scalar(ints[:, 0, :], ints[:, 0, :], BLK - 1, ALU.bitwise_and)
            dve.drain()
            nc.vector.tensor_tensor(ea3[:, 2, :], ea_part[:], ea3[:, 1, :], ALU.subtract)
            nc.vector.tensor_copy(hist_b[:, 1, :], ints[:, 0, :])
            nc.vector.tensor_copy(hist_b[:, 0, :], srcb_t)
            nc.vector.tensor_copy(hist_a[:, 0, :], srca_t)
            phase_end(dve, 2)
            with dve.Fori(0, TILES // HT // 2) as i:
                for s in range(2):
                    dve.wait_ge(hist_used, i * 2 + s + 1)
                    tiles = bass.ds(i * 2 * HT + s * HT, HT)
                    rows = hot_b[:, 2 * s:2 * s + 2, :].rearrange("p k (b t) -> p k b t", t=HT)
                    cols = hot_a[:, 5 * s:5 * s + 5, :].rearrange("p k (a t) -> p k a t", t=HT)
                    nc.vector.tensor_tensor(cols[:, 0:2], iota_t[:, 0:NB, :].unsqueeze(1).broadcast_to([BLK, 2, NB, HT]),
                                            hist_a[:, :, tiles].unsqueeze(2).broadcast_to([BLK, 2, NB, HT]), ALU.is_equal)
                    nc.vector.tensor_tensor(rows, iota_t[:].unsqueeze(1).broadcast_to([BLK, 2, BLK, HT]),
                                            hist_b[:, :, tiles].unsqueeze(2).broadcast_to([BLK, 2, BLK, HT]), ALU.is_equal)
                    dve.drain()
                    nc.vector.tensor_tensor(cols[:, 2:5], cols[:, 1:2].broadcast_to([BLK, 3, NB, HT]),
                                            ea3[:, :, tiles].unsqueeze(2).broadcast_to([BLK, 3, NB, HT]), ALU.mult).then_inc(hist_ready, 1)
            dve.wait_ge(hist_done, 1)
            nc.vector.tensor_scalar(out_deg[:], psum[:, 0, 0:NB], 1.0, None, ALU.max)
            nc.vector.tensor_copy(in_deg[:, 0, :], psum[:, 1, 0:NB])
            nc.vector.tensor_reduce(ea_sum[:], psum[:, 1, NB:4 * NB].rearrange("p (k a) -> p a k", k=3), AX.X, ALU.add)
            nc.vector.memset(prefix[:, 0, 0:1], 0.0)
            dve.drain()
            nc.vector.tensor_copy(prefix[:, 0, 1:NB], in_deg[:, 0, 0:NB - 1])
            dve.drain()
            at, step = 0, 1
            while step < NB:
                nc.vector.tensor_copy(prefix[:, 1 - at, 0:step], prefix[:, at, 0:step])
                nc.vector.tensor_tensor(prefix[:, 1 - at, step:NB], prefix[:, at, step:NB], prefix[:, at, 0:NB - step], ALU.add)
                dve.drain()
                at, step = 1 - at, 2 * step
            assert at == 0
            dve.drain().then_inc(degrees_ready, 1)
            dve.wait_ge(starts_summed, 1)
            nc.vector.tensor_copy(sub_at[:], psum[0:SUBS, 2, 0:NB])
            nc.vector.tensor_copy(sub_num[:], psum[0:SUBS, 3, 0:NB])
            dve.drain()
            nc.vector.tensor_single_scalar(sub_at[:], sub_at[:], PACK.bit_length() - 1, ALU.arith_shift_left)
            dve.drain()
            nc.vector.tensor_tensor(sub_at[:], sub_at[:], sub_num[:], ALU.bitwise_or)
            dve.drain().then_inc(starts_ready, 1)
            nc.vector.memset(sub_max[:], 0.0)
            dve.drain()
            nc.vector.tensor_reduce(sub_max[:, 0:1], psum[0:SUBS, 3, 0:NB - 1], AX.X, ALU.max)
            real = -(-(N - (NB - 1) * BLK) // SUB)
            nc.vector.tensor_copy(sub_max[0:real, 1:2], psum[0:real, 3, NB - 1:NB])
            dve.drain()
            nc.vector.tensor_scalar(sub_max[:], sub_max[:], float(CAP), None, ALU.is_gt)
            dve.drain()
            nc.vector.tensor_tensor(misfit[0:SUBS, 1:2], sub_max[:, 0:1], sub_max[:, 1:2], ALU.add)
            dve.drain()
            nc.vector.tensor_tensor(misfit[:, 2:3], misfit[:, 0:1], misfit[:, 1:2], ALU.add)
            dve.drain().then_inc(misfit_ready, 1)
            dve.wait_ge(misfit_turned, 1)
            nc.vector.tensor_reduce(misfit_top[:], psum[0:1, 4, 0:BLK], AX.X, ALU.max)
            dve.drain()
            nc.vector.tensor_scalar(misfit_top[:], misfit_top[:], 0.0, None, ALU.is_equal)
            dve.drain()
            nc.vector.tensor_copy(starts[:, 2 * NWIN:2 * NWIN + 1], misfit_top[:])
            phase_end(dve, 3)
            nc.vector.memset(stage[:, 1, :], 0.0)
            dve.drain().then_inc(stage_ready, 1)
            fast = dve.value_load(starts[0:1, 2 * NWIN:2 * NWIN + 1], min_val=0, max_val=1)
            with dve.If(fast == 1):
                l0_features(L_in, L_xc, L_sq, L12, L3p)
                dve.drain().then_inc(l0_ready, 1)
                dve.sem_inc(keys_ready, WS)
                with dve.Fori(0, NH) as h:
                    for k in range(WH):
                        s, at = k % WS, k % SS
                        dve.wait_ge(rel_ready, h * WH + (k + WS + 1))
                        dve.wait_ge(turn_done, h * WH + (k + 1))
                        nc.vector.tensor_tensor(sub_src[:, at], iota_t[:, :, 0:2 * ST],
                                                src_rel[:, s, :].unsqueeze(1).broadcast_to([BLK, BLK, 2 * ST]), ALU.is_equal)
                        for t in range(2 * ST):
                            last = nc.vector.tensor_scalar(sub_key[:, at, t, :], sub_iota[:, t // ST, :],
                                                           key_rel[:, s, t:t + 1], None, ALU.is_equal)
                        last.then_inc(keys_ready, 1)
            with dve.If(fast == 0):
                visits = dve.alloc_register("dve_visits")
                dve.reg_mov(visits, 0)
                with dve.Fori(0, NWIN) as w:
                    lo = dve.value_load(bounds[0:1, bass.ds(w + NWIN, 1)], min_val=0, max_val=TILES // 2 - 1)
                    hi = dve.value_load(bounds[0:1, bass.ds(w, 1)], min_val=1, max_val=TILES // 2)
                    with dve.Fori(lo, hi) as i:
                        v = dve.snap(visits)
                        dve.wait_ge(slot_free, v + 1)
                        for t in range(2):
                            nc.vector.tensor_scalar(ap1(hot_key[:, bass.ds(v % SL, 1), t * NB * WIN:(t + 1) * NB * WIN]),
                                                    key_iota.rearrange("p a d -> p (a d)"), key_t[:, bass.ds(i * 2 + t, 1)],
                                                    neg_key[:, bass.ds(w, 1)], ALU.subtract, ALU.is_equal)
                            last = nc.vector.tensor_scalar(ap1(hot_src[:, bass.ds(v % SL, 1), t * BLK:(t + 1) * BLK]), iota_b[:],
                                                    srcb_t[:, bass.ds(i * 2 + t, 1)], None, ALU.is_equal)
                        last.then_inc(keys_ready, 1)
                        dve.reg_add(visits, visits, 1)
            phase_end(dve, 4)
            def count_sums(n):
                with dve.Fori(0, CHUNKS) as c:
                    dve.wait_ge(agg_turned, c + n)
                    dve.wait_ge(agg_done, c + (n + 1))
                    nc.vector.tensor_copy(TB[0:D + 1, :].rearrange("p (t d) -> p t d", t=2), psum[0:D + 1, 2:4, 0:HALF]).then_inc(agg_kept, 1)

            AGG3 = AGG[:, 0:NB * (D + 1)].rearrange("p (a f) -> p a f", a=NB)

            for (_, fo, _, a_both, a_rows, _, _, _) in att:
                nc.vector.tensor_scalar(a_rows[:], ones[0:fo, :], a_both[:, 0:1], None, ALU.mult)
            with dve.If(fast == 0):
                l0_features(HIN, XC, SQ, H12, H3)
            with dve.If(fast == 1):
                nc.vector.tensor_tensor(HIN[:], L12[:, :, 0:D], L12[:, :, D:2 * D], ALU.add)
                dve.drain()
                nc.vector.tensor_tensor(HIN[:], HIN[:], L3p[:, :, 0:D], ALU.add)
            phase_end(dve, 5)
            with dve.If(fast == 0):
                count_sums(0)
            phase_end(dve, 6)
            nc.vector.tensor_copy(deg[:], AGG3[:, :, D])
            nc.vector.tensor_tensor(XC[:], AGG3[:, :, 0:D], HIN[:], ALU.subtract)
            dve.drain()
            nc.vector.tensor_scalar(stat[2][:], deg[:], -1.0, 1.0, ALU.add, ALU.max)
            root(3)
            nc.vector.tensor_tensor(XC[:], XC[:], per_node(stat[1]), ALU.mult)
            dve.drain()
            nc.vector.tensor_tensor(X[:], X[:], XC[:], ALU.add)
            dve.drain()
            layernorm_relu(4)
            for l, (ki, fo, W, a_both, a_rows, _, _, _) in enumerate(att):
                dve.drain().then_inc(input_ready, 1)
                with dve.Fori(0, CHUNKS) as c:
                    dve.wait_ge(feats_done, c + (l * CHUNKS + 1))
                    HF3 = HF[:, 0:NB * (fo + 1)].rearrange("p (a f) -> p a f", a=NB)
                    nc.vector.tensor_copy(HF3[:, bass.ds(c * CB, CB), 0:fo], psum[:, 2, 0:CB * fo].rearrange("p (a f) -> p a f", a=CB)).then_inc(feats_kept, 1)
                    dve.wait_ge(scores_done, c + (l * CHUNKS + 1))
                    nc.vector.tensor_copy(ROW1[:, bass.ds(c * CW, CW)].rearrange("p (t d) -> p t d", t=2), psum[:, 5:7, 0:HALF])
                    scores = psum[:, 7, 0:2 * CB].rearrange("p (a k) -> p a k", k=2)
                    nc.vector.tensor_scalar(sj8[:, bass.ds(c * CB, CB)], scores[:, :, 0], 1.0 - SLOPE, None, ALU.mult)
                    nc.vector.tensor_scalar(sj2[:, bass.ds(c * CB, CB)], scores[:, :, 0], SLOPE, None, ALU.mult)
                    nc.vector.tensor_copy(si[:, bass.ds(c * CB, CB)], scores[:, :, 1]).then_inc(scores_kept, 1)
                nc.vector.memset(HF3[:, :, fo:fo + 1], 1.0)
                dve.drain()
                nc.vector.tensor_reduce(low[:], ROW1[:], AX.X, ALU.min)
                dve.drain()
                nc.vector.tensor_scalar(ROW1[:], ROW1[:], low[:, 0:1], 1.0, ALU.subtract, ALU.add)
                phase_end(dve, 7 + 4 * l)
                def greatest(b, count):
                    for s in range(count):
                        dve.wait_ge(link_in[s], b * 16 + (l * (NB // LS) + 1) * 16)
                        if s == 0:
                            nc.vector.memset(top_now[:], 0.0)
                            dve.drain()
                        else:
                            nc.vector.tensor_copy(top[:, bass.ds(b * LS + (s - 1), 1)], top_now[:, s - 1:s])
                        nc.vector.tensor_tensor_reduce(out=junk[:], in0=link[:, s, :], in1=ROW1[:], scale=1.0, scalar=0.0,
                                                       op0=ALU.mult, op1=ALU.max, accum_out=top_now[:, s:s + 1])
                        dve.drain().then_inc(link_free, 1)
                    nc.vector.tensor_copy(top[:, bass.ds(b * LS + (count - 1), 1)], top_now[:, count - 1:count])
                    dve.drain()

                with dve.Fori(0, NB // LS) as b:
                    greatest(b, LS)
                dve.drain()
                nc.vector.tensor_scalar(top[:], top[:], low[:, 0:1], -1.0, ALU.add, ALU.add)
                dve.drain()
                nc.vector.tensor_tensor(c1[:], si[:], top[:], ALU.add)
                dve.drain()
                nc.vector.scalar_tensor_tensor(top[:], c1[:], SLOPE, c1[:], ALU.mult, ALU.max)
                dve.drain()
                nc.vector.tensor_tensor(c1[:], si[:], top[:], ALU.subtract)
                nc.vector.scalar_tensor_tensor(c2[:], si[:], SLOPE, top[:], ALU.mult, ALU.subtract)
                phase_end(dve, 8 + 4 * l)
                with dve.Fori(0, CHUNKS) as c:
                    dve.wait_ge(diag_spread, c + (l * CHUNKS + 1))
                    for k, v in enumerate((c1, c2)):
                        for b in range(CB):
                            to = ap1(YE[:, bass.ds(c % 2 * 2 + k, 1), b * BLK:(b + 1) * BLK])
                            last = nc.vector.tensor_scalar(to, ident[:], v[:, bass.ds(c * CB + b, 1)], None, ALU.mult)
                    last.then_inc(diag_ready, 1)
                phase_end(dve, 9 + 4 * l)

                def exponent(r, c):
                    nc.vector.scalar_tensor_tensor(YE[:, slot(r, 4), :], ROW1[:, bass.ds(c * CW, CW)], sj8[:, r:r + 1],
                                                   ROW2[:, bass.ds(c * CW, CW)], ALU.add, ALU.max).then_inc(y_ready, 1)

                def chunk(c, last):
                    for r in range(NB):
                        if r + 2 < NB or not last:
                            if r >= 2 and r + 2 != NB - 1:
                                back = 2 if r + 2 < NB else 3
                                dve.wait_ge(p_ready, c * NB + (l * ROWS + r + 1 - back))
                            exponent((r + 2) % NB, c + (r + 2) // NB)
                        g, j = divmod(r, GRP)
                        if j == 0:
                            dve.wait_ge(cnt_in[g], c * 32 + 32 * ((1 + l) * CHUNKS + 1))
                        dve.wait_ge(e_ready, c * NB + (l * ROWS + r + 1))
                        if r < NB - 1:
                            dve.wait_ge(p_used, c * NB + (l * ROWS + (r if r < 3 else r + 1)))
                        nc.vector.scalar_tensor_tensor(PW[:, slot(r, 3), :], YE[:, slot(r, 4), :], 1.0, counts_of(g, j),
                                                       ALU.min, ALU.mult).then_inc(p_ready, 1)
                        if j == GRP - 1:
                            dve.drain().then_inc(cnt_free, 1)

                exponent(0, 0)
                exponent(1, 0)
                with dve.Fori(0, CHUNKS - 1) as c:
                    chunk(c, False)
                chunk(CHUNKS - 1, True)
                phase_end(dve, 10 + 4 * l)
                A3 = AGG[:, 0:NB * (fo + 1)].rearrange("p (a f) -> p a f", a=NB)
                XO = XC[:, :, 0:fo]
                nc.vector.tensor_scalar(stat[0][:], A3[:, :, fo], DEN_EPS * UNIT, None, ALU.add)
                dve.drain()
                nc.vector.reciprocal(stat[0][:], stat[0][:])
                dve.drain()
                nc.vector.tensor_tensor(XO, A3[:, :, 0:fo], per_node(stat[0], fo), ALU.mult)
                dve.drain()
                if l == 0:
                    nc.vector.tensor_tensor(XO, XO, per_feature(row['L1_gnn_b1'], fo), ALU.add)
                    dve.drain()
                    nc.vector.tensor_scalar(HIN[:, :, 0:fo], XO, 0.0, None, ALU.max)
                    dve.drain()
                if l == 1:
                    nc.vector.tensor_tensor(XO, XO, per_feature(row['L1_gnn_b2']), ALU.add)
                    dve.drain()
                    nc.vector.tensor_tensor(X[:], X[:], XO, ALU.add)
                    dve.drain()
                    layernorm_relu(5)
                if l == 2:
                    nc.vector.tensor_tensor(XO, XO, per_feature(row['L2_gnn_bias']), ALU.add)
                    dve.drain()
                    nc.vector.tensor_tensor(SQ[:], XO, XO, ALU.mult)
                    dve.drain()
                    nc.vector.tensor_reduce(stat[2][:], SQ[:], AX.X, ALU.add)
                    dve.drain().then_inc(root_in, 1)
                    dve.wait_ge(root_out, 6)
                    nc.vector.tensor_scalar(stat[1][:], stat[1][:], NORM_EPS, None, ALU.max)
                    dve.drain()
                    nc.vector.reciprocal(stat[1][:], stat[1][:])
                    dve.drain()
                    nc.vector.tensor_tensor(XO, XO, per_node(stat[1]), ALU.mult)
                    dve.drain()
                    nc.vector.tensor_tensor(X[:], X[:], XO, ALU.add)
                    dve.drain()
                    layernorm_relu(7)
            split_features()
            phase_end(dve, 19)
            count_sums(4 * CHUNKS)
            phase_end(dve, 20)
            nc.vector.tensor_tensor(US[:, :, 0:D], HIN[:], per_node(deg), ALU.mult)
            nc.vector.tensor_copy(US[:, :, D:2 * D], AGG3[:, :, 0:D])
            nc.vector.tensor_copy(DE[:, :, 0], deg[:])
            nc.vector.tensor_copy(DE[:, :, 1], ea_sum[:])
            dve.drain().then_inc(mlp_copied, 1)
            def degrees_out(c):
                dve.wait_ge(mlp_turned, c + 1)
                nc.vector.tensor_copy(DET, banks(2, 2)[0:2, 0:CW]).then_inc(mlp_kept, 1)

            def dense_out(c):
                dve.wait_ge(mlp_out2, c + 1)
                both = banks(4, 2)[:, 0:CW].rearrange("p (a f) -> p a f", a=CB)
                nc.vector.tensor_copy(GI[:, bass.ds(c * CB, CB), :], both[:, :, 0:D])
                nc.vector.tensor_copy(HIN[:, bass.ds(c * CB, CB), :], both[:, :, D:2 * D])
                dve.drain().then_inc(mlp_stored, 1)

            degrees_out(0)
            with dve.Fori(0, CHUNKS - 1) as c:
                dve.wait_ge(mlp_out, c + 1)
                degrees_out(c + 1)
                dense_out(c)
            dense_out(CHUNKS - 1)
            split_features()
            phase_end(dve, 21)
            count_sums(5 * CHUNKS)
            phase_end(dve, 22)
            nc.vector.tensor_tensor(GI[:], GI[:], per_feature(row['L3_gnn_b2']), ALU.add)
            nc.vector.tensor_copy(XC[:], per_feature(row['we2']))
            dve.drain()
            nc.vector.tensor_tensor(GI[:], GI[:], per_node(deg), ALU.mult)
            nc.vector.tensor_tensor(XC[:], XC[:], per_node(ea_sum), ALU.mult)
            dve.drain()
            nc.vector.tensor_tensor(GI[:], GI[:], AGG3[:, :, 0:D], ALU.add)
            dve.drain()
            nc.vector.tensor_tensor(GI[:], GI[:], XC[:], ALU.add)
            dve.drain()
            nc.vector.tensor_scalar(GI[:], GI[:], 0.0, None, ALU.max)
            dve.drain()
            nc.vector.tensor_reduce(stat[0][:], GI[:], AX.X, ALU.max)
            dve.drain()
            nc.vector.tensor_tensor(GI[:], GI[:], per_node(stat[0]), ALU.subtract)
            dve.drain().then_inc(root_in, 1)
            dve.wait_ge(root_out, 8)
            nc.vector.tensor_reduce(stat[2][:], SQ[:], AX.X, ALU.add)
            dve.drain().then_inc(root_in, 1)
            dve.wait_ge(root_out, 9)
            nc.vector.tensor_tensor(GI[:], GI[:], per_node(stat[1]), ALU.subtract)
            dve.drain()
            nc.vector.tensor_tensor(X[:], X[:], GI[:], ALU.add)
            phase_end(dve, 23)

        @block.tensor
        def _(pe):
            phase_end(pe, 1)
            with pe.Fori(0, G) as g:
                pe.wait_ge(group_copied, g + 1)
                for k in range(5):
                    last = nc.tensor.transpose(banks(0, 2)[:, k * BLK:(k + 1) * BLK], grp[:, k, :], ident[:])
                last.then_inc(group_turned, 1)
                pe.wait_ge(group_kept, 2 * (g + 1))
            pe.wait_ge(hilo_ready, 1)
            for s in range(2):
                for q in range(4):
                    k = s * 4 + q
                    last = nc.tensor.transpose(banks(2, 2)[0:BQ, k * BLK:(k + 1) * BLK], hilo[:, s, q * BQ:(q + 1) * BQ], ident[:])
            last.then_inc(hilo_turned, 1)
            phase_end(pe, 2)
            pe.sem_inc(hist_used, 2)
            for k in range(2):
                nc.tensor.matmul(psum[:, k, 0:4 * NB], zero_b[:, 0:BLK], zero_b[:, 0:4 * NB], start=True, stop=False, skip_group_check=True)
            with pe.Fori(0, TILES // HT // 2) as i:
                for s in range(2):
                    pe.wait_ge(hist_ready, i * 2 + s + 1)
                    for t in range(HT):
                        rows = hot_b[:, 2 * s:2 * s + 2, :].rearrange("p k (b t) -> p k b t", t=HT)[:, :, :, t]
                        cols = hot_a[:, 5 * s:5 * s + 5, :].rearrange("p k (a t) -> p k a t", t=HT)[:, :, :, t]
                        nc.tensor.matmul(psum[:, 0, 0:NB], rows[:, 0, :], cols[:, 0, :], start=False, stop=False, skip_group_check=True)
                        last = nc.tensor.matmul(psum[:, 1, 0:4 * NB], rows[:, 1, :], cols[:, 1:5, :], start=False, stop=False, skip_group_check=True)
                    last.then_inc(hist_used, 1)
            for k in range(2):
                last = nc.tensor.matmul(psum[:, k, 0:4 * NB], zero_b[:, 0:BLK], zero_b[:, 0:4 * NB], start=False, stop=True, skip_group_check=True)
            last.then_inc(hist_done, 1)
            pe.wait_ge(degrees_ready, 1)
            nc.tensor.matmul(psum[0:SUBS, 2, 0:NB], sub_rows[:, 0, :], in_deg[:, 0, :], start=True, stop=False)
            nc.tensor.matmul(psum[0:SUBS, 2, 0:NB], ones[:, 0:SUBS], prefix[:, 0, :], start=False, stop=True)
            nc.tensor.matmul(psum[0:SUBS, 3, 0:NB], sub_rows[:, 1, :], in_deg[:, 0, :], start=True, stop=True).then_inc(starts_summed, 1)
            pe.wait_ge(misfit_ready, 1)
            nc.tensor.matmul(psum[0:1, 4, 0:BLK], misfit[:, 2:3], ident[:], start=True, stop=True).then_inc(misfit_turned, 1)
            phase_end(pe, 3)
            fast = pe.value_load(starts[0:1, 2 * NWIN:2 * NWIN + 1], min_val=0, max_val=1)
            with pe.If(fast == 1):
                pe.sem_inc(window_free, 2)
                pe.sem_inc(turned_kept, 1)
                pe.sem_inc(turn_done, SS)
                for b in range(2):
                    last = nc.tensor.matmul(psum[:, 6 + b, 0:HALF], zero_b[:, 0:BLK], iota_t[:, 0:HALF // HT, :], start=True, stop=True)
                last.then_inc(half_summed, 1)
                pe.wait_ge(l0_ready, 1)

                def chunk_back():
                    for b in range(CB):
                        to = psum[:, 6, b * (D + 1):(b + 1) * (D + 1)]
                        nc.tensor.matmul(to, LA[:, b * BLK:(b + 1) * BLK], fold[:], start=True, stop=False)
                        last = nc.tensor.matmul(to, LB[0:D + 1, b * BLK:(b + 1) * BLK], unscale[:], start=False, stop=True)
                    last.then_inc(chunk_turned, 1)

                def behind(slot, k, n, c, h):
                    pe.wait_ge(turned_kept, n + 1)
                    part = part_at(k // (2 * GRP), k // GRP % 2)
                    for j in range(GRP):
                        at = (k % GRP * GRP + j) * HALF + part
                        last = nc.tensor.matmul(banks(4, 2)[:, j * BLK:(j + 1) * BLK], stage[:, slot, at:at + BLK], ident16[:],
                                                start=True, stop=True)
                    last.then_inc(turn_done, 1)
                    if k == 0:
                        pe.wait_ge(half_out, h + 1)
                        if slot == 0:
                            chunk_back()
                    if k == 2 and slot == 0:
                        pe.wait_ge(chunk_out, c + 1)
                    if k >= 2:
                        for r in range(NB * (k - 2) // (WH - 2), NB * (k - 1) // (WH - 2)):
                            counts_r = stage[:, slot, r * HALF:(r + 1) * HALF]
                            nc.tensor.matmul(psum[:, 6, 0:HALF], L12[:, r, :], counts_r, start=(r == 0), stop=(r == NB - 1))
                            last = nc.tensor.matmul(psum[0:D + 1, 7, 0:HALF], L3p[:, r, :], counts_r, start=(r == 0), stop=(r == NB - 1))
                    if k == WH - 1:
                        last.then_inc(half_summed, 1)

                with pe.Fori(0, CHUNKS) as c:
                    for odd in range(2):
                        h = c * 2 + odd
                        for k in range(WH):
                            w = h * WH + k
                            s = k % SS
                            pe.wait_ge(keys_ready, w + (WS + 1))
                            pe.wait_ge(window_free, w + 1)
                            for t in range(2 * ST):
                                last = nc.tensor.matmul(psum[:, k % 2 * 2 + t // ST, 0:NB * SUB], sub_src[:, s, :, t],
                                                        sub_key[:, s, t, :], start=t % ST == 0, stop=t % ST == ST - 1)
                            last.then_inc(window_done, 1)
                            if k == 0:
                                pe.wait_ge(stage_ready, h + 1)
                            behind(1 - odd, k, w, c, h)
                pe.wait_ge(stage_ready, NH + 1)
                for k in range(WH):
                    behind(1, k, NWIN + k, CHUNKS, NH)
                pe.wait_ge(half_out, NH + 2)
                chunk_back()
            with pe.If(fast == 0):
                pe.sem_inc(slot_free, SL)
                pe.wait_ge(stage_ready, 1)
                pe.sem_inc(window_free, 2)
                pe.sem_inc(turned_kept, 1)
                visits = pe.alloc_register("pe_visits")
                pe.reg_mov(visits, 0)

                def turn(slot, at, r, n):
                    pe.wait_ge(turned_kept, n + 1)
                    for j in range(GRP):
                        last = nc.tensor.matmul(banks(4, 2)[:, j * BLK:(j + 1) * BLK],
                                                ap1(stage[:, bass.ds(slot, 1), bass.ds((r * GRP + j) * HALF + at, BLK)]),
                                                ident16[:], start=True, stop=True)
                    last.then_inc(turned, 1)

                with pe.Fori(0, NH) as h:
                    with pe.Fori(0, 2) as pair:
                        for odd in range(2):
                            q = pair * 2 + odd
                            with pe.Fori(0, GRP) as r:
                                w = h * 28 + q * 7 + r
                                lo = pe.value_load(bounds[0:1, bass.ds(w + NWIN, 1)], min_val=0, max_val=TILES // 2 - 1)
                                hi = pe.value_load(bounds[0:1, bass.ds(w, 1)], min_val=1, max_val=TILES // 2)
                                pe.wait_ge(window_free, w + 1)
                                buf = (q + r) % 2

                                def bank(k, n0, n1, buf=buf):
                                    return ap1(psum[:, bass.ds(buf * 2 + k, 1), n0:n1])

                                for k in range(2):
                                    nc.tensor.matmul(bank(k, 0, 4), zero16[:], ident16[:, 0:4], start=True, stop=False, skip_group_check=True)
                                with pe.Fori(lo, hi) as i:
                                    v = pe.snap(visits)
                                    pe.wait_ge(keys_ready, v + 1)
                                    s = v % SL
                                    for t in range(2):
                                        src = ap1(hot_src[:, bass.ds(s, 1), t * BLK:(t + 1) * BLK])
                                        at = t * NB * WIN
                                        nc.tensor.matmul(bank(0, 0, A0 * WIN), src, ap1(hot_key[:, bass.ds(s, 1), at:at + A0 * WIN]),
                                                         start=False, stop=False, skip_group_check=True)
                                        last = nc.tensor.matmul(bank(1, 0, A1 * WIN), src, ap1(hot_key[:, bass.ds(s, 1), at + A0 * WIN:at + NB * WIN]),
                                                         start=False, stop=False, skip_group_check=True)
                                    last.then_inc(slot_free, 1)
                                    pe.reg_add(visits, visits, 1)
                                for k in range(2):
                                    last = nc.tensor.matmul(bank(k, 0, 4), zero16[:], ident16[:, 0:4], start=False, stop=True, skip_group_check=True)
                                last.then_inc(window_done, 1)
                                turn((h + 1) % 2, part_at(pair, odd), r, w)
                    pe.wait_ge(stage_ready, h + 2)
                with pe.Fori(0, 2) as pair:
                    for odd in range(2):
                        q = pair * 2 + odd
                        with pe.Fori(0, GRP) as r:
                            turn((NH - 1) % 2, part_at(pair, odd), r, q * 7 + r + NWIN)
            phase_end(pe, 4)
            def count_sums(L, kept):
                def turn_back():
                    for b in range(CB):
                        to = psum[:, 4, b * (D + 1):(b + 1) * (D + 1)]
                        nc.tensor.matmul(to, TA[:, b * BLK:(b + 1) * BLK], fold[:], start=True, stop=False)
                        last = nc.tensor.matmul(to, TB[0:D + 1, b * BLK:(b + 1) * BLK], unscale[:], start=False, stop=True)
                    last.then_inc(agg_turned, 1)

                def chunk(c, first):
                    for g in range(NGRP):
                        pe.wait_ge(cnt_in[g], c * 32 + 32 * (L * CHUNKS + 1))
                        for j in range(GRP):
                            r = g * GRP + j
                            for k, part_of in enumerate((H12[:, r, :], H3[:, r, :])):
                                for t in range(2):
                                    to = psum[:, 2 * k + t, 0:HALF] if k == 0 else psum[0:D + 1, 2 * k + t, 0:HALF]
                                    last = nc.tensor.matmul(to, part_of, counts_of(g, j)[:, t * HALF:(t + 1) * HALF],
                                                            start=(r == 0), stop=(r == NB - 1))
                        if g < NGRP - 1:
                            last.then_inc(cnt_free, 1)
                        if g == 0 and not first:
                            turn_back()
                    last.then_inc(agg_done, 1)
                    pe.wait_ge(agg_kept, c * 2 + (kept + 2))
                    pe.sem_inc(cnt_free, 1)

                chunk(0, True)
                with pe.Fori(1, CHUNKS) as c:
                    chunk(c, False)
                turn_back()

            phase_end(pe, 5)
            with pe.If(fast == 0):
                count_sums(0, 0)
            phase_end(pe, 6)
            for l, (ki, fo, W, a_both, a_rows, _, _, _) in enumerate(att):
                n = l * CHUNKS + 1

                def turn_input(c):
                    pe.wait_ge(input_placed, c * 2 + (2 * n - 1))
                    for b in range(CB):
                        last = nc.tensor.matmul(banks(0, 2)[0:ki, b * BLK:(b + 1) * BLK], TA[:, b * ki:(b + 1) * ki], ident[:],
                                                start=True, stop=True)
                    last.then_inc(input_turned, 1)

                def features(c):
                    pe.wait_ge(input_placed, c * 2 + 2 * n)
                    for b in range(CB):
                        nc.tensor.matmul(psum[:, 2, b * fo:(b + 1) * fo], TB[0:ki, b * BLK:(b + 1) * BLK], W[:], start=True, stop=True)
                    for t in range(2):
                        last = nc.tensor.matmul(psum[0:fo, 3 + t, 0:HALF], W[:], TB[0:ki, t * HALF:(t + 1) * HALF], start=True, stop=True)
                    last.then_inc(feats_done, 1)

                def scores(c):
                    pe.wait_ge(feats_kept, c * 2 + 2 * n)
                    pe.wait_ge(scores_kept, c + n)
                    for t in range(2):
                        nc.tensor.matmul(psum[:, 5 + t, 0:HALF], a_rows[:], YE[0:fo, 0, t * HALF:(t + 1) * HALF], start=True, stop=True)
                    for b in range(CB):
                        last = nc.tensor.matmul(psum[:, 7, 2 * b:2 * b + 2], YE[0:fo, 0, b * BLK:(b + 1) * BLK], a_both[:], start=True, stop=True)
                    last.then_inc(scores_done, 1)

                if l == 0:
                    pe.sem_inc(scores_kept, 1)
                turn_input(0)
                with pe.Fori(0, CHUNKS - 1) as c:
                    features(c)
                    turn_input(c + 1)
                    scores(c)
                features(CHUNKS - 1)
                scores(CHUNKS - 1)
                phase_end(pe, 7 + 4 * l)
                phase_end(pe, 8 + 4 * l)
                if l == 0:
                    pe.sem_inc(diag_spread, 2)
                with pe.Fori(0, CHUNKS) as c:
                    pe.wait_ge(diag_ready, c + (l * CHUNKS + 1))
                    pe.wait_ge(diag_kept, c + (l * CHUNKS + 1))
                    for k in range(2):
                        for t in range(2):
                            last = nc.tensor.matmul(ap1(psum[:, bass.ds(c % 2 * 4 + (2 * k + t), 1), 0:HALF]), ones[:],
                                                    ap1(YE[:, bass.ds(c % 2 * 2 + k, 1), t * HALF:(t + 1) * HALF]), start=True, stop=True)
                    last.then_inc(diag_spread, 1)
                phase_end(pe, 9 + 4 * l)
                if l == 0:
                    pe.sem_inc(p_used, 3)
                def turn_back():
                    for b in range(CB):
                        last = nc.tensor.matmul(psum[:, 4, b * (fo + 1):(b + 1) * (fo + 1)], TA[0:fo + 1, b * BLK:(b + 1) * BLK],
                                                ident[0:fo + 1, 0:fo + 1], start=True, stop=True)
                    last.then_inc(agg_turned, 1)

                def chunk(c, first):
                    for r in range(NB):
                        pe.wait_ge(p_ready, c * NB + (l * ROWS + r + 1))
                        for t in range(2):
                            last = nc.tensor.matmul(psum[0:fo + 1, t, 0:HALF], HF[:, r * (fo + 1):(r + 1) * (fo + 1)],
                                                    PW[:, slot(r, 3), t * HALF:(t + 1) * HALF], start=(r == 0), stop=(r == NB - 1))
                        last.then_inc(p_used, 1)
                        if r == TURN and not first:
                            turn_back()
                    pe.drain().then_inc(agg_done, 1)
                    pe.wait_ge(agg_kept, c + (2 * CHUNKS + l * CHUNKS + 1))

                chunk(0, True)
                with pe.Fori(1, CHUNKS) as c:
                    chunk(c, False)
                turn_back()
                phase_end(pe, 10 + 4 * l)
            phase_end(pe, 19)
            count_sums(4, CHUNKS * 5)
            phase_end(pe, 20)
            pe.sem_inc(mlp_stored, 1)

            def turn_input(c):
                pe.wait_ge(mlp_copied, c + 2)
                for b in range(CB):
                    nc.tensor.transpose(banks(0, 2)[:, b * BLK:(b + 1) * BLK], MA[:, b * BLK:(b + 1) * BLK], ident[:])
                    last = nc.tensor.transpose(banks(2, 2)[0:2, b * BLK:(b + 1) * BLK], TD[:, b * 2:b * 2 + 2], ident[:])
                last.then_inc(mlp_turned, 1)

            def first_layer(c):
                pe.wait_ge(mlp_kept, c * 2 + 2)
                pe.wait_ge(mlp_stored, c + 1)
                for b in range(CB):
                    to = banks(4, 2)[:, b * BLK:(b + 1) * BLK]
                    nc.tensor.matmul(to, TB[:, b * BLK:(b + 1) * BLK], W3a[:], start=True, stop=False)
                    last = nc.tensor.matmul(to, DET[:, b * BLK:(b + 1) * BLK], W3b[:], start=False, stop=True)
                last.then_inc(mlp_out, 1)

            def second_layer(c):
                pe.wait_ge(mlp_relu, c + 1)
                for b in range(CB):
                    last = nc.tensor.transpose(banks(6, 2)[:, b * BLK:(b + 1) * BLK], TA[:, b * BLK:(b + 1) * BLK], ident[:])
                last.then_inc(mlp_turned2, 1)
                pe.wait_ge(mlp_kept2, c + 1)
                for b in range(CB):
                    last = nc.tensor.matmul(banks(4, 2)[:, b * BLK:(b + 1) * BLK], MB[:, b * BLK:(b + 1) * BLK],
                                            W4[:].rearrange("k t f -> k (t f)"), start=True, stop=True)
                last.then_inc(mlp_out2, 1)

            turn_input(0)
            with pe.Fori(0, CHUNKS - 1) as c:
                first_layer(c)
                turn_input(c + 1)
                second_layer(c)
            first_layer(CHUNKS - 1)
            second_layer(CHUNKS - 1)
            phase_end(pe, 21)
            count_sums(5, CHUNKS * 7)
            phase_end(pe, 22)
            phase_end(pe, 23)

        @block.scalar
        def _(act):
            def root(k):
                act.wait_ge(root_in, k)
                nc.scalar.activation(stat[1][:], stat[2][:], ACT.Sqrt).then_inc(root_out, 1)

            phase_end(act, 1)
            with act.Fori(0, G) as g:
                nc.scalar.copy(grp[:], raw[:, :, bass.ds(g * BLK, BLK)]).then_inc(group_copied, 1)
                act.wait_ge(group_turned, g + 1)
                nc.scalar.copy(et[:, :, bass.ds(g * BLK, BLK)], psum[:, 0, :].rearrange("p (k n) -> p k n", k=4)).then_inc(group_kept, 1)
                nc.scalar.copy(ea_rest[:, bass.ds(g * BLK, BLK)], psum[:, 1, 0:BLK]).then_inc(group_kept, 1)
            phase_end(act, 2)
            phase_end(act, 3)
            PIECE_AT = (3, 8, 11, 15, 18)
            PIECE = NB // 4 * HALF
            fast = act.value_load(starts[0:1, 2 * NWIN:2 * NWIN + 1], min_val=0, max_val=1)
            with act.If(fast == 1):
                root(1)
                root(2)
                act.wait_ge(l0_ready, 1)
                act.sem_inc(counts_stored, 80)
                for q in range(2):
                    act.sem_inc(linked_stored[q], 16)

                def half_sums(odd, h):
                    act.wait_ge(half_summed, h + 1)
                    nc.scalar.copy(LA[:, odd * HALF:(odd + 1) * HALF], psum[:, 6, 0:HALF])
                    nc.scalar.copy(LB[0:D + 1, odd * HALF:(odd + 1) * HALF], psum[0:D + 1, 7, 0:HALF]).then_inc(half_out, 1)

                def chunk_sums(c):
                    act.wait_ge(chunk_turned, c + 1)
                    wide = CB * (D + 1)
                    to = LAGG[:, bass.ds(c * wide, wide)] if not isinstance(c, int) else LAGG[:, c * wide:(c + 1) * wide]
                    nc.scalar.copy(to, psum[:, 6, 0:wide]).then_inc(chunk_out, 1)

                def keep_part(k, n):
                    act.wait_ge(turn_done, n + (SS + 1))
                    r = k % GRP
                    nc.scalar.activation(linked_sb[:, k // GRP % 2, r * CW:(r + 1) * CW], banks(4, 2)[:, 0:CW], ACT.Sign).then_inc(turned_kept, 1)

                def store_linked(k, h):
                    pair, q = divmod(k // GRP, 2)
                    act.drain()
                    if q == 1:
                        act.wait_ge(linked_stored[0], (h * 2 + pair) * 16 + 32)
                    act.dma_start(linked[bass.ds(h * HALF + part_at(pair, q), BLK), :], linked_sb[:, q, :]).then_inc(linked_stored[q], 16)

                def store_piece(slot, p, h):
                    n0, n1 = p * PIECE, (p + 1) * PIECE if p < 4 else NB * HALF
                    act.dma_start(counts[bass.ds(h, 1)].rearrange("o b a d -> b (o a d)")[:, n0:n1], stage[:, slot, n0:n1]).then_inc(counts_stored, 16)

                with act.Fori(0, CHUNKS) as c:
                    for odd in range(2):
                        h = c * 2 + odd
                        act.wait_ge(counts_stored, (h + 1) * 80)
                        to = stage[:, odd, :].rearrange("p (a d) -> p a d", a=NB)
                        for k in range(WH):
                            if k % GRP == 0:
                                q = k // GRP
                                act.wait_ge(linked_stored[q % 2], (h * 2 + q // 2 + 1) * 16)
                            w = h * WH + k
                            act.wait_ge(window_done, w + 1)
                            nc.scalar.activation(to[:, :, k * WIN:(k + 1) * WIN].rearrange("p a (k d) -> p k a d", k=2),
                                                 psum[:, k % 2 * 2:k % 2 * 2 + 2, 0:NB * SUB].rearrange("p k (a d) -> p k a d", a=NB),
                                                 ACT.Copy, scale=UNIT).then_inc(window_free, 1)
                            if k == WH - 1:
                                act.drain().then_inc(stage_full, 1)
                            if k == 0:
                                half_sums(odd, h)
                            keep_part(k, w)
                            if k == 2:
                                act.wait_ge(stage_ready, h + 1)
                            if k in PIECE_AT:
                                store_piece(1 - odd, PIECE_AT.index(k), h)
                            if k == 1 and odd == 1:
                                chunk_sums(c)
                            if k % GRP == GRP - 1:
                                store_linked(k, h)
                act.wait_ge(stage_ready, NH + 1)
                act.dma_start(counts[NH].rearrange("b a d -> b (a d)"), stage[:, (NH - 1) % 2, :]).then_inc(counts_stored, 16)
                half_sums(0, NH)
                for k in range(WH):
                    if k % GRP == 0:
                        act.wait_ge(linked_stored[k // GRP % 2], (NH * 2 + k // GRP // 2 + 1) * 16)
                    keep_part(k, NWIN + k)
                    if k % GRP == GRP - 1:
                        store_linked(k, NH)
                half_sums(1, NH + 1)
                chunk_sums(CHUNKS)
                act.wait_ge(counts_stored, (NH + 1) * 80 + 16)
                for q in range(2):
                    act.wait_ge(linked_stored[q], (2 * NH + 3) * 16)
            with act.If(fast == 0):
                act.sem_inc(stage_free, 2)
                act.sem_inc(linked_free, 6)
                with act.Fori(0, NH) as h:
                    act.wait_ge(stage_free, h + 1)
                    with act.Fori(0, 4) as q:
                        act.wait_ge(linked_free, h * 4 + q + 1)
                        with act.Fori(0, GRP) as r:
                            w = h * 28 + q * 7 + r
                            act.wait_ge(window_done, w + 1)
                            buf = (q + r) % 2
                            to = ap1(stage[:, bass.ds(h % 2, 1), :]).rearrange("p (a d) -> p a d", a=NB)
                            to = to[:, :, bass.ds((q * 7 + r) * WIN, WIN)]
                            nc.scalar.activation(to[:, 0:A0, :], ap1(psum[:, bass.ds(buf * 2, 1), 0:A0 * WIN]).rearrange("p (a d) -> p a d", a=A0),
                                                     ACT.Copy, scale=UNIT)
                            nc.scalar.activation(to[:, A0:NB, :], ap1(psum[:, bass.ds(buf * 2 + 1, 1), 0:A1 * WIN]).rearrange("p (a d) -> p a d", a=A1),
                                                     ACT.Copy, scale=UNIT
                                           ).then_inc(window_free, 1)
                            act.wait_ge(turned, w + 1)
                            nc.scalar.activation(ap1(linked_sb[:, bass.ds(q % 2, 1), bass.ds(r * CW, CW)]), banks(4, 2)[:, 0:CW],
                                                 ACT.Sign).then_inc(turned_kept, 1)
                        act.drain().then_inc(linked_full, 1)
                    act.drain().then_inc(stage_full, 1)
                with act.Fori(0, 4) as q:
                    act.wait_ge(linked_free, NH * 4 + q + 1)
                    with act.Fori(0, GRP) as r:
                        act.wait_ge(turned, NWIN + q * 7 + r + 1)
                        nc.scalar.activation(ap1(linked_sb[:, bass.ds(q % 2, 1), bass.ds(r * CW, CW)]), banks(4, 2)[:, 0:CW],
                                             ACT.Sign).then_inc(turned_kept, 1)
                    act.drain().then_inc(linked_full, 1)
            phase_end(act, 4)
            def count_sums(n):
                def parts_out(c):
                    act.wait_ge(agg_done, c + (n + 1))
                    nc.scalar.copy(TA[:].rearrange("p (t d) -> p t d", t=2), psum[:, 0:2, 0:HALF]).then_inc(agg_kept, 1)

                def sums_out(c):
                    act.wait_ge(agg_turned, c + (n + 1))
                    nc.scalar.copy(AGG[:, bass.ds(c * CB * (D + 1), CB * (D + 1))], psum[:, 4, 0:CB * (D + 1)])

                parts_out(0)
                with act.Fori(0, CHUNKS - 1) as c:
                    sums_out(c)
                    parts_out(c + 1)
                sums_out(CHUNKS - 1)

            with act.If(fast == 0):
                root(1)
                root(2)
            with act.If(fast == 1):
                nc.scalar.copy(AGG[:], LAGG[:, CB * (D + 1):(CHUNKS + 1) * CB * (D + 1)])
            phase_end(act, 5)
            with act.If(fast == 0):
                count_sums(0)
            phase_end(act, 6)
            root(3)
            root(4)
            for l, (ki, fo, W, a_both, a_rows, _, _, _) in enumerate(att):
                act.wait_ge(input_ready, l + 1)
                n = l * CHUNKS + 1

                def place_input(c):
                    nc.scalar.copy(TA[:, 0:CB * ki].rearrange("p (a f) -> p a f", a=CB), HIN[:, bass.ds(c * CB, CB), 0:ki]).then_inc(input_placed, 1)

                def turned_out(c):
                    act.wait_ge(input_turned, c + n)
                    nc.scalar.copy(TB[0:ki, :], banks(0, 2)[0:ki, 0:CW]).then_inc(input_placed, 1)

                def features_out(c):
                    act.wait_ge(feats_done, c + n)
                    nc.scalar.copy(YE[0:fo, 0, :].rearrange("p (t d) -> p t d", t=2), psum[0:fo, 3:5, 0:HALF]).then_inc(feats_kept, 1)

                place_input(0)
                turned_out(0)
                with act.Fori(0, CHUNKS - 1) as c:
                    place_input(c + 1)
                    features_out(c)
                    turned_out(c + 1)
                features_out(CHUNKS - 1)
                phase_end(act, 7 + 4 * l)
                phase_end(act, 8 + 4 * l)
                if l == 0:
                    act.sem_inc(diag_kept, 2)
                with act.Fori(0, CHUNKS) as c:
                    act.wait_ge(diag_spread, c + (l * CHUNKS + 3))
                    for k, row_of in enumerate((ROW1, ROW2)):
                        last = nc.scalar.copy(row_of[:, bass.ds(c * CW, CW)].rearrange("p (t d) -> p t d", t=2),
                                              psum[:, bass.ds(c % 2 * 4 + 2 * k, 2), 0:HALF])
                    last.then_inc(diag_kept, 1)
                phase_end(act, 9 + 4 * l)
                def sums_out(c):
                    act.wait_ge(agg_turned, c + (CHUNKS + l * CHUNKS + 1))
                    nc.scalar.copy(AGG[:, bass.ds(c * CB * (fo + 1), CB * (fo + 1))], psum[:, 4, 0:CB * (fo + 1)])

                def parts_out(c):
                    act.wait_ge(agg_done, c + (CHUNKS + l * CHUNKS + 1))
                    nc.scalar.copy(TA[0:fo + 1, :].rearrange("p (t d) -> p t d", t=2), psum[0:fo + 1, 0:2, 0:HALF]).then_inc(agg_kept, 1)

                def chunk(c, first):
                    for r in range(NB):
                        act.wait_ge(y_ready, c * NB + (l * ROWS + r + 1))
                        y = YE[:, slot(r, 4), :]
                        nc.scalar.activation(y, y, ACT.Exp, bias=sj2[:, r:r + 1]).then_inc(e_ready, 1)
                        if r == 1 and not first:
                            parts_out(c - 1)
                        if r == TURN + 4 and not first:
                            sums_out(c - 1)

                chunk(0, True)
                with act.Fori(1, CHUNKS) as c:
                    chunk(c, False)
                parts_out(CHUNKS - 1)
                sums_out(CHUNKS - 1)
                phase_end(act, 10 + 4 * l)
                if l == 1:
                    root(5)
                if l == 2:
                    root(6)
                    root(7)
            phase_end(act, 19)
            count_sums(CHUNKS * 4)
            phase_end(act, 20)
            act.wait_ge(mlp_copied, 1)

            def place_dense(c):
                nc.scalar.copy(TD[:, 0:2 * CB].rearrange("p (a f) -> p a f", a=CB), DE[:, bass.ds(c * CB, CB), :])
                nc.scalar.copy(MA.rearrange("p (a f) -> p a f", a=CB), US[:, bass.ds(c * CB, CB), :]).then_inc(mlp_copied, 1)

            def turned_in(c):
                act.wait_ge(mlp_turned, c + 1)
                nc.scalar.copy(TB[:], banks(0, 2)[:, 0:CW]).then_inc(mlp_kept, 1)

            def relu_out(c):
                act.wait_ge(mlp_out, c + 1)
                nc.scalar.activation(TA[:], banks(4, 2)[:, 0:CW], ACT.Relu).then_inc(mlp_relu, 1)

            def turned_mid(c):
                act.wait_ge(mlp_turned2, c + 1)
                nc.scalar.copy(MB, banks(6, 2)[:, 0:CW]).then_inc(mlp_kept2, 1)

            place_dense(0)
            turned_in(0)
            with act.Fori(0, CHUNKS - 1) as c:
                place_dense(c + 1)
                relu_out(c)
                turned_in(c + 1)
                turned_mid(c)
            relu_out(CHUNKS - 1)
            turned_mid(CHUNKS - 1)
            phase_end(act, 21)
            count_sums(CHUNKS * 5)
            phase_end(act, 22)
            act.wait_ge(root_in, 8)
            nc.scalar.activation(SQ[:], GI[:], ACT.Exp).then_inc(root_out, 1)
            act.wait_ge(root_in, 9)
            nc.scalar.activation(stat[1][:], stat[2][:], ACT.Ln).then_inc(root_out, 1)
            phase_end(act, 23)


_INS = ['x', 'src', 'dst', 'edge_weight1', 'L1_gnn_W1', 'L1_gnn_a_src1', 'L1_gnn_a_dst1', 'L1_gnn_b1', 'L1_gnn_W2',
        'L1_gnn_a_src2', 'L1_gnn_a_dst2', 'L1_gnn_b2', 'L2_gnn_weight', 'L2_gnn_att', 'L2_gnn_bias', 'L3_gnn_W1',
        'L3_gnn_b1', 'L3_gnn_W2', 'L3_gnn_b2']


def kernel(**inputs):
    import numpy as _np
    import concourse.bacc as _bacc
    from concourse import mybir as _mybir
    from concourse.bass_utils import run_bass_kernel_spmd as _run

    nc = _bacc.Bacc("TRN2", target_bir_lowering=False, num_devices=1)
    arrays, aps = {}, {}
    for name in _INS:
        a = _np.ascontiguousarray(inputs[name])
        arrays["in_" + name] = a
        aps[name] = nc.dram_tensor("in_" + name, a.shape, _mybir.dt.from_np(a.dtype), kind="ExternalInput").ap()
    out = nc.dram_tensor("out_0", (N, D), _mybir.dt.from_np(_np.dtype("float32")), kind="ExternalOutput").ap()
    gnn_kernel(nc, aps, out)
    r = _run(nc, [arrays], core_ids=[0])
    return r.results[0]["out_0"]
```
